# Optimizing a Trainium2 kernel written in Bass

```python
import numpy as np
import jax
import jax.numpy as jnp

def _softmax(x, axis=-1):
    return jax.nn.softmax(x, axis=axis)

def _gelu(x):
    return jax.nn.gelu(x, approximate=True)

def _silu(x):
    return jax.nn.silu(x)

def _sigmoid(x):
    return jax.nn.sigmoid(x)

def _layernorm(x, axis=-1, eps=1e-05):
    m = jnp.mean(x, axis=axis, keepdims=True)
    v = jnp.var(x, axis=axis, keepdims=True)
    return (x - m) / jnp.sqrt(v + eps)

def _scatter_add(tgt, idx, src, axis=0):
    return tgt.at[idx].add(src)

def _segment_sum(src, seg, n):
    return jax.ops.segment_sum(src, seg, n)
kernel_name = 'mk_perceiver_d4_seqx_r8_f678ea'

def setup_inputs(seed: int=0):
    np.random.seed(seed)
    _w = jnp.asarray

    def _rec_inputs():
        import jax
        import jax.numpy as jnp
        _rk = jax.random.key(seed)
        x = -0.0003929 + 0.9999 * jax.random.normal(jax.random.fold_in(_rk, 1), (16, 64, 128), jnp.float32)
        _lenS = 64 - jax.random.randint(jax.random.fold_in(_rk, 7), (16,), 0, max(1, 64 // 4) + 1, jnp.int32)
        _lenS2 = 128 - jax.random.randint(jax.random.fold_in(_rk, 8), (16,), 0, max(1, 128 // 4) + 1, jnp.int32)
        _ctx_1024P = jax.random.normal(jax.random.fold_in(_rk, 11), (16, 16, 128), jnp.float32)
        _ctx_1024c = jax.random.dirichlet(jax.random.fold_in(_rk, 511), 0.3 * jnp.ones((16,), jnp.float32), (16, 128))
        _ctx_1024t = jnp.einsum('bsk,bkd->bsd', _ctx_1024c, _ctx_1024P)
        _ctx_1024t = _ctx_1024t * jax.lax.rsqrt(jnp.mean(jnp.square(_ctx_1024t)) + 1e-12) * 0.953939
        ctx_1024 = 2.81802e-05 + 1.00001 * (_ctx_1024t + 0.3 * jax.random.normal(jax.random.fold_in(_rk, 611), (16, 128, 128), jnp.float32))
        return (x, ctx_1024)
    x, ctx_1024 = _rec_inputs()

    def _L0_xattn_setup():
        import jax, jax.numpy as jnp
        import numpy as np
        key = jax.random.key(seed)
        k1, k2, k3, k4 = jax.random.split(key, 4)
        B, L1, L2, D = (32, 64, 64, 128)
        ix = jax.random.normal(k1, (B, L1, D), dtype=jnp.float32)
        iother = jax.random.normal(k2, (B, L2, D), dtype=jnp.float32)
        scale = 1.0 / np.sqrt(D)
        W = jax.random.uniform(k3, (D, D), dtype=jnp.float32, minval=-scale, maxval=scale)
        b = jax.random.uniform(k4, (D,), dtype=jnp.float32, minval=-scale, maxval=scale)
        return {'ix': ix, 'iother': iother, 'W': W, 'b': b}
    _L0_xattn_all = _L0_xattn_setup()
    _L0_xattn_in = {k: v for k, v in _L0_xattn_all.items() if k in ('W', 'b')}
    del _L0_xattn_all

    def _L0_attn_setup():
        import jax, jax.numpy as jnp
        import numpy as np
        B, S, H, NH = (8, 512, 128, 16)
        HD = H // NH
        EPS_ATTN = 1e-06
        EPS_LN = 1e-12
        key = jax.random.key(seed)
        ks = jax.random.split(key, 10)
        s = 1.0 / np.sqrt(H)
        return {'input_tensor': jax.random.normal(ks[0], (B, S, H), dtype=jnp.float32), 'attention_mask': jnp.zeros((B, S), dtype=jnp.int32), 'Wq': jax.random.normal(ks[1], (H, H), dtype=jnp.float32) * s, 'bq': jnp.zeros((H,), dtype=jnp.float32), 'Wk': jax.random.normal(ks[2], (H, H), dtype=jnp.float32) * s, 'bk': jnp.zeros((H,), dtype=jnp.float32), 'Wv': jax.random.normal(ks[3], (H, H), dtype=jnp.float32) * s, 'bv': jnp.zeros((H,), dtype=jnp.float32), 'Wd': jax.random.normal(ks[4], (H, H), dtype=jnp.float32) * s, 'bd': jnp.zeros((H,), dtype=jnp.float32), 'gamma': jnp.ones((H,), dtype=jnp.float32), 'beta': jnp.zeros((H,), dtype=jnp.float32)}
    _L0_attn_all = _L0_attn_setup()
    _L0_attn_in = {k: v for k, v in _L0_attn_all.items() if k in ('attention_mask', 'Wq', 'bq', 'Wk', 'bk', 'Wv', 'bv', 'Wd', 'bd', 'gamma', 'beta')}
    del _L0_attn_all

    def _L0_ffn_setup():
        import jax, jax.numpy as jnp
        import numpy as np
        E = 8
        K = 2
        CAP_FACTOR = 1.0
        key = jax.random.key(seed)
        k0, k1, k2, k3 = jax.random.split(key, 4)
        B, S, M, H = (4, 256, 128, 512)
        x = jax.random.normal(k0, (B, S, M), jnp.float32)
        wg = jax.random.normal(k1, (M, E), jnp.float32) * 0.02
        w1 = jax.random.normal(k2, (E, M, H), jnp.float32) * 0.02
        b1 = jnp.zeros((E, H), jnp.float32)
        w2 = jax.random.normal(k3, (E, H, M), jnp.float32) * 0.02
        b2 = jnp.zeros((E, M), jnp.float32)
        return {'x': x, 'wg': wg, 'w1': w1, 'b1': b1, 'w2': w2, 'b2': b2}
    _L0_ffn_all = _L0_ffn_setup()
    _L0_ffn_in = {k: v for k, v in _L0_ffn_all.items() if k in ('wg', 'w1', 'b1', 'w2', 'b2')}
    del _L0_ffn_all

    def _L1_xattn_setup():
        import jax, jax.numpy as jnp
        import numpy as np
        import math
        D_MODEL = 128
        N_HEADS = 16
        D_HEAD = D_MODEL // N_HEADS
        key = jax.random.key(seed)
        ks = jax.random.split(key, 11)
        N, L, S = (2, 256, 256)
        inp = {'queries': jax.random.normal(ks[0], (N, L, D_MODEL), dtype=jnp.float32), 'keys': jax.random.normal(ks[1], (N, S, D_MODEL), dtype=jnp.float32), 'values': jax.random.normal(ks[2], (N, S, D_MODEL), dtype=jnp.float32), 'Wq': jax.random.normal(ks[3], (D_MODEL, N_HEADS * D_HEAD), dtype=jnp.float32) / math.sqrt(D_MODEL), 'bq': jnp.zeros((N_HEADS * D_HEAD,), dtype=jnp.float32), 'Wk': jax.random.normal(ks[4], (D_MODEL, N_HEADS * D_HEAD), dtype=jnp.float32) / math.sqrt(D_MODEL), 'bk': jnp.zeros((N_HEADS * D_HEAD,), dtype=jnp.float32), 'Wv': jax.random.normal(ks[5], (D_MODEL, N_HEADS * D_HEAD), dtype=jnp.float32) / math.sqrt(D_MODEL), 'bv': jnp.zeros((N_HEADS * D_HEAD,), dtype=jnp.float32), 'Wo': jax.random.normal(ks[6], (N_HEADS * D_HEAD, D_MODEL), dtype=jnp.float32) / math.sqrt(N_HEADS * D_HEAD), 'bo': jnp.zeros((D_MODEL,), dtype=jnp.float32)}
        return inp
    _L1_xattn_all = _L1_xattn_setup()
    _L1_xattn_in = {k: v for k, v in _L1_xattn_all.items() if k in ('Wq', 'bq', 'Wk', 'bk', 'Wv', 'bv', 'Wo', 'bo')}
    del _L1_xattn_all

    def _L1_attn_setup():
        import jax, jax.numpy as jnp
        import numpy as np
        D_MODEL = 128
        N_HEADS = 16
        N_WAVES = 16
        D_FF = 4 * D_MODEL
        LN_EPS = 1e-05
        NORM_EPS = 1e-12

        def _layernorm(x, g, b):
            m = jnp.mean(x, axis=-1, keepdims=True)
            v = jnp.mean(jnp.square(x - m), axis=-1, keepdims=True)
            return (x - m) * jax.lax.rsqrt(v + LN_EPS) * g + b

        def _l2norm(x):
            n = jnp.sqrt(jnp.sum(jnp.square(x), axis=-1, keepdims=True))
            return x / jnp.maximum(n, NORM_EPS)

        def _wave_block(x, ln1_g, ln1_b, Wqf, bqf, Wkf, bkf, Wqp, bqp, Wkp, bkp, Wv, bv, Wo, bo, iscale, ln2_g, ln2_b, W1, b1, W2, b2):
            B, T, C = x.shape
            H, W, Dh = (N_HEADS, N_WAVES, C // N_HEADS)
            xn = _layernorm(x, ln1_g, ln1_b)

            def proj(Wm, bm):
                return (xn @ Wm + bm).reshape(B, T, H, W).transpose(0, 2, 1, 3)
            q_f, k_f = (proj(Wqf, bqf), proj(Wkf, bkf))
            q_p, k_p = (proj(Wqp, bqp), proj(Wkp, bkp))
            v = (xn @ Wv + bv).reshape(B, T, H, Dh).transpose(0, 2, 1, 3)
            t_pos = jnp.arange(T, dtype=x.dtype)[None, None, :, None]
            q_norm = _l2norm(jnp.sin(q_f * t_pos + q_p))
            k_norm = _l2norm(jnp.sin(k_f * t_pos + k_p))
            inter = jnp.einsum('bhtw,bhsw->bhts', q_norm, k_norm) * iscale
            causal = jnp.tril(jnp.ones((T, T), dtype=x.dtype))
            inter = inter * causal
            num_attended = jnp.sqrt(jnp.arange(1, T + 1, dtype=x.dtype))[None, None, :, None]
            attn = inter / num_attended
            out = jnp.einsum('bhts,bhsd->bhtd', attn, v)
            out = out.transpose(0, 2, 1, 3).reshape(B, T, C) @ Wo + bo
            x = x + out
            hpre = _layernorm(x, ln2_g, ln2_b) @ W1 + b1
            hact = jax.nn.gelu(hpre, approximate=False) + 0.1 * jnp.sin(hpre)
            x = x + hact @ W2 + b2
            return x
        key = jax.random.key(seed)
        ks = jax.random.split(key, 16)
        d, h, w, ff = (D_MODEL, N_HEADS, N_WAVES, D_FF)
        s = 0.02
        return {'x': jax.random.normal(ks[0], (2, 256, d), dtype=jnp.float32), 'ln1_g': jnp.ones((d,), jnp.float32), 'ln1_b': jnp.zeros((d,), jnp.float32), 'Wqf': jax.random.normal(ks[1], (d, h * w), jnp.float32) * s, 'bqf': jnp.zeros((h * w,), jnp.float32), 'Wkf': jax.random.normal(ks[2], (d, h * w), jnp.float32) * s, 'bkf': jnp.zeros((h * w,), jnp.float32), 'Wqp': jax.random.normal(ks[3], (d, h * w), jnp.float32) * s, 'bqp': jnp.zeros((h * w,), jnp.float32), 'Wkp': jax.random.normal(ks[4], (d, h * w), jnp.float32) * s, 'bkp': jnp.zeros((h * w,), jnp.float32), 'Wv': jax.random.normal(ks[5], (d, d), jnp.float32) * s, 'bv': jnp.zeros((d,), jnp.float32), 'Wo': jax.random.normal(ks[6], (d, d), jnp.float32) * s, 'bo': jnp.zeros((d,), jnp.float32), 'iscale': jnp.ones((h, 1, 1), jnp.float32), 'ln2_g': jnp.ones((d,), jnp.float32), 'ln2_b': jnp.zeros((d,), jnp.float32), 'W1': jax.random.normal(ks[7], (d, ff), jnp.float32) * s, 'b1': jnp.zeros((ff,), jnp.float32), 'W2': jax.random.normal(ks[8], (ff, d), jnp.float32) * s, 'b2': jnp.zeros((d,), jnp.float32)}
    _L1_attn_all = _L1_attn_setup()
    _L1_attn_in = {k: v for k, v in _L1_attn_all.items() if k in ('ln1_g', 'ln1_b', 'Wqf', 'bqf', 'Wkf', 'bkf', 'Wqp', 'bqp', 'Wkp', 'bkp', 'Wv', 'bv', 'Wo', 'bo', 'iscale', 'ln2_g', 'ln2_b', 'W1', 'b1', 'W2', 'b2')}
    del _L1_attn_all

    def _L1_ffn_setup():
        import jax, jax.numpy as jnp
        import numpy as np
        import math
        DMODEL = 128
        DFF = 512
        NUM_EXPERTS = 8
        TOPK = 2
        CAP_FACTOR = 1.25
        EPS = 1.1920929e-07

        def _trunc_normal(key, shape, fan_in, scale=1.0):
            std = scale * (1.0 / fan_in) ** 0.5
            return jax.random.truncated_normal(key, -2.0, 2.0, shape, jnp.float32) * std
        key = jax.random.key(seed)
        ks = jax.random.split(key, 5)
        return {'x': jax.random.normal(ks[0], (2, 256, DMODEL), jnp.float32), 'router_weight': _trunc_normal(ks[1], (NUM_EXPERTS, DMODEL), DMODEL), 'ff_pre_act_weight': _trunc_normal(ks[2], (NUM_EXPERTS, DFF, DMODEL), DMODEL), 'gate_weight': _trunc_normal(ks[3], (NUM_EXPERTS, DFF, DMODEL), DMODEL), 'ff_post_act_weight': _trunc_normal(ks[4], (NUM_EXPERTS, DMODEL, DFF), DFF)}
    _L1_ffn_all = _L1_ffn_setup()
    _L1_ffn_in = {k: v for k, v in _L1_ffn_all.items() if k in ('router_weight', 'ff_pre_act_weight', 'gate_weight', 'ff_post_act_weight')}
    del _L1_ffn_all

    def _L2_xattn_setup():
        import jax, jax.numpy as jnp
        import numpy as np
        DIM_IN = 128
        DIM_QK = 128
        DIM_V = 128
        key = jax.random.key(seed)
        ks = jax.random.split(key, 8)
        s = DIM_IN ** (-0.5)
        return {'x': jax.random.normal(ks[0], (16, 256, DIM_IN), dtype=jnp.float32), 'encoder_output': jax.random.normal(ks[1], (16, 256, DIM_IN), dtype=jnp.float32), 'W_q': jax.random.normal(ks[2], (DIM_IN, DIM_QK), dtype=jnp.float32) * s, 'b_q': jnp.zeros((DIM_QK,), dtype=jnp.float32), 'W_k': jax.random.normal(ks[3], (DIM_IN, DIM_QK), dtype=jnp.float32) * s, 'b_k': jnp.zeros((DIM_QK,), dtype=jnp.float32), 'W_v': jax.random.normal(ks[4], (DIM_IN, DIM_V), dtype=jnp.float32) * s, 'b_v': jnp.zeros((DIM_V,), dtype=jnp.float32)}
    _L2_xattn_all = _L2_xattn_setup()
    _L2_xattn_in = {k: v for k, v in _L2_xattn_all.items() if k in ('W_q', 'b_q', 'W_k', 'b_k', 'W_v', 'b_v')}
    del _L2_xattn_all

    def _L2_attn_setup():
        import jax, jax.numpy as jnp
        import numpy as np
        import math
        N_HEAD = 16
        N_EMBD = 128
        HEAD_D = N_EMBD // N_HEAD
        BASE = 1250

        def rope(Y):
            d = Y.shape[-1]
            t = Y.shape[-2]
            theta = BASE ** (-2.0 * jnp.arange(d // 2, dtype=Y.dtype) / d)
            theta2 = jnp.concatenate([theta, theta], axis=0)
            pos = jnp.arange(1, t + 1, dtype=Y.dtype)
            C = pos[:, None] * theta2[None, :]
            cos, sin = (jnp.cos(C), jnp.sin(C))
            Y2 = jnp.concatenate([-Y[..., d // 2:], Y[..., :d // 2]], axis=-1)
            return Y * cos + Y2 * sin
        key = jax.random.key(seed)
        ks = jax.random.split(key, 9)
        s = 0.02
        x = jax.random.normal(ks[0], (4, 256, N_EMBD), dtype=jnp.float32)
        Wq = jax.random.normal(ks[1], (N_EMBD, N_EMBD), dtype=jnp.float32) * s
        bq = jnp.zeros((N_EMBD,), dtype=jnp.float32)
        Wk = jax.random.normal(ks[2], (N_EMBD, N_EMBD), dtype=jnp.float32) * s
        bk = jnp.zeros((N_EMBD,), dtype=jnp.float32)
        Wv = jax.random.normal(ks[3], (N_EMBD, N_EMBD), dtype=jnp.float32) * s
        bv = jnp.zeros((N_EMBD,), dtype=jnp.float32)
        Wo = jax.random.normal(ks[4], (N_EMBD, N_EMBD), dtype=jnp.float32) * s
        bo = jnp.zeros((N_EMBD,), dtype=jnp.float32)
        return {'x': x, 'Wq': Wq, 'bq': bq, 'Wk': Wk, 'bk': bk, 'Wv': Wv, 'bv': bv, 'Wo': Wo, 'bo': bo}
    _L2_attn_all = _L2_attn_setup()
    _L2_attn_in = {k: v for k, v in _L2_attn_all.items() if k in ('Wq', 'bq', 'Wk', 'bk', 'Wv', 'bv', 'Wo', 'bo')}
    del _L2_attn_all

    def _L2_ffn_setup():
        import jax, jax.numpy as jnp
        import numpy as np
        TOPK = 4
        key = jax.random.key(seed)
        ks = jax.random.split(key, 9)
        B, T, D = (4, 256, 128)
        E, H = (32, 128)
        HS = H * TOPK
        s = lambda k, shape, fan: jax.random.normal(k, shape, dtype=jnp.float32) / np.sqrt(fan)
        return {'x': jax.random.normal(ks[0], (B, T, D), dtype=jnp.float32), 'router_w': s(ks[1], (E, D), D), 'router_bias': jnp.zeros((E,), dtype=jnp.float32), 'gate_w': s(ks[2], (E, H, D), D), 'up_w': s(ks[3], (E, H, D), D), 'down_w': s(ks[4], (E, D, H), H), 'sgate_w': s(ks[5], (HS, D), D), 'sup_w': s(ks[6], (HS, D), D), 'sdown_w': s(ks[7], (D, HS), HS)}
    _L2_ffn_all = _L2_ffn_setup()
    _L2_ffn_in = {k: v for k, v in _L2_ffn_all.items() if k in ('router_w', 'router_bias', 'gate_w', 'up_w', 'down_w', 'sgate_w', 'sup_w', 'sdown_w')}
    del _L2_ffn_all

    def _L3_xattn_setup():
        import jax, jax.numpy as jnp
        import numpy as np
        NUM_HEADS = 16
        D_MODEL = 128
        D_K = D_MODEL // NUM_HEADS

        def _split_heads(x):
            B, S, _ = x.shape
            return x.reshape(B, S, NUM_HEADS, D_K).transpose(0, 2, 1, 3)
        key = jax.random.key(seed)
        ks = jax.random.split(key, 11)
        B, S, D = (1, 512, D_MODEL)
        scale = 1.0 / np.sqrt(D)
        return {'Q': jax.random.normal(ks[0], (B, S, D), jnp.float32), 'K': jax.random.normal(ks[1], (B, S, D), jnp.float32), 'V': jax.random.normal(ks[2], (B, S, D), jnp.float32), 'W_Q': jax.random.normal(ks[3], (D, D), jnp.float32) * scale, 'b_Q': jax.random.normal(ks[4], (D,), jnp.float32) * 0.02, 'W_K': jax.random.normal(ks[5], (D, D), jnp.float32) * scale, 'b_K': jax.random.normal(ks[6], (D,), jnp.float32) * 0.02, 'W_V': jax.random.normal(ks[7], (D, D), jnp.float32) * scale, 'b_V': jax.random.normal(ks[8], (D,), jnp.float32) * 0.02, 'W_O': jax.random.normal(ks[9], (D, D), jnp.float32) * scale, 'b_O': jax.random.normal(ks[10], (D,), jnp.float32) * 0.02}
    _L3_xattn_all = _L3_xattn_setup()
    _L3_xattn_in = {k: v for k, v in _L3_xattn_all.items() if k in ('W_Q', 'b_Q', 'W_K', 'b_K', 'W_V', 'b_V', 'W_O', 'b_O')}
    del _L3_xattn_all

    def _L3_attn_setup():
        import jax, jax.numpy as jnp
        import numpy as np
        EMB = 128
        HEADS = 16
        HEAD_DIM = EMB // HEADS
        ROPE_BASE = 10000.0

        def rotate_half(x):
            x1 = x[..., ::2]
            x2 = x[..., 1::2]
            return jnp.stack((-x2, x1), axis=-1).reshape(x.shape)

        def rope_cos_sin(seq_len, head_dim):
            inv_freq = 1.0 / ROPE_BASE ** (jnp.arange(0, head_dim, 2, dtype=jnp.float32) / head_dim)
            pos = jnp.arange(seq_len, dtype=jnp.float32)
            freqs = jnp.outer(pos, inv_freq)
            emb = jnp.concatenate([freqs, freqs], -1)
            return (jnp.cos(emb)[None, None], jnp.sin(emb)[None, None])
        key = jax.random.key(seed)
        ks = jax.random.split(key, 5)
        B, S = (2, 256)
        x = jax.random.normal(ks[0], (B, S, EMB), dtype=jnp.float32)
        scale = EMB ** (-0.5)
        Wq = jax.random.normal(ks[1], (EMB, EMB), dtype=jnp.float32) * scale
        Wk = jax.random.normal(ks[2], (EMB, EMB), dtype=jnp.float32) * scale
        Wv = jax.random.normal(ks[3], (EMB, EMB), dtype=jnp.float32) * scale
        Wo = jax.random.normal(ks[4], (EMB, EMB), dtype=jnp.float32) * scale
        return {'x': x, 'Wq': Wq, 'Wk': Wk, 'Wv': Wv, 'Wo': Wo}
    _L3_attn_all = _L3_attn_setup()
    _L3_attn_in = {k: v for k, v in _L3_attn_all.items() if k in ('Wq', 'Wk', 'Wv', 'Wo')}
    del _L3_attn_all

    def _L3_ffn_setup():
        import jax, jax.numpy as jnp
        import numpy as np
        N_EXPERTS = 32
        TOP_K = 8
        N_GROUP = 4
        TOPK_GROUP = 2
        ROUTED_SCALING = 2.5

        def _gate(x, gate_w, gate_bias):
            T, E = (x.shape[0], gate_w.shape[0])
            logits = jnp.einsum('th,eh->te', x, gate_w)
            scores = jax.nn.sigmoid(logits)
            scores_choice = scores + gate_bias[None, :]
            grp = scores_choice.reshape(T, N_GROUP, E // N_GROUP)
            top2, _ = jax.lax.top_k(grp, 2)
            group_scores = top2.sum(-1)
            _, grp_idx = jax.lax.top_k(group_scores, TOPK_GROUP)
            group_mask = jax.nn.one_hot(grp_idx, N_GROUP, dtype=scores.dtype).sum(1)
            expert_mask = jnp.repeat(group_mask, E // N_GROUP, axis=1)
            masked = jnp.where(expert_mask > 0, scores_choice, 0.0)
            _, topk_idx = jax.lax.top_k(masked, TOP_K)
            topk_w = jnp.take_along_axis(scores, topk_idx, axis=1)
            topk_w = topk_w / (topk_w.sum(-1, keepdims=True) + 1e-20)
            topk_w = topk_w * ROUTED_SCALING
            return (topk_idx, topk_w)

        def _mlp(x, wg, wu, wd):
            return jnp.einsum('...i,hi->...h', jax.nn.silu(jnp.einsum('...h,ih->...i', x, wg)) * jnp.einsum('...h,ih->...i', x, wu), wd)
        key = jax.random.key(seed)
        ks = jax.random.split(key, 9)
        B, S, H, I = (2, 64, 128, 64)
        w = 0.02
        return {'hidden_states': jax.random.normal(ks[0], (B, S, H), jnp.float32), 'gate_w': jax.random.normal(ks[1], (N_EXPERTS, H), jnp.float32) * w, 'gate_bias': jax.random.normal(ks[2], (N_EXPERTS,), jnp.float32) * w, 'expert_gate': jax.random.normal(ks[3], (N_EXPERTS, I, H), jnp.float32) * w, 'expert_up': jax.random.normal(ks[4], (N_EXPERTS, I, H), jnp.float32) * w, 'expert_down': jax.random.normal(ks[5], (N_EXPERTS, H, I), jnp.float32) * w, 'shared_gate': jax.random.normal(ks[6], (2 * I, H), jnp.float32) * w, 'shared_up': jax.random.normal(ks[7], (2 * I, H), jnp.float32) * w, 'shared_down': jax.random.normal(ks[8], (H, 2 * I), jnp.float32) * w}
    _L3_ffn_all = _L3_ffn_setup()
    _L3_ffn_in = {k: v for k, v in _L3_ffn_all.items() if k in ('gate_w', 'gate_bias', 'expert_gate', 'expert_up', 'expert_down', 'shared_gate', 'shared_up', 'shared_down')}
    del _L3_ffn_all
    return {'x': x, 'ctx_1024': ctx_1024, 'L0_xattn_W': _L0_xattn_in['W'], 'L0_xattn_b': _L0_xattn_in['b'], 'L0_attn_attention_mask': _L0_attn_in['attention_mask'], 'L0_attn_Wq': _L0_attn_in['Wq'], 'L0_attn_bq': _L0_attn_in['bq'], 'L0_attn_Wk': _L0_attn_in['Wk'], 'L0_attn_bk': _L0_attn_in['bk'], 'L0_attn_Wv': _L0_attn_in['Wv'], 'L0_attn_bv': _L0_attn_in['bv'], 'L0_attn_Wd': _L0_attn_in['Wd'], 'L0_attn_bd': _L0_attn_in['bd'], 'L0_attn_gamma': _L0_attn_in['gamma'], 'L0_attn_beta': _L0_attn_in['beta'], 'L0_ffn_wg': _L0_ffn_in['wg'], 'L0_ffn_w1': _L0_ffn_in['w1'], 'L0_ffn_b1': _L0_ffn_in['b1'], 'L0_ffn_w2': _L0_ffn_in['w2'], 'L0_ffn_b2': _L0_ffn_in['b2'], 'L1_xattn_Wq': _L1_xattn_in['Wq'], 'L1_xattn_bq': _L1_xattn_in['bq'], 'L1_xattn_Wk': _L1_xattn_in['Wk'], 'L1_xattn_bk': _L1_xattn_in['bk'], 'L1_xattn_Wv': _L1_xattn_in['Wv'], 'L1_xattn_bv': _L1_xattn_in['bv'], 'L1_xattn_Wo': _L1_xattn_in['Wo'], 'L1_xattn_bo': _L1_xattn_in['bo'], 'L1_attn_ln1_g': _L1_attn_in['ln1_g'], 'L1_attn_ln1_b': _L1_attn_in['ln1_b'], 'L1_attn_Wqf': _L1_attn_in['Wqf'], 'L1_attn_bqf': _L1_attn_in['bqf'], 'L1_attn_Wkf': _L1_attn_in['Wkf'], 'L1_attn_bkf': _L1_attn_in['bkf'], 'L1_attn_Wqp': _L1_attn_in['Wqp'], 'L1_attn_bqp': _L1_attn_in['bqp'], 'L1_attn_Wkp': _L1_attn_in['Wkp'], 'L1_attn_bkp': _L1_attn_in['bkp'], 'L1_attn_Wv': _L1_attn_in['Wv'], 'L1_attn_bv': _L1_attn_in['bv'], 'L1_attn_Wo': _L1_attn_in['Wo'], 'L1_attn_bo': _L1_attn_in['bo'], 'L1_attn_iscale': _L1_attn_in['iscale'], 'L1_attn_ln2_g': _L1_attn_in['ln2_g'], 'L1_attn_ln2_b': _L1_attn_in['ln2_b'], 'L1_attn_W1': _L1_attn_in['W1'], 'L1_attn_b1': _L1_attn_in['b1'], 'L1_attn_W2': _L1_attn_in['W2'], 'L1_attn_b2': _L1_attn_in['b2'], 'L1_ffn_router_weight': _L1_ffn_in['router_weight'], 'L1_ffn_ff_pre_act_weight': _L1_ffn_in['ff_pre_act_weight'], 'L1_ffn_gate_weight': _L1_ffn_in['gate_weight'], 'L1_ffn_ff_post_act_weight': _L1_ffn_in['ff_post_act_weight'], 'L2_xattn_W_q': _L2_xattn_in['W_q'], 'L2_xattn_b_q': _L2_xattn_in['b_q'], 'L2_xattn_W_k': _L2_xattn_in['W_k'], 'L2_xattn_b_k': _L2_xattn_in['b_k'], 'L2_xattn_W_v': _L2_xattn_in['W_v'], 'L2_xattn_b_v': _L2_xattn_in['b_v'], 'L2_attn_Wq': _L2_attn_in['Wq'], 'L2_attn_bq': _L2_attn_in['bq'], 'L2_attn_Wk': _L2_attn_in['Wk'], 'L2_attn_bk': _L2_attn_in['bk'], 'L2_attn_Wv': _L2_attn_in['Wv'], 'L2_attn_bv': _L2_attn_in['bv'], 'L2_attn_Wo': _L2_attn_in['Wo'], 'L2_attn_bo': _L2_attn_in['bo'], 'L2_ffn_router_w': _L2_ffn_in['router_w'], 'L2_ffn_router_bias': _L2_ffn_in['router_bias'], 'L2_ffn_gate_w': _L2_ffn_in['gate_w'], 'L2_ffn_up_w': _L2_ffn_in['up_w'], 'L2_ffn_down_w': _L2_ffn_in['down_w'], 'L2_ffn_sgate_w': _L2_ffn_in['sgate_w'], 'L2_ffn_sup_w': _L2_ffn_in['sup_w'], 'L2_ffn_sdown_w': _L2_ffn_in['sdown_w'], 'L3_xattn_W_Q': _L3_xattn_in['W_Q'], 'L3_xattn_b_Q': _L3_xattn_in['b_Q'], 'L3_xattn_W_K': _L3_xattn_in['W_K'], 'L3_xattn_b_K': _L3_xattn_in['b_K'], 'L3_xattn_W_V': _L3_xattn_in['W_V'], 'L3_xattn_b_V': _L3_xattn_in['b_V'], 'L3_xattn_W_O': _L3_xattn_in['W_O'], 'L3_xattn_b_O': _L3_xattn_in['b_O'], 'L3_attn_Wq': _L3_attn_in['Wq'], 'L3_attn_Wk': _L3_attn_in['Wk'], 'L3_attn_Wv': _L3_attn_in['Wv'], 'L3_attn_Wo': _L3_attn_in['Wo'], 'L3_ffn_gate_w': _L3_ffn_in['gate_w'], 'L3_ffn_gate_bias': _L3_ffn_in['gate_bias'], 'L3_ffn_expert_gate': _L3_ffn_in['expert_gate'], 'L3_ffn_expert_up': _L3_ffn_in['expert_up'], 'L3_ffn_expert_down': _L3_ffn_in['expert_down'], 'L3_ffn_shared_gate': _L3_ffn_in['shared_gate'], 'L3_ffn_shared_up': _L3_ffn_in['shared_up'], 'L3_ffn_shared_down': _L3_ffn_in['shared_down']}

def reference(x, ctx_1024, L0_xattn_W, L0_xattn_b, L0_attn_attention_mask, L0_attn_Wq, L0_attn_bq, L0_attn_Wk, L0_attn_bk, L0_attn_Wv, L0_attn_bv, L0_attn_Wd, L0_attn_bd, L0_attn_gamma, L0_attn_beta, L0_ffn_wg, L0_ffn_w1, L0_ffn_b1, L0_ffn_w2, L0_ffn_b2, L1_xattn_Wq, L1_xattn_bq, L1_xattn_Wk, L1_xattn_bk, L1_xattn_Wv, L1_xattn_bv, L1_xattn_Wo, L1_xattn_bo, L1_attn_ln1_g, L1_attn_ln1_b, L1_attn_Wqf, L1_attn_bqf, L1_attn_Wkf, L1_attn_bkf, L1_attn_Wqp, L1_attn_bqp, L1_attn_Wkp, L1_attn_bkp, L1_attn_Wv, L1_attn_bv, L1_attn_Wo, L1_attn_bo, L1_attn_iscale, L1_attn_ln2_g, L1_attn_ln2_b, L1_attn_W1, L1_attn_b1, L1_attn_W2, L1_attn_b2, L1_ffn_router_weight, L1_ffn_ff_pre_act_weight, L1_ffn_gate_weight, L1_ffn_ff_post_act_weight, L2_xattn_W_q, L2_xattn_b_q, L2_xattn_W_k, L2_xattn_b_k, L2_xattn_W_v, L2_xattn_b_v, L2_attn_Wq, L2_attn_bq, L2_attn_Wk, L2_attn_bk, L2_attn_Wv, L2_attn_bv, L2_attn_Wo, L2_attn_bo, L2_ffn_router_w, L2_ffn_router_bias, L2_ffn_gate_w, L2_ffn_up_w, L2_ffn_down_w, L2_ffn_sgate_w, L2_ffn_sup_w, L2_ffn_sdown_w, L3_xattn_W_Q, L3_xattn_b_Q, L3_xattn_W_K, L3_xattn_b_K, L3_xattn_W_V, L3_xattn_b_V, L3_xattn_W_O, L3_xattn_b_O, L3_attn_Wq, L3_attn_Wk, L3_attn_Wv, L3_attn_Wo, L3_ffn_gate_w, L3_ffn_gate_bias, L3_ffn_expert_gate, L3_ffn_expert_up, L3_ffn_expert_down, L3_ffn_shared_gate, L3_ffn_shared_up, L3_ffn_shared_down):
    import jax
    import jax.numpy as jnp

    def _L0_xattn_ref(ix, iother, W, b):
        import jax, jax.numpy as jnp
        import numpy as np
        ex = jnp.einsum('bld,ed->ble', ix, W) + b
        eother = jnp.einsum('bld,ed->ble', iother, W) + b
        scores = jnp.einsum('bld,bmd->blm', ex, eother)
        attn = jax.nn.softmax(scores, axis=-1)
        aligned = jnp.einsum('blm,bmd->bld', attn, iother)
        return aligned

    def _L0_attn_ref(input_tensor, attention_mask, Wq, bq, Wk, bk, Wv, bv, Wd, bd, gamma, beta):
        import jax, jax.numpy as jnp
        import numpy as np
        B, S, H, NH = (8, 512, 128, 16)
        HD = H // NH
        EPS_ATTN = 1e-06
        EPS_LN = 1e-12
        x = input_tensor
        b, s, h = x.shape
        q = (x @ Wq.T + bq).reshape(b, s, NH, HD)
        k = (x @ Wk.T + bk).reshape(b, s, NH, HD)
        v = (x @ Wv.T + bv).reshape(b, s, NH, HD)
        q = jax.nn.elu(q) + 1.0
        k = jax.nn.elu(k) + 1.0
        kv = jnp.einsum('nshd,nshm->nhmd', k, v)
        z = 1.0 / jnp.einsum('nlhd,nhd->nlh', q, k.sum(axis=1) + EPS_ATTN)
        ctx = jnp.einsum('nlhd,nhmd,nlh->nlhm', q, kv, z).reshape(b, s, h)
        hs = ctx @ Wd.T + bd
        hs = hs + x
        mu = hs.mean(axis=-1, keepdims=True)
        var = ((hs - mu) ** 2).mean(axis=-1, keepdims=True)
        out = (hs - mu) / jnp.sqrt(var + EPS_LN) * gamma + beta
        return out

    def _L0_ffn_ref(x, wg, w1, b1, w2, b2):
        import jax, jax.numpy as jnp
        import numpy as np
        E = 8
        K = 2
        CAP_FACTOR = 1.0
        B, S, M = x.shape
        N = B * S
        capacity = int(CAP_FACTOR * K * N // E)
        xt = x.reshape(N, M)
        logits = xt @ wg
        scores = jax.nn.softmax(logits, axis=-1)
        topv, topi = jax.lax.top_k(scores, K)
        topv = topv / jnp.sum(topv, axis=-1, keepdims=True)
        masks = jax.nn.one_hot(topi.T, E, dtype=jnp.int32)
        flat = masks.reshape(K * N, E)
        locs = jnp.cumsum(flat, axis=0) - 1
        pos = jnp.sum(locs * flat, axis=-1).reshape(K, N).T
        valid = pos < capacity
        gate = topv * valid.astype(topv.dtype)
        pos_c = jnp.where(valid, pos, 0)
        xk = xt[:, None, :] * valid[..., None].astype(xt.dtype)
        disp = jnp.zeros((E, capacity, M), xt.dtype)
        disp = disp.at[topi, pos_c].add(xk)
        h = jax.nn.relu(jnp.einsum('ecm,emh->ech', disp, w1) + b1[:, None, :])
        y = jnp.einsum('ech,ehm->ecm', h, w2) + b2[:, None, :]
        out = jnp.sum(gate[..., None] * y[topi, pos_c], axis=1)
        return out.reshape(B, S, M)

    def _L1_xattn_ref(queries, keys, values, Wq, bq, Wk, bk, Wv, bv, Wo, bo):
        import jax, jax.numpy as jnp
        import numpy as np
        import math
        D_MODEL = 128
        N_HEADS = 16
        D_HEAD = D_MODEL // N_HEADS
        N, L, _ = queries.shape
        S = keys.shape[1]
        H, D = (N_HEADS, D_HEAD)
        q = (queries @ Wq + bq).reshape(N, L, H, D)
        k = (keys @ Wk + bk).reshape(N, S, H, D)
        v = (values @ Wv + bv).reshape(N, S, H, D)
        sm = jnp.einsum('nlhd,nshd->nlhs', q, k) / math.sqrt(D)
        sm = jax.nn.softmax(sm, axis=1)
        attn = jnp.einsum('nlhs,nshd->nlhd', sm, v).reshape(N, L, H * D)
        return attn @ Wo + bo

    def _L1_attn_ref(x, ln1_g, ln1_b, Wqf, bqf, Wkf, bkf, Wqp, bqp, Wkp, bkp, Wv, bv, Wo, bo, iscale, ln2_g, ln2_b, W1, b1, W2, b2):
        import jax, jax.numpy as jnp
        import numpy as np
        D_MODEL = 128
        N_HEADS = 16
        N_WAVES = 16
        D_FF = 4 * D_MODEL
        LN_EPS = 1e-05
        NORM_EPS = 1e-12

        def _layernorm(x, g, b):
            m = jnp.mean(x, axis=-1, keepdims=True)
            v = jnp.mean(jnp.square(x - m), axis=-1, keepdims=True)
            return (x - m) * jax.lax.rsqrt(v + LN_EPS) * g + b

        def _l2norm(x):
            n = jnp.sqrt(jnp.sum(jnp.square(x), axis=-1, keepdims=True))
            return x / jnp.maximum(n, NORM_EPS)

        def _wave_block(x, ln1_g, ln1_b, Wqf, bqf, Wkf, bkf, Wqp, bqp, Wkp, bkp, Wv, bv, Wo, bo, iscale, ln2_g, ln2_b, W1, b1, W2, b2):
            B, T, C = x.shape
            H, W, Dh = (N_HEADS, N_WAVES, C // N_HEADS)
            xn = _layernorm(x, ln1_g, ln1_b)

            def proj(Wm, bm):
                return (xn @ Wm + bm).reshape(B, T, H, W).transpose(0, 2, 1, 3)
            q_f, k_f = (proj(Wqf, bqf), proj(Wkf, bkf))
            q_p, k_p = (proj(Wqp, bqp), proj(Wkp, bkp))
            v = (xn @ Wv + bv).reshape(B, T, H, Dh).transpose(0, 2, 1, 3)
            t_pos = jnp.arange(T, dtype=x.dtype)[None, None, :, None]
            q_norm = _l2norm(jnp.sin(q_f * t_pos + q_p))
            k_norm = _l2norm(jnp.sin(k_f * t_pos + k_p))
            inter = jnp.einsum('bhtw,bhsw->bhts', q_norm, k_norm) * iscale
            causal = jnp.tril(jnp.ones((T, T), dtype=x.dtype))
            inter = inter * causal
            num_attended = jnp.sqrt(jnp.arange(1, T + 1, dtype=x.dtype))[None, None, :, None]
            attn = inter / num_attended
            out = jnp.einsum('bhts,bhsd->bhtd', attn, v)
            out = out.transpose(0, 2, 1, 3).reshape(B, T, C) @ Wo + bo
            x = x + out
            hpre = _layernorm(x, ln2_g, ln2_b) @ W1 + b1
            hact = jax.nn.gelu(hpre, approximate=False) + 0.1 * jnp.sin(hpre)
            x = x + hact @ W2 + b2
            return x
        return _wave_block(x, ln1_g, ln1_b, Wqf, bqf, Wkf, bkf, Wqp, bqp, Wkp, bkp, Wv, bv, Wo, bo, iscale, ln2_g, ln2_b, W1, b1, W2, b2)

    def _L1_ffn_ref(x, router_weight, ff_pre_act_weight, gate_weight, ff_post_act_weight):
        import jax, jax.numpy as jnp
        import numpy as np
        import math
        DMODEL = 128
        DFF = 512
        NUM_EXPERTS = 8
        TOPK = 2
        CAP_FACTOR = 1.25
        EPS = 1.1920929e-07

        def _trunc_normal(key, shape, fan_in, scale=1.0):
            std = scale * (1.0 / fan_in) ** 0.5
            return jax.random.truncated_normal(key, -2.0, 2.0, shape, jnp.float32) * std
        orig_shape = x.shape
        h = x.reshape(-1, DMODEL)
        T = h.shape[0]
        logits = jnp.einsum('th,eh->te', h, router_weight)
        probs = jax.nn.softmax(logits.astype(jnp.float32), axis=-1)
        topk_probs, selected = jax.lax.top_k(probs, TOPK)
        topk_probs = topk_probs / jnp.maximum(topk_probs.sum(-1, keepdims=True), EPS)
        flat_tokens = jnp.repeat(jnp.arange(T), TOPK)
        flat_experts = selected.reshape(-1)
        flat_weights = topk_probs.reshape(-1)
        A = T * TOPK
        capacity = max(1, math.ceil(CAP_FACTOR * A / NUM_EXPERTS))
        weight_order = jnp.argsort(-flat_weights, stable=True)
        grouped_order = jnp.argsort(flat_experts[weight_order], stable=True)
        sort_order = weight_order[grouped_order]
        se = flat_experts[sort_order]
        st = flat_tokens[sort_order]
        sw = flat_weights[sort_order]
        counts = jnp.bincount(se, length=NUM_EXPERTS)
        offsets = jnp.cumsum(counts) - counts
        slot = jnp.arange(A) - offsets[se]
        keep = slot < capacity
        sw = jnp.where(keep, sw, 0.0)
        token_wsum = jnp.zeros(T, jnp.float32).at[st].add(sw)
        kept_w = sw / jnp.maximum(token_wsum[st], EPS)
        FC = NUM_EXPERTS * capacity
        dispatch = jnp.where(keep, se * capacity + slot, FC)
        expert_inputs = jnp.zeros((FC + 1, DMODEL), x.dtype).at[dispatch].set(h[st])
        expert_inputs = expert_inputs[:FC].reshape(NUM_EXPERTS, capacity, DMODEL)
        pre = jnp.einsum('ech,edh->ecd', expert_inputs, ff_pre_act_weight)
        gate = jnp.einsum('ech,edh->ecd', expert_inputs, gate_weight)
        expert_out = jnp.einsum('ecd,ehd->ech', pre * jax.nn.silu(gate), ff_post_act_weight)
        eo_flat = jnp.concatenate([expert_out.reshape(FC, DMODEL), jnp.zeros((1, DMODEL), x.dtype)], axis=0)
        updates = eo_flat[dispatch] * kept_w.astype(x.dtype)[:, None]
        out = jnp.zeros((T, DMODEL), x.dtype).at[st].add(updates)
        return out.reshape(orig_shape)

    def _L2_xattn_ref(x, encoder_output, W_q, b_q, W_k, b_k, W_v, b_v):
        import jax, jax.numpy as jnp
        import numpy as np
        DIM_IN = 128
        DIM_QK = 128
        DIM_V = 128
        Q = x @ W_q + b_q
        K = encoder_output @ W_k + b_k
        V = encoder_output @ W_v + b_v
        scores = jnp.einsum('bqd,bkd->bqk', Q, K) * K.shape[-1] ** (-0.5)
        weights = jax.nn.softmax(scores, axis=-1)
        H = jnp.einsum('bqk,bkv->bqv', weights, V)
        return H

    def _L2_attn_ref(x, Wq, bq, Wk, bk, Wv, bv, Wo, bo):
        import jax, jax.numpy as jnp
        import numpy as np
        import math
        N_HEAD = 16
        N_EMBD = 128
        HEAD_D = N_EMBD // N_HEAD
        BASE = 1250

        def rope(Y):
            d = Y.shape[-1]
            t = Y.shape[-2]
            theta = BASE ** (-2.0 * jnp.arange(d // 2, dtype=Y.dtype) / d)
            theta2 = jnp.concatenate([theta, theta], axis=0)
            pos = jnp.arange(1, t + 1, dtype=Y.dtype)
            C = pos[:, None] * theta2[None, :]
            cos, sin = (jnp.cos(C), jnp.sin(C))
            Y2 = jnp.concatenate([-Y[..., d // 2:], Y[..., :d // 2]], axis=-1)
            return Y * cos + Y2 * sin
        b, t, _ = x.shape

        def split_heads(y):
            return y.reshape(b, t, N_HEAD, HEAD_D).transpose(0, 2, 1, 3)
        q = split_heads(x @ Wq.T + bq)
        k = split_heads(x @ Wk.T + bk)
        v = split_heads(x @ Wv.T + bv)
        q, k = (rope(q), rope(k))
        scale = math.sqrt(HEAD_D)
        att = jnp.einsum('bhqd,bhkd->bhqk', q, k) / scale
        mask = jnp.tril(jnp.ones((t, t), dtype=bool))
        att = jnp.where(mask, att, -jnp.inf)
        att = jax.nn.softmax(att, axis=-1)
        y = jnp.einsum('bhqk,bhkd->bhqd', att, v)
        y = y.transpose(0, 2, 1, 3).reshape(b, t, N_EMBD)
        return y @ Wo.T + bo

    def _L2_ffn_ref(x, router_w, router_bias, gate_w, up_w, down_w, sgate_w, sup_w, sdown_w):
        import jax, jax.numpy as jnp
        import numpy as np
        TOPK = 4
        B, T, D = x.shape
        flat = x.reshape(B * T, D)
        logits = flat.astype(jnp.float32) @ router_w.T + router_bias
        scores = jax.nn.softmax(logits, axis=-1)
        topk_scores, topk_idx = jax.lax.top_k(scores, TOPK)
        topk_scores = topk_scores / jnp.clip(topk_scores.sum(axis=-1, keepdims=True), 1e-12, None)
        h = jax.nn.silu(jnp.einsum('nd,ehd->neh', flat, gate_w)) * jnp.einsum('nd,ehd->neh', flat, up_w)
        expert_out = jnp.einsum('neh,edh->ned', h, down_w)
        sel = jnp.take_along_axis(expert_out, topk_idx[:, :, None], axis=1)
        out = (sel * topk_scores.astype(flat.dtype)[:, :, None]).sum(axis=1)
        out = out + jax.nn.silu(flat @ sgate_w.T) * (flat @ sup_w.T) @ sdown_w.T
        return out.reshape(B, T, D)

    def _L3_xattn_ref(Q, K, V, W_Q, b_Q, W_K, b_K, W_V, b_V, W_O, b_O):
        import jax, jax.numpy as jnp
        import numpy as np
        NUM_HEADS = 16
        D_MODEL = 128
        D_K = D_MODEL // NUM_HEADS

        def _split_heads(x):
            B, S, _ = x.shape
            return x.reshape(B, S, NUM_HEADS, D_K).transpose(0, 2, 1, 3)
        q = _split_heads(Q @ W_Q + b_Q)
        k = _split_heads(K @ W_K + b_K)
        v = _split_heads(V @ W_V + b_V)
        inv_sqrt_dk = jnp.asarray(1.0 / np.sqrt(D_K), q.dtype)
        scores = jnp.einsum('bhqd,bhkd->bhqk', q, k) * inv_sqrt_dk
        weights = jax.nn.softmax(scores, axis=-1)
        out = jnp.einsum('bhqk,bhkd->bhqd', weights, v)
        B, _, S, _ = out.shape
        combined = out.transpose(0, 2, 1, 3).reshape(B, S, D_MODEL)
        return combined @ W_O + b_O

    def _L3_attn_ref(x, Wq, Wk, Wv, Wo):
        import jax, jax.numpy as jnp
        import numpy as np
        EMB = 128
        HEADS = 16
        HEAD_DIM = EMB // HEADS
        ROPE_BASE = 10000.0

        def rotate_half(x):
            x1 = x[..., ::2]
            x2 = x[..., 1::2]
            return jnp.stack((-x2, x1), axis=-1).reshape(x.shape)

        def rope_cos_sin(seq_len, head_dim):
            inv_freq = 1.0 / ROPE_BASE ** (jnp.arange(0, head_dim, 2, dtype=jnp.float32) / head_dim)
            pos = jnp.arange(seq_len, dtype=jnp.float32)
            freqs = jnp.outer(pos, inv_freq)
            emb = jnp.concatenate([freqs, freqs], -1)
            return (jnp.cos(emb)[None, None], jnp.sin(emb)[None, None])
        B, S, E = x.shape

        def shape_heads(t):
            return t.reshape(B, S, HEADS, HEAD_DIM).transpose(0, 2, 1, 3)
        q = shape_heads(x @ Wq.T)
        k = shape_heads(x @ Wk.T)
        v = shape_heads(x @ Wv.T)
        cos, sin = rope_cos_sin(S, HEAD_DIM)
        q = q * cos + rotate_half(q) * sin
        k = k * cos + rotate_half(k) * sin
        scale = HEAD_DIM ** (-0.5)
        scores = jnp.einsum('bhqd,bhkd->bhqk', q, k) * scale
        causal = jnp.triu(jnp.ones((S, S), dtype=bool), k=1)
        scores = jnp.where(causal, -jnp.inf, scores)
        attn = jax.nn.softmax(scores, axis=-1)
        out = jnp.einsum('bhqk,bhkd->bhqd', attn, v)
        out = out.transpose(0, 2, 1, 3).reshape(B, S, E)
        return out @ Wo.T

    def _L3_ffn_ref(hidden_states, gate_w, gate_bias, expert_gate, expert_up, expert_down, shared_gate, shared_up, shared_down):
        import jax, jax.numpy as jnp
        import numpy as np
        N_EXPERTS = 32
        TOP_K = 8
        N_GROUP = 4
        TOPK_GROUP = 2
        ROUTED_SCALING = 2.5

        def _gate(x, gate_w, gate_bias):
            T, E = (x.shape[0], gate_w.shape[0])
            logits = jnp.einsum('th,eh->te', x, gate_w)
            scores = jax.nn.sigmoid(logits)
            scores_choice = scores + gate_bias[None, :]
            grp = scores_choice.reshape(T, N_GROUP, E // N_GROUP)
            top2, _ = jax.lax.top_k(grp, 2)
            group_scores = top2.sum(-1)
            _, grp_idx = jax.lax.top_k(group_scores, TOPK_GROUP)
            group_mask = jax.nn.one_hot(grp_idx, N_GROUP, dtype=scores.dtype).sum(1)
            expert_mask = jnp.repeat(group_mask, E // N_GROUP, axis=1)
            masked = jnp.where(expert_mask > 0, scores_choice, 0.0)
            _, topk_idx = jax.lax.top_k(masked, TOP_K)
            topk_w = jnp.take_along_axis(scores, topk_idx, axis=1)
            topk_w = topk_w / (topk_w.sum(-1, keepdims=True) + 1e-20)
            topk_w = topk_w * ROUTED_SCALING
            return (topk_idx, topk_w)

        def _mlp(x, wg, wu, wd):
            return jnp.einsum('...i,hi->...h', jax.nn.silu(jnp.einsum('...h,ih->...i', x, wg)) * jnp.einsum('...h,ih->...i', x, wu), wd)
        orig_shape = hidden_states.shape
        H = orig_shape[-1]
        residuals = hidden_states
        x = hidden_states.reshape(-1, H)
        topk_idx, topk_w = _gate(x, gate_w, gate_bias)
        g = jnp.einsum('th,eih->eti', x, expert_gate)
        u = jnp.einsum('th,eih->eti', x, expert_up)
        outs = jnp.einsum('eti,ehi->eth', jax.nn.silu(g) * u, expert_down)
        outs_t = jnp.transpose(outs, (1, 0, 2))
        gathered = jnp.take_along_axis(outs_t, topk_idx[:, :, None], axis=1)
        final = (gathered * topk_w[:, :, None]).sum(1)
        shared = _mlp(residuals, shared_gate, shared_up, shared_down)
        return final.reshape(orig_shape) + shared
    x = x + _L0_xattn_ref(_layernorm(x, axis=-1), ctx_1024, L0_xattn_W, L0_xattn_b)
    x = x + _L0_attn_ref(_layernorm(x, axis=-1), L0_attn_attention_mask, L0_attn_Wq, L0_attn_bq, L0_attn_Wk, L0_attn_bk, L0_attn_Wv, L0_attn_bv, L0_attn_Wd, L0_attn_bd, L0_attn_gamma, L0_attn_beta)
    x = x + _L0_ffn_ref(_layernorm(x, axis=-1), L0_ffn_wg, L0_ffn_w1, L0_ffn_b1, L0_ffn_w2, L0_ffn_b2)
    x = x + _L1_xattn_ref(_layernorm(x, axis=-1), ctx_1024, ctx_1024, L1_xattn_Wq, L1_xattn_bq, L1_xattn_Wk, L1_xattn_bk, L1_xattn_Wv, L1_xattn_bv, L1_xattn_Wo, L1_xattn_bo)
    x = x + _L1_attn_ref(_layernorm(x, axis=-1), L1_attn_ln1_g, L1_attn_ln1_b, L1_attn_Wqf, L1_attn_bqf, L1_attn_Wkf, L1_attn_bkf, L1_attn_Wqp, L1_attn_bqp, L1_attn_Wkp, L1_attn_bkp, L1_attn_Wv, L1_attn_bv, L1_attn_Wo, L1_attn_bo, L1_attn_iscale, L1_attn_ln2_g, L1_attn_ln2_b, L1_attn_W1, L1_attn_b1, L1_attn_W2, L1_attn_b2)
    x = x + _L1_ffn_ref(_layernorm(x, axis=-1), L1_ffn_router_weight, L1_ffn_ff_pre_act_weight, L1_ffn_gate_weight, L1_ffn_ff_post_act_weight)
    x = x + _L2_xattn_ref(_layernorm(x, axis=-1), ctx_1024, L2_xattn_W_q, L2_xattn_b_q, L2_xattn_W_k, L2_xattn_b_k, L2_xattn_W_v, L2_xattn_b_v)
    x = x + _L2_attn_ref(_layernorm(x, axis=-1), L2_attn_Wq, L2_attn_bq, L2_attn_Wk, L2_attn_bk, L2_attn_Wv, L2_attn_bv, L2_attn_Wo, L2_attn_bo)
    x = x + _L2_ffn_ref(_layernorm(x, axis=-1), L2_ffn_router_w, L2_ffn_router_bias, L2_ffn_gate_w, L2_ffn_up_w, L2_ffn_down_w, L2_ffn_sgate_w, L2_ffn_sup_w, L2_ffn_sdown_w)
    x = x + _L3_xattn_ref(_layernorm(x, axis=-1), ctx_1024, ctx_1024, L3_xattn_W_Q, L3_xattn_b_Q, L3_xattn_W_K, L3_xattn_b_K, L3_xattn_W_V, L3_xattn_b_V, L3_xattn_W_O, L3_xattn_b_O)
    x = x + _L3_attn_ref(_layernorm(x, axis=-1), L3_attn_Wq, L3_attn_Wk, L3_attn_Wv, L3_attn_Wo)
    x = x + _L3_ffn_ref(_layernorm(x, axis=-1), L3_ffn_gate_w, L3_ffn_gate_bias, L3_ffn_expert_gate, L3_ffn_expert_up, L3_ffn_expert_down, L3_ffn_shared_gate, L3_ffn_shared_up, L3_ffn_shared_down)
    return x

_drawn_inputs = setup_inputs


def setup_inputs(seed=0):
    import zlib

    import numpy as np

    out = dict(_drawn_inputs(seed))
    spreads = {'L0_attn_bq': (0.0, 0.8),
     'L0_attn_bk': (0.0, 0.8),
     'L0_attn_bv': (0.0, 0.1),
     'L0_attn_bd': (0.0, 0.1),
     'L0_attn_gamma': (1.0, 0.2),
     'L0_attn_beta': (0.0, 0.1),
     'L0_ffn_b1': (0.0, 0.697),
     'L0_ffn_b2': (0.0, 0.28),
     'L1_xattn_bq': (0.0, 0.8),
     'L1_xattn_bk': (0.0, 0.1),
     'L1_xattn_bv': (0.0, 0.1),
     'L1_xattn_bo': (0.0, 0.1),
     'L1_attn_ln1_g': (1.0, 0.6),
     'L1_attn_ln1_b': (0.0, 0.8),
     'L1_attn_bqf': (0.0, 0.8),
     'L1_attn_bkf': (0.0, 0.8),
     'L1_attn_bqp': (0.0, 0.8),
     'L1_attn_bkp': (0.0, 0.8),
     'L1_attn_bv': (0.0, 0.8),
     'L1_attn_bo': (0.0, 0.1),
     'L1_attn_iscale': (1.0, 0.6),
     'L1_attn_ln2_g': (1.0, 0.6),
     'L1_attn_ln2_b': (0.0, 0.8),
     'L1_attn_b1': (0.0, 0.767),
     'L1_attn_b2': (0.0, 0.1),
     'L2_xattn_b_q': (0.0, 0.8),
     'L2_xattn_b_k': (0.0, 0.8),
     'L2_xattn_b_v': (0.0, 0.275),
     'L2_attn_bq': (0.0, 0.8),
     'L2_attn_bk': (0.0, 0.8),
     'L2_attn_bv': (0.0, 0.8),
     'L2_attn_bo': (0.0, 0.272),
     'L2_ffn_router_bias': (0.0, 0.408)}
    factors = {'L0_attn_Wq': 3.928,
     'L0_ffn_w1': 2.953,
     'L1_attn_Wqf': 8.0,
     'L1_attn_Wkf': 8.0,
     'L1_attn_Wqp': 8.0,
     'L1_attn_Wkp': 8.0,
     'L1_attn_Wv': 8.0,
     'L1_attn_Wo': 8.0,
     'L1_attn_W1': 2.879,
     'L2_attn_Wq': 8.0,
     'L2_attn_Wk': 8.0,
     'L2_attn_Wv': 6.105,
     'L2_attn_Wo': 4.958,
     'L3_xattn_b_Q': 8.0,
     'L3_xattn_b_K': 8.0,
     'L3_xattn_b_V': 8.0,
     'L3_xattn_b_O': 8.0,
     'L3_ffn_gate_w': 8.0,
     'L3_ffn_gate_bias': 8.0,
     'L3_ffn_expert_gate': 8.0,
     'L3_ffn_expert_up': 8.0,
     'L3_ffn_expert_down': 8.0,
     'L3_ffn_shared_gate': 8.0,
     'L3_ffn_shared_up': 8.0,
     'L3_ffn_shared_down': 8.0}
    for name, (base, spread) in spreads.items():
        noise = np.random.default_rng([zlib.crc32(name.encode()), seed]).standard_normal(out[name].shape)
        drawn = base * np.exp(spread * noise) if base else spread * noise
        out[name] = jnp.asarray(drawn.astype(out[name].dtype))
    for name, factor in factors.items():
        out[name] = (out[name] * factor).astype(out[name].dtype)
    return out
```

```python
from contextlib import ExitStack

import numpy as np
import concourse.bass as bass
from concourse import mybir

F32 = mybir.dt.float32
BF16 = mybir.dt.bfloat16
I32 = mybir.dt.int32
U32 = mybir.dt.uint32
ALU = mybir.AluOpType
ACT = mybir.ActivationFunctionType
AX = mybir.AxisListType

D = 128
B = 16
L = 64
S = 128
N = B * L
T = N // 128
H = 16
HD = D // H
W = 16
STAGES = 12



def const_columns():
    p = np.arange(128)
    c = {}
    c["ident"] = np.eye(128)
    c["ones"] = np.ones((128, 128))
    c["same_head"] = (p[:, None] // HD == p[None, :] // HD)
    c["head"] = (p[:, None] // HD == np.arange(H)[None, :])
    c["head_eps"] = c["head"] * 1e-6
    c["head_pair"] = (p[:, None] // (2 * HD) == np.arange(H // 2)[None, :])
    c["head_parity"] = (p[:, None] // HD % 2 == np.arange(2)[None, :])
    c["head_of_four"] = (p[:, None] // HD % 4 == np.arange(4)[None, :])
    c["wave_pair"] = (p[:, None] // (2 * W) == np.arange(4)[None, :])
    c["wave_parity"] = (p[:, None] // W % 2 == np.arange(2)[None, :])
    c["same_wave_head"] = (p[:, None] // W == p[None, :] // W)
    col = np.arange(32)
    ii, j = col // 16, col // 8 % 2
    r = p[:, None, None] // L
    k = np.arange(2)[None, :, None]
    c["value_soft"] = ((ii == r) & (j == k)).reshape(128, 64)
    c["value_wave"] = ((j == r) & (ii == k)).reshape(128, 64)
    s, t = p[:, None] % L, np.arange(L)[None, :]
    c["wave_causal"] = (s <= t) / np.sqrt(t + 1.0)
    c["position"] = np.broadcast_to(t, (128, L))
    f32 = np.float32
    d = p[:, None] % HD
    theta = f32(1250) ** (f32(-2.0) * (d % (HD // 2)).astype(f32) / f32(HD))
    ang = (t + 1).astype(f32) * theta.astype(f32)
    c["rope2_cos"] = np.cos(ang.astype(f32))
    c["rope2_sin"] = np.sin(ang.astype(f32)) * np.where(d < HD // 2, -1.0, 1.0)
    freq = f32(1.0) / f32(10000.0) ** ((2 * (d % (HD // 2))).astype(f32) / f32(HD))
    ang = t.astype(f32) * freq.astype(f32)
    c["rope3_cos"] = np.cos(ang.astype(f32))
    c["rope3_sin"] = np.sin(ang.astype(f32)) * np.where(d % 2 == 0, -1.0, 1.0)
    c["iota"] = np.broadcast_to(np.arange(32)[None, :], (128, 32))
    c["expert_row"] = (p[:, None] == np.arange(8)[None, :])
    return {k: np.asarray(v, np.float32) for k, v in c.items()}


def const_bf_columns():
    p = np.arange(128)
    c = {}
    c["identb"] = np.eye(128)
    c["earlier"] = (p[:, None] < p[None, :])
    c["onesb"] = np.ones((128, 128))
    c["same_expert"] = (p[:, None] % 8 == p[None, :] % 8)
    c["causal"] = np.where(np.arange(L)[None, None, :] <= p[:, None, None] % L, 0.0, -1e30) * np.ones((1, 8, 1))
    return {k: np.asarray(v, np.float32).reshape(128, -1) for k, v in c.items()}


SHIFTS = [26, 22, 18, 14, 10, 6, 2, 0]


def const_int_columns():
    return (np.arange(128)[:, None] // 8 << np.array(SHIFTS)[None, :]).astype(np.int32)



WEIGHTS = [
    [("l0x_w", 128)],
    [("l0a_wq", 128), ("l0a_wkv", 256), ("l0a_wd", 128)],
    [("l0f_wg", 8), ("l0f_b2", 1024)],
    [("l1x_wq", 128), ("l1x_wk", 128), ("l1x_wv", 128), ("l1x_wo", 128)],
    [("l1a_wqf", 256), ("l1a_wqp", 256), ("l1a_wkf", 256), ("l1a_wkp", 256), ("l1a_wv", 128),
     ("l1a_wo", 128), ("l1a_w1", 512), ("l1a_w2", 512)],
    [("l1f_wr", 8)],
    [("l2x_wq", 128), ("l2x_wk", 128), ("l2x_wv", 128)],
    [("l2a_wq", 128), ("l2a_wqr", 128), ("l2a_wk", 128), ("l2a_wkr", 128), ("l2a_wv", 128), ("l2a_wo", 128)],
    [("l2f_wr", 32)],
    [("l3x_wq", 128), ("l3x_wk", 128), ("l3x_wv", 128), ("l3x_wo", 128)],
    [("l3a_wq", 128), ("l3a_wqr", 128), ("l3a_wk", 128), ("l3a_wkr", 128), ("l3a_wv", 128), ("l3a_wo", 128)],
    [("l3f_wg", 32)],
]
ROWS = [("l0a_bkv", 256), ("l0a_bd", 128), ("l0a_gamma", 128), ("l0a_beta", 128), ("l1x_bv", 128), ("l1x_bo", 128),
        ("l1a_g1", 128), ("l1a_be1", 128), ("l1a_bv", 128), ("l1a_bo", 128), ("l1a_iscale", 16), ("l1a_g2", 128),
        ("l1a_be2", 128), ("l1a_b2", 128), ("l2x_bv", 128), ("l2a_bv", 128), ("l2a_bo", 128), ("l2f_br", 32),
        ("l3x_bv", 128), ("l3x_bo", 128), ("l3f_bg", 32)]
BIASES = [("l0x_b", 1), ("l0a_bq", 1), ("l1x_bq", 1), ("l1x_bk", 1), ("l1a_bqf", 2), ("l1a_bqp", 2), ("l1a_bkf", 2),
          ("l1a_bkp", 2), ("l1a_b1", 4), ("l2x_bq", 1), ("l2x_bk", 1), ("l2a_bq", 1), ("l2a_bqr", 1), ("l2a_bk", 1),
          ("l2a_bkr", 1), ("l3x_bq", 1), ("l3x_bk", 1)]


def places(items):
    at, out = 0, {}
    for name, width in items:
        out[name] = (at, width)
        at += width
    return out, at


WEIGHT_AT, WEIGHT_COLUMNS = places([w for group in WEIGHTS for w in group])
ROW_AT, ROW_COLUMNS = places(ROWS)
BIAS_AT, BIAS_COLUMNS = places(BIASES)
L0F_SLOT = 512 + 512 + 4
L1F_SLOT = 512 + 512 + 512
L2F_SLOT = 128 + 128 + 128
L3F_SLOT = 128 + 128 + 256
L2F_EXPERTS = 32 + 4
L3F_PAIRS = 16 + 1


def perceiver(nc, xin, ctx_cols, ctx_rows, weights, rows, biases, l0f, l1f, l2f, l3f, cf, cb, ci, out):
    F_AT, F_COLUMNS = places([(k, v.shape[1]) for k, v in const_columns().items()])
    B_AT, B_COLUMNS = places([(k, v.shape[1]) for k, v in const_bf_columns().items()])
    with ExitStack() as ctx:
        def sb(name, shape, dt=F32):
            return ctx.enter_context(nc.sbuf_tensor(name, shape, dt))

        def sem(name):
            return ctx.enter_context(nc.semaphore(name))

        x = sb("x", [128, T, D])
        xn = sb("xn", [128, T, D])
        xi = sb("xi", [128, T, D])
        xnt = sb("xnt", [128, N])
        ctxc = sb("ctxc", [128, B * S])
        ctxr = sb("ctxr", [128, B, D])
        wsb = sb("wsb", [128, WEIGHT_COLUMNS])
        rsb = sb("rsb", [128, ROW_COLUMNS])
        bsb = sb("bsb", [128, BIAS_COLUMNS])
        cfs = sb("cfs", [128, F_COLUMNS])
        cbs = sb("cbs", [128, B_COLUMNS], BF16)
        cis = sb("cis", [128, len(SHIFTS)], I32)
        minus_half = sb("minus_half", [128, T])
        stats = sb("stats", [128, T, 6])
        moments = sb("moments", [128, T, 2])
        variance = sb("variance", [128, T])
        rstd = sb("rstd", [128, T])
        q = sb("q", [128, N])
        k = sb("k", [128, B * S])
        v = sb("v", [128, B, S])
        e = sb("e", [128, B * S])
        et = sb("et", [128, B * S])
        at = sb("at", [128, N])
        big = sb("big", [128, 4096])
        work = sb("work", [128, 4096])
        slots = sb("slots", [128, 4, L1F_SLOT])
        small = sb("small", [128, 32, 16])
        ps = ctx.enter_context(nc.psum_tensor("ps", [128, 8, 512], F32))

        def w(name, a=0, n=None):
            at0, width = WEIGHT_AT[name]
            return wsb[:, at0 + a:at0 + a + (width if n is None else n)]

        def row(name):
            at0, width = ROW_AT[name]
            return rsb[:, at0:at0 + width]

        def bias(name, i=0):
            return bsb[:, BIAS_AT[name][0] + i:BIAS_AT[name][0] + i + 1]

        def cst(name):
            at0, width = F_AT[name]
            return cfs[:, at0:at0 + width]

        def cstb(name):
            at0, width = B_AT[name]
            return cbs[:, at0:at0 + width]

        def rows_of(ap, n=T):
            return ap.unsqueeze(1).to_broadcast([128, n, ap.shape[1]])

        def bank(i):
            return ps[:, i, :]

        def banks(i, n, width):
            return ps[:, i:i + n, :].rearrange("p b (c w) -> p (b c) w", w=width)

        const_loaded = sem("const_loaded")
        x_loaded = sem("x_loaded")
        ctx_loaded = sem("ctx_loaded")
        w_loaded = [sem(f"w_loaded{i}") for i in range(STAGES)]
        half_set = sem("half_set")
        ones_set = sem("ones_set")
        x_done = sem("x_done")
        stats_ready = sem("stats_ready")
        rstd_ready = sem("rstd_ready")
        rows_ready = sem("rows_ready")
        turned = sem("turned")
        xnt_ready = sem("xnt_ready")


        def dve_norm(dve, n, src, dst, eps, gain=None, shift=None, publish=True):
            for t in range(T):
                dve.bn_stats(stats[:, t, :], src[:, t, :])
            dve.drain()
            for t in range(T):
                dve.bn_aggr(moments[:, t, :], stats[:, t, :])
            dve.drain()
            dve.tensor_scalar(variance[:, :], moments[:, :, 1], eps, None, ALU.add).then_inc(stats_ready, 1)
            dve.wait_ge(rstd_ready, n + 1)
            for t in range(T):
                last = dve.tensor_scalar(dst[:, t, :], src[:, t, :], moments[:, t, 0:1], rstd[:, t:t + 1],
                                         ALU.subtract, ALU.mult)
                if publish and gain is None:
                    last.then_inc(rows_ready, 1)
            if gain is not None:
                dve.drain()
                dve.tensor_tensor(dst[:, :, :], dst[:, :, :], rows_of(gain), ALU.mult)
                dve.drain()
                last = dve.tensor_tensor(dst[:, :, :], dst[:, :, :], rows_of(shift), ALU.add)
                if publish:
                    last.then_inc(rows_ready, T)

        def pool_rstd(pool, n):
            pool.wait_ge(stats_ready, n + 1)
            pool.tensor_tensor(rstd[:, :], variance[:, :], minus_half[:, :], ALU.pow).then_inc(rstd_ready, 1)

        def pe_turn(pe, m, src):
            for t in range(T):
                pe.wait_ge(rows_ready, T * m + t + 1)
                last = pe.transpose(bank(6 + t // 4)[:, t % 4 * 128:t % 4 * 128 + 128], src[:, t, :], cst("ident"))
                if t % 4 == 3:
                    last.then_inc(turned, 1)

        def act_turn(act, m):
            for h in range(2):
                act.wait_ge(turned, 2 * m + h + 1)
                act.copy(xnt[:, 512 * h:512 * h + 512], bank(6 + h)).then_inc(xnt_ready, 1)

        def mm(pe, o, lhs, rhs, start=True, stop=True):
            return pe.matmul(o, lhs, rhs, start=start, stop=stop)

        def peeled(eng, n, body):
            body(0)
            if n > 1:
                with eng.Fori(1, n) as i:
                    body(i)

        def wait(eng, s, value):
            if not isinstance(value, int) or value > 0:
                eng.wait_ge(s, value)

        def waitfrom(eng, s, base, more):
            if not isinstance(more, int) or more > 0:
                eng.wait_ge(s, base + more)

        kproj = sem("kproj")
        k_ready = sem("k_ready")
        vproj = sem("vproj")
        v_ready = sem("v_ready")
        qproj = sem("qproj")
        q_ready = sem("q_ready")
        VBANK = [4, 5, 0, 1]
        CROSS = [("l0x_w", "l0x_b", "l0x_w", "l0x_b", None, None)] + [
            (f"l{i}x_wq", f"l{i}x_bq", f"l{i}x_wk", f"l{i}x_bk", f"l{i}x_wv", f"l{i}x_bv") for i in (1, 2, 3)]

        def pe_project(pe, n, stage, m):
            wq, _, wk, _, wv, _ = CROSS[n]
            if stage:
                pe.wait_ge(x_done, stage)
            else:
                pe.wait_ge(ctx_loaded, 32)
                pe.wait_ge(const_loaded, 80)
            pe.wait_ge(w_loaded[stage], 16)
            for c in range(4):
                mm(pe, bank(c), w(wk), ctxc[:, 512 * c:512 * c + 512]).then_inc(kproj, 1)
            if n:
                for c in range(4):
                    if c >= 2:
                        pe.wait_ge(k_ready, 4 * n + c - 1)
                    for i in range(4):
                        b = 4 * c + i
                        last = mm(pe, bank(VBANK[c])[:, 128 * i:128 * i + 128], ctxc[:, 128 * b:128 * b + 128], w(wv))
                    last.then_inc(vproj, 1)
            pe_turn(pe, m, xn)
            pe.wait_ge(k_ready, 4 * n + 4)
            for h in range(2):
                pe.wait_ge(xnt_ready, 2 * m + h + 1)
                mm(pe, bank(2 + h), w(wq), xnt[:, 512 * h:512 * h + 512]).then_inc(qproj, 1)

        def act_project(act, n, m):
            _, bq, _, bk, _, _ = CROSS[n]
            for c in range(4):
                act.wait_ge(kproj, 4 * n + c + 1)
                act.activation(k[:, 512 * c:512 * c + 512], bank(c), ACT.Identity, bias=bias(bk)).then_inc(k_ready, 1)
            act_turn(act, m)
            for h in range(2):
                act.wait_ge(qproj, 2 * n + h + 1)
                act.activation(q[:, 512 * h:512 * h + 512], bank(2 + h), ACT.Identity, bias=bias(bq)).then_inc(q_ready, 1)

        def dve_values(dve, n):
            for c in range(4):
                dve.wait_ge(vproj, 4 * (n - 1) + c + 1)
                dve.tensor_tensor(v[:, 4 * c:4 * c + 4, :], banks(VBANK[c], 1, 128), rows_of(row(CROSS[n][5]), 4),
                                  ALU.add).then_inc(v_ready, 1)

        xs_score = sem("xs_score")
        xs_less = sem("xs_less")
        xs_exp = sem("xs_exp")
        xs_turn = sem("xs_turn")
        xs_et = sem("xs_et")
        xs_out = sem("xs_out")

        def pe_xs(pe, n, stage, m):
            c = 2 * n
            pe_project(pe, c, stage, m)
            if n:
                pe.wait_ge(v_ready, 4 * c)
            for h in range(2):
                pe.wait_ge(q_ready, 2 * c + h + 1)
                for i in range(8):
                    b = 8 * h + i
                    o = bank(h)[64 * (b % 2):64 * (b % 2) + 64, i // 2 * 128:i // 2 * 128 + 128]
                    last = mm(pe, o, q[:, L * b:L * b + L], k[:, S * b:S * b + S])
                last.then_inc(xs_score, 1)
            for h in range(2):
                pe.wait_ge(xs_exp, 2 * n + h + 1)
                for i in range(4):
                    t = 4 * h + i
                    last = pe.transpose(bank(2 + h)[:, 128 * i:128 * i + 128], e[:, 128 * t:128 * t + 128], cst("ident"))
                last.then_inc(xs_turn, 1)
            for h in range(2):
                pe.wait_ge(xs_et, 2 * n + h + 1)
                for i in range(8):
                    b = 8 * h + i
                    o = bank(4 + h)[64 * (b % 2):64 * (b % 2) + 64, i // 2 * 128:i // 2 * 128 + 128]
                    last = mm(pe, o, et[:, L * b:L * b + L], v[:, b, :] if n else ctxr[:, b, :])
                last.then_inc(xs_out, 1)

        def act_xs(act, n, m):
            act_project(act, 2 * n, m)
            for h in range(2):
                act.wait_ge(xs_less, 2 * n + h + 1)
                act.activation(e[:, 512 * h:512 * h + 512], big[:, 512 * h:512 * h + 512], ACT.Exp,
                               scale=float(D) ** -0.5 if n else 1.0).then_inc(xs_exp, 1)
            for h in range(2):
                act.wait_ge(xs_turn, 2 * n + h + 1)
                act.copy(et[:, 512 * h:512 * h + 512], bank(2 + h)).then_inc(xs_et, 1)

        def dve_xs(dve, n, norm):
            dve_norm(dve, norm, x, xn, 1e-5)
            if n:
                dve_values(dve, 2 * n)
            top, total, inverse = small[:, 0, 0:8], small[:, 1, 0:8], small[:, 2, 0:8]
            for h in range(2):
                dve.wait_ge(xs_score, 2 * n + h + 1)
                dve.tensor_reduce(top[:, 4 * h:4 * h + 4], banks(h, 1, 128), AX.X, ALU.max)
                dve.drain()
                dve.tensor_tensor(big[:, 512 * h:512 * h + 512].rearrange("p (t s) -> p t s", s=S), banks(h, 1, 128),
                                  top[:, 4 * h:4 * h + 4].unsqueeze(2).to_broadcast([128, 4, S]),
                                  ALU.subtract).then_inc(xs_less, 1)
            for h in range(2):
                dve.wait_ge(xs_exp, 2 * n + h + 1)
                dve.tensor_reduce(total[:, 4 * h:4 * h + 4], e[:, 512 * h:512 * h + 512].rearrange("p (t s) -> p t s", s=S),
                                  AX.X, ALU.add)
            dve.drain()
            dve.reciprocal(inverse, total)
            dve.drain()
            for h in range(2):
                dve.wait_ge(xs_out, 2 * n + h + 1)
                for i in range(4):
                    t = 4 * h + i
                    last = dve.scalar_tensor_tensor(x[:, t, :], bank(4 + h)[:, 128 * i:128 * i + 128],
                                                    inverse[:, t:t + 1], x[:, t, :], ALU.mult, ALU.add)
            last.then_inc(x_done, 1)
            dve.drain()

        la_q = sem("la_q")
        la_kv = sem("la_kv")
        la_neg = sem("la_neg")
        la_exp = sem("la_exp")
        la_feat = sem("la_feat")
        la_sum = sem("la_sum")
        la_kvm = sem("la_kvm")
        la_ctx = sem("la_ctx")
        la_div = sem("la_div")
        la_turn = sem("la_turn")
        la_cols = sem("la_cols")
        la_out = sem("la_out")
        KV = D + 1
        KVH = D + H
        vone = work[:, 0:T * KV].rearrange("p (t c) -> p t c", c=KV)
        kfeat = big[:, 0:N].rearrange("p (t c) -> p t c", c=D)
        kvm = slots[:, 0:2, :].rearrange("p a b -> p (a b)")[:, 0:B * KVH].rearrange("p (b c) -> p b c", c=KVH)

        def pe_la(pe, stage, m):
            pe_turn(pe, m, xn)
            pe.wait_ge(w_loaded[stage], 16)
            for h in range(2):
                pe.wait_ge(xnt_ready, 2 * m + h + 1)
                mm(pe, bank(4 + h), w("l0a_wq"), xnt[:, 512 * h:512 * h + 512]).then_inc(la_q, 1)
            for t in range(T):
                last = mm(pe, bank(t // 2)[:, 256 * (t % 2):256 * (t % 2) + 256], xnt[:, 128 * t:128 * t + 128],
                          w("l0a_wkv"))
                if t % 2:
                    last.then_inc(la_kv, 1)
            pe.wait_ge(la_feat, 3)
            for b in range(B):
                p = 64 * (b % 2)
                t = b // 2
                last = mm(pe, bank(3 * (b % 2) + t // 3)[:, KV * (t % 3):KV * (t % 3) + KV], kfeat[p:p + 64, t, :],
                          vone[p:p + 64, t, :])
            last.then_inc(la_sum, 1)
            pe.wait_ge(la_kvm, 1)
            for b in range(B):
                t, p = b // 2, 64 * (b % 2)
                last = mm(pe, bank(t // 3)[p:p + 64, KVH * (t % 3):KVH * (t % 3) + KVH], q[:, L * b:L * b + L],
                          kvm[:, T * (b % 2) + t, :])
            last.then_inc(la_ctx, 1)
            pe.wait_ge(la_div, 1)
            for t in range(T):
                last = pe.transpose(bank(6 + t // 4)[:, t % 4 * 128:t % 4 * 128 + 128], xi[:, t, :], cst("ident"))
                if t % 4 == 3:
                    last.then_inc(la_turn, 1)
            for t in range(T):
                pe.wait_ge(la_cols, t // 4 + 1)
                last = mm(pe, bank(3 + t // 4)[:, t % 4 * 128:t % 4 * 128 + 128], at[:, 128 * t:128 * t + 128],
                          w("l0a_wd"))
            last.then_inc(la_out, 1)

        def act_la(act, m):
            act_turn(act, m)
            act.wait_ge(la_neg, 1)
            act.activation(e[:, 0:N], e[:, 0:N], ACT.Exp).then_inc(la_exp, 1)
            act.wait_ge(la_neg, 2)
            act.activation(et[:, 0:N], et[:, 0:N], ACT.Exp).then_inc(la_exp, 1)
            for h in range(2):
                act.wait_ge(la_turn, h + 1)
                act.copy(at[:, 512 * h:512 * h + 512], bank(6 + h)).then_inc(la_cols, 1)

        def dve_la(dve, norm):
            dve_norm(dve, norm, x, xn, 1e-5)
            dve.wait_ge(la_q, 2)
            dve.tensor_scalar(e[:, 0:N], ps[:, 4:6, :].rearrange("p b c -> p (b c)"), bias("l0a_bq"), 0.0,
                              ALU.add, ALU.min).then_inc(la_neg, 1)
            dve.tensor_scalar(q[:, :], ps[:, 4:6, :].rearrange("p b c -> p (b c)"), bias("l0a_bq"), 0.0,
                              ALU.add, ALU.max)
            dve.wait_ge(la_kv, 4)
            kv = banks(0, 4, 256)
            krow = rows_of(row("l0a_bkv")[:, 0:128])
            vrow = rows_of(row("l0a_bkv")[:, 128:256])
            dve.tensor_tensor(kfeat, kv[:, :, 0:128], krow, ALU.add)
            dve.memset(vone[:, :, 128:129], 1.0)
            dve.tensor_tensor(vone[:, :, 0:128], kv[:, :, 128:256], vrow, ALU.add).then_inc(la_feat, 1)
            dve.drain()
            dve.tensor_scalar(et[:, 0:N], big[:, 0:N], 0.0, None, ALU.min).then_inc(la_neg, 1)
            dve.wait_ge(la_exp, 1)
            dve.tensor_tensor(q[:, :], q[:, :], e[:, 0:N], ALU.add).then_inc(la_feat, 1)
            dve.wait_ge(la_exp, 2)
            dve.scalar_tensor_tensor(big[:, 0:N], big[:, 0:N], 0.0, et[:, 0:N], ALU.max,
                                     ALU.add).then_inc(la_feat, 1)
            dve.wait_ge(la_sum, 1)
            for g in range(6):
                nb, a = min(3, T - 3 * (g % 3)), T * (g // 3) + 3 * (g % 3)
                src = bank(g)[:, 0:nb * KV].rearrange("p (b c) -> p b c", c=KV)
                dve.tensor_tensor(kvm[:, a:a + nb, 0:128], src[:, :, 0:128], rows_of(cst("same_head"), nb), ALU.mult)
                dve.tensor_tensor(kvm[:, a:a + nb, 128:KVH], rows_of(cst("head"), nb),
                                  src[:, :, 128:129].to_broadcast([128, nb, H]), ALU.mult)
            dve.drain()
            dve.tensor_tensor(kvm[:, :, 128:KVH], kvm[:, :, 128:KVH], rows_of(cst("head_eps"), B), ALU.add)\
               .then_inc(la_kvm, 1)
            dve.wait_ge(la_ctx, 1)
            z = small[:, 0:8, :]
            for g in range(3):
                nt = min(3, T - 3 * g)
                src = bank(g)[:, 0:nt * KVH].rearrange("p (t c) -> p t c", c=KVH)
                dve.reciprocal(z[:, 3 * g:3 * g + nt, :], src[:, :, 128:KVH])
            dve.drain()
            for t in range(T):
                src = bank(t // 3)[:, KVH * (t % 3):KVH * (t % 3) + 128].rearrange("p (h d) -> p h d", d=HD)
                last = dve.tensor_tensor(xi[:, t, :].rearrange("p (h d) -> p h d", d=HD), src,
                                         z[:, t, :].unsqueeze(2).to_broadcast([128, H, HD]), ALU.mult)
            last.then_inc(la_div, 1)
            dve.wait_ge(la_out, 1)
            dve.tensor_tensor(xi[:, :, :], banks(3, 2, 128), rows_of(row("l0a_bd")), ALU.add)
            dve.drain()
            dve.tensor_tensor(xi[:, :, :], xi[:, :, :], xn[:, :, :], ALU.add)
            dve.drain()
            dve_norm(dve, norm + 1, xi, xi, 1e-12, row("l0a_gamma"), row("l0a_beta"), publish=False)
            dve.drain()
            dve.tensor_tensor(x[:, :, :], x[:, :, :], xi[:, :, :], ALU.add).then_inc(x_done, 1)
            dve.drain()

        route_logit = sem("route_logit")
        route_less = sem("route_less")
        route_exp = sem("route_exp")
        choice = sem("choice")
        counted = sem("counted")
        NB = 36
        lg = sb("lg", [128, T, 32])
        probs = sb("probs", [128, T, 32])
        best = sb("best", [128, T, 8])
        best_at = sb("best_at", [128, T, 8], U32)
        best_atf = sb("best_atf", [128, T, 8])
        picks = sb("picks", [128, 4, T, 32])
        share = sb("share", [128, T, 8])
        tot = sb("tot", [128, T])
        gates = sb("gates", [128, T, NB])
        picksb = sb("picksb", [128, 2 * T, 8], BF16)
        tmp = sb("tmp", [128, T, 32])
        gcol = sb("gcol", [128, 4, 2 * T])

        def pe_route(pe, m, stage, wname, E):
            pe.wait_ge(w_loaded[stage], 16)
            for t in range(T):
                pe.wait_ge(xnt_ready, 2 * m + t // 4 + 1)
                last = mm(pe, bank(5)[:, E * t:E * t + E], xnt[:, 128 * t:128 * t + 128], w(wname))
            last.then_inc(route_logit, 1)

        def per_token(ap, E):
            return ap.unsqueeze(2).to_broadcast([128, T, E])

        def dve_probs(dve, n, E, brow=None):
            lgE, pr = lg[:, :, 0:E], probs[:, :, 0:E]
            dve.wait_ge(route_logit, n + 1)
            src = bank(5)[:, 0:T * E].rearrange("p (t e) -> p t e", e=E)
            if brow is None:
                dve.tensor_copy(lgE, src)
            else:
                dve.tensor_tensor(lgE, src, rows_of(row(brow)), ALU.add)
            dve.drain()
            dve.tensor_reduce(tot[:, :], lgE, AX.X, ALU.max)
            dve.drain()
            dve.tensor_tensor(lgE, lgE, per_token(tot[:, :], E), ALU.subtract).then_inc(route_less, 1)
            dve.wait_ge(route_exp, n + 1)
            dve.tensor_reduce(tot[:, :], pr, AX.X, ALU.add)
            dve.drain()
            dve.reciprocal(tot[:, :], tot[:, :])
            dve.drain()
            dve.tensor_tensor(pr, pr, per_token(tot[:, :], E), ALU.mult)
            dve.drain()

        def act_probs(act, n, E, scale=1.0):
            act.wait_ge(route_less, n + 1)
            act.activation(probs[:, :, 0:E], lg[:, :, 0:E], ACT.Exp, scale=scale).then_inc(route_exp, 1)

        def dve_best(dve, E, K, floor):
            for t in range(T):
                dve.max(best[:, t, :], probs[:, t, 0:E])
            dve.drain()
            for t in range(T):
                dve.max_index(best_at[:, t, :], best[:, t, :], probs[:, t, 0:E])
            dve.tensor_reduce(tot[:, :], best[:, :, 0:K], AX.X, ALU.add)
            dve.drain()
            dve.tensor_copy(best_atf[:, :, :], best_at[:, :, :])
            if floor:
                dve.tensor_scalar(tot[:, :], tot[:, :], floor, None, ALU.max)
            dve.drain()
            for j in range(K):
                dve.tensor_tensor(picks[:, j, :, 0:E], rows_of(cst("iota")[:, 0:E]),
                                  best_atf[:, :, j:j + 1].to_broadcast([128, T, E]), ALU.is_equal)
            dve.reciprocal(tot[:, :], tot[:, :])
            dve.drain()
            dve.tensor_tensor(share[:, :, 0:K], best[:, :, 0:K], per_token(tot[:, :], K), ALU.mult)
            dve.drain()

        def dve_gates(dve, E, K):
            dve.tensor_tensor(gates[:, :, 0:E], picks[:, 0, :, 0:E], share[:, :, 0:1].to_broadcast([128, T, E]), ALU.mult)
            for j in range(1, K):
                if j > 1:
                    dve.drain()
                dve.tensor_tensor(tmp[:, :, 0:E], picks[:, j, :, 0:E], share[:, :, j:j + 1].to_broadcast([128, T, E]),
                                  ALU.mult)
                dve.drain()
                dve.tensor_tensor(gates[:, :, 0:E], gates[:, :, 0:E], tmp[:, :, 0:E], ALU.add)
            dve.drain()

        def pe_prefix(pe, o, src, n):
            pe.matmul(o, cstb("earlier"), src, start=True, stop=False)
            for d in range(1, n):
                last = pe.matmul(o[:, 8 * d:8 * n], cstb("onesb"), src[:, 0:8 * (n - d)], start=False, stop=(d == n - 1))
            return last

        f0_up = sem("f0_up")
        f0_h = sem("f0_h")
        f0_y = sem("f0_y")
        f0_acc = sem("f0_acc")
        f0_b = sem("f0_b")
        f0_w = [sem(f"f0_w{i}") for i in range(2)]
        f0_gates = sem("f0_gates")
        L0_CAPACITY = 2 * N // 8

        def h_at(u, c):
            return big[:, 2048 * (u % 2) + 512 * c:2048 * (u % 2) + 512 * c + 512]

        def sp_experts(sp, src, width, n, per, sems, y_done, units_back):
            def body(i):
                for s in range(per):
                    wait(sp, y_done, 2 * (per * (i - 1) + s) + 2)
                    sp.dma_start(slots[:, s, 0:width], src[per * i + s]).then_inc(sems[s], 16)
            peeled(sp, n // per, body)
            for s in range(n % per):
                i = n // per
                wait(sp, y_done, 2 * (per * (i - 1) + s) + 2)
                sp.dma_start(slots[:, s, 0:width], src[per * i + s]).then_inc(sems[s], 16)

        def pe_f0(pe, stage, m):
            pe_turn(pe, m, xn)
            pe_route(pe, m, stage, "l0f_wg", 8)
            pe.wait_ge(choice, 1)
            pe_prefix(pe, bank(6)[:, 0:16 * 8], picksb[:, :, :].rearrange("p t e -> p (t e)"), 2 * T).then_inc(counted, 1)

            def y(u, s):
                pe.wait_ge(f0_h, 4 * u + 4)
                wait(pe, f0_acc, u - 1)
                for t in range(4):
                    for c in range(4):
                        last = mm(pe, bank(4 + s % 2)[:, 128 * t:128 * t + 128], h_at(s % 2, c)[:, 128 * t:128 * t + 128],
                                  slots[:, s // 2, 512 + 128 * c:640 + 128 * c], start=(c == 0), stop=(c == 3))
                last.then_inc(f0_y, 1)

            def body(i):
                for s in range(4):
                    u = 4 * i + s
                    if s % 2 == 0:
                        pe.wait_ge(f0_w[s // 2], 16 * (i + 1))
                    for c in range(4):
                        wait(pe, f0_h, 4 * u + c - 3)
                        mm(pe, bank(c), slots[:, s // 2, 128 * c:128 * c + 128],
                           xnt[:, 512 * (s % 2):512 * (s % 2) + 512]).then_inc(f0_up, 1)
                        if c == 1 and (s or not isinstance(i, int)):
                            y(u - 1, (s - 1) % 4)
            pe.wait_ge(f0_gates, 1)
            peeled(pe, 4, body)
            y(15, 3)
            pe.transpose(bank(7)[0:64, 0:128], xi[:, 0, 0:64], cst("ident")).then_inc(f0_b, 1)
            pe.wait_ge(f0_b, 2)
            pe.wait_ge(f0_acc, 16)
            for t in range(T):
                last = mm(pe, bank(t // 4)[:, t % 4 * 128:t % 4 * 128 + 128], et[0:64, 0:128],
                          w("l0f_b2", 128 * t, 128)[0:64, :])
            last.then_inc(f0_b, 1)

        def act_f0(act, m):
            act_turn(act, m)
            act_probs(act, 0, 8)

            def body(i):
                for s in range(4):
                    u = 4 * i + s
                    for c in range(4):
                        act.wait_ge(f0_up, 4 * u + c + 1)
                        if c == 0:
                            wait(act, f0_y, u - 1)
                        act.activation(h_at(s % 2, c), bank(c), ACT.Relu,
                                       bias=slots[:, s // 2, 1024 + c:1025 + c]).then_inc(f0_h, 1)
            peeled(act, 4, body)
            act.wait_ge(f0_b, 1)
            act.copy(et[0:64, 0:128], bank(7)[0:64, 0:128]).then_inc(f0_b, 1)

        def dve_add_gated(dve, t, src, gate):
            return dve.scalar_tensor_tensor(x[:, t, :], src, gate, x[:, t, :], ALU.mult, ALU.add)

        def dve_f0(dve, norm):
            dve_norm(dve, norm, x, xn, 1e-5)
            dve_probs(dve, 0, 8)
            dve_best(dve, 8, 2, None)
            for j in range(2):
                last = dve.tensor_copy(picksb[:, T * j:T * j + T, :], picks[:, j, :, 0:8])
            last.then_inc(choice, 1)
            dve.wait_ge(counted, 1)
            place = bank(6)[:, 0:128].rearrange("p (t e) -> p t e", e=8)
            for j in range(2):
                dve.scalar_tensor_tensor(picks[:, j, :, 0:8], place[:, T * j:T * j + T, :], float(L0_CAPACITY),
                                         picks[:, j, :, 0:8], ALU.is_lt, ALU.mult)
            dve.drain()
            dve_gates(dve, 8, 2)
            dve.tensor_copy(xi[:, 0, 0:64].rearrange("p (t e) -> p t e", e=8), gates[:, :, 0:8]).then_inc(f0_gates, 1)

            def body(i):
                for s in range(4):
                    u = 4 * i + s
                    if s % 2 == 0:
                        dve.tensor_copy(gcol[:, s // 2, 0:T], gates[:, :, bass.ds(2 * i + s // 2, 1)].rearrange("p t o -> p (t o)"))
                    dve.drain()
                    dve.wait_ge(f0_y, u + 1)
                    for t in range(4):
                        tt = 4 * (s % 2) + t
                        last = dve_add_gated(dve, tt, bank(4 + s % 2)[:, 128 * t:128 * t + 128], gcol[:, s // 2, tt:tt + 1])
                    last.then_inc(f0_acc, 1)
            peeled(dve, 4, body)
            dve.drain()
            dve.wait_ge(f0_b, 3)
            dve.tensor_tensor(x[:, :, :], x[:, :, :], banks(0, 2, 128), ALU.add).then_inc(x_done, 1)
            dve.drain()


        ha_in = sem("ha_in")
        ha_val = sem("ha_val")
        ha_score = sem("ha_score")
        ha_less = sem("ha_less")
        ha_exp = sem("ha_exp")
        ha_v = sem("ha_v")
        ha_turn = sem("ha_turn")
        ha_et = sem("ha_et")
        ha_av = sem("ha_av")
        ha_at = sem("ha_at")
        ha_out = sem("ha_out")
        USES = {3: "in score less exp v av at", 4: "in val score less av at", 7: "in val score less exp turn et av at",
                9: "in val score less exp turn et av at", 10: "in val score less exp turn et av at"}

        def base(name, stage, per=B):
            return per * sum(name in uses.split() for st, uses in USES.items() if st < stage)

        moving = big[:, 0:2048].rearrange("p (a c) -> p a c", a=2)
        exps = big[:, 2048:4096].rearrange("p (a c) -> p a c", a=2)
        still = work[:, 0:512].rearrange("p (a c) -> p a c", a=2)
        values = work[:, 512:1024].rearrange("p (a c) -> p a c", a=2)
        scratch = work[:, 1024:2048].rearrange("p (a c) -> p a c", a=2)
        exps_t = et[:, :].rearrange("p (a c) -> p a c", a=2)
        SCALE = float(HD) ** -0.5

        def rounds(eng, step, lags):
            def body(i):
                for s in range(2):
                    step(2 * i + s, s)
            peeled(eng, B // 2, body)
            for b in range(B, B + lags):
                step(b, b % 2)

        def has(b, lag):
            return not isinstance(b, int) or 0 <= b - lag < B

        def seq(ap, b, n):
            return ap[:, bass.ds(b * n, n)] if not isinstance(b, int) else ap[:, b * n:b * n + n]

        def pe_out_heads(pe, stage, wname, wo_banks):
            pe.wait_ge(ha_at, base("at", stage) + B)
            for t in range(T):
                last = mm(pe, bank(wo_banks + t // 4)[:, t % 4 * 128:t % 4 * 128 + 128], at[:, 128 * t:128 * t + 128],
                          w(wname))
            last.then_inc(ha_out, 1)

        def dve_out_heads(dve, stage, brow):
            dve.wait_ge(ha_out, base("at", stage, 1) + 1)
            dve.tensor_tensor(x[:, :, :], x[:, :, :], banks(0, 2, 128), ALU.add)
            dve.drain()
            if brow:
                dve.tensor_tensor(x[:, :, :], x[:, :, :], rows_of(row(brow)), ALU.add)
                dve.drain()
            dve.nop().then_inc(x_done, 1)

        def dve_pick_heads(dve, src, dst, parts):
            for n in range(parts):
                dve.tensor_tensor(scratch[:, 0, 256 * n:256 * n + 256].rearrange("p (j l) -> p j l", l=L),
                                  src[:, 256 * n:256 * n + 256].rearrange("p (j l) -> p j l", l=L),
                                  cst("head_of_four").unsqueeze(2).to_broadcast([128, 4, L]), ALU.mult)
            dve.drain()
            for n in range(parts):
                last = dve.tensor_reduce(dst[n], scratch[:, 0, 256 * n:256 * n + 256].rearrange("p (j l) -> p l j", l=L),
                                         AX.X, ALU.add)
            return last


        def pool_l1x(pool):
            st = 3
            pool.wait_ge(q_ready, 2 * 1 + 2)
            pool.wait_ge(k_ready, 4 * 1 + 4)

            def step(b, s):
                waitfrom(pool, ha_score, base("score", st), b - 1)
                pool.tensor_tensor(moving[:, s, :].rearrange("p (h l) -> p h l", l=L),
                                   seq(q, b, L).unsqueeze(1).to_broadcast([128, H, L]),
                                   cst("head").unsqueeze(2).to_broadcast([128, H, L]), ALU.mult)
                pool.tensor_copy(still[:, s, 0:128], seq(k, b, S)).then_inc(ha_in, 1)
            rounds(pool, step, 0)

        def pe_l1x(pe, stage, m):
            st = 3
            pe_project(pe, 1, stage, m)
            pe.wait_ge(v_ready, 4)
            pe.wait_ge(q_ready, 4)

            def step(b, s):
                if has(b, 0):
                    pe.wait_ge(ha_in, base("in", st) + b + 1)
                    waitfrom(pe, ha_less, base("less", st), b - 1)
                    for h in range(2):
                        last = mm(pe, bank(2 * s + h), still[:, s, 0:128], moving[:, s, 512 * h:512 * h + 512])
                    last.then_inc(ha_score, 1)
                if has(b, 1):
                    z = 1 - s
                    pe.wait_ge(ha_v, base("v", st) + b)
                    waitfrom(pe, ha_at, base("at", st), b - 2)
                    for g in range(4):
                        last = mm(pe, bank(4 + z)[32 * g:32 * g + 32, 0:256], values[:, z, 32 * g:32 * g + 32],
                                  exps[:, z, 256 * g:256 * g + 256])
                    last.then_inc(ha_av, 1)
            rounds(pe, step, 1)
            pe_out_heads(pe, stage, "l1x_wo", 0)

        def act_l1x(act, m):
            st = 3
            act_project(act, 1, m)

            def step(b, s):
                act.wait_ge(ha_less, base("less", st) + b + 1)
                act.activation(exps[:, s, :], exps[:, s, :], ACT.Exp, scale=SCALE).then_inc(ha_exp, 1)
            rounds(act, step, 0)

        def dve_l1x(dve, norm):
            st = 3
            dve_norm(dve, norm, x, xn, 1e-5)
            dve_values(dve, 1)

            def step(b, s):
                top, total, z = small[:, s, :], small[:, 2 + s, :], 1 - s
                if has(b, 0):
                    dve.wait_ge(ha_score, base("score", st) + b + 1)
                    sc = banks(2 * s, 2, L)
                    dve.tensor_reduce(top, sc, AX.X, ALU.max)
                    dve.drain()
                    waitfrom(dve, ha_av, base("av", st), b - 1)
                    dve.tensor_tensor(exps[:, s, :].rearrange("p (h l) -> p h l", l=L), sc,
                                      top.unsqueeze(2).to_broadcast([128, H, L]), ALU.subtract).then_inc(ha_less, 1)
                if has(b, 1):
                    total = small[:, 2 + z, :]
                    dve.wait_ge(ha_exp, base("exp", st) + b)
                    dve.tensor_reduce(total, exps[:, z, :].rearrange("p (h l) -> p h l", l=L), AX.X, ALU.add)
                    dve.drain()
                    dve.reciprocal(total, total)
                    dve.drain()
                    vb = seq(v[:, :, :].rearrange("p b c -> p (b c)"), b - 1, D)
                    dve.tensor_tensor(values[:, z, 0:128].rearrange("p (h d) -> p h d", d=HD),
                                      vb.rearrange("p (h d) -> p h d", d=HD),
                                      total.unsqueeze(2).to_broadcast([128, H, HD]), ALU.mult).then_inc(ha_v, 1)
                if has(b, 2):
                    dve.drain()
                    dve.wait_ge(ha_av, base("av", st) + b - 1)
                    dve_pick_heads(dve, bank(4 + s), [seq(at, b - 2, L)], 1).then_inc(ha_at, 1)
            rounds(dve, step, 2)
            dve_out_heads(dve, 3, "l1x_bo")


        def pool_l3x(pool):
            st = 9
            pool.wait_ge(q_ready, 2 * 3 + 2)
            pool.wait_ge(k_ready, 4 * 3 + 4)
            pool.wait_ge(v_ready, 12)

            def step(b, s):
                waitfrom(pool, ha_score, base("score", st), b - 1)
                pool.tensor_tensor(moving[:, s, :].rearrange("p (i c) -> p i c", c=S),
                                   seq(k, b, S).unsqueeze(1).to_broadcast([128, 8, S]),
                                   cst("head_pair").unsqueeze(2).to_broadcast([128, 8, S]), ALU.mult)
                pool.tensor_tensor(still[:, s, 0:128].rearrange("p (j l) -> p j l", l=L),
                                   seq(q, b, L).unsqueeze(1).to_broadcast([128, 2, L]),
                                   cst("head_parity").unsqueeze(2).to_broadcast([128, 2, L]), ALU.mult).then_inc(ha_in, 1)
                waitfrom(pool, ha_av, base("av", st), b - 1)
                pool.tensor_copy(values[:, s, 0:128], seq(v[:, :, :].rearrange("p b c -> p (b c)"), b, D)).then_inc(ha_val, 1)
            rounds(pool, step, 0)

        def pe_l3x(pe, stage, m):
            st = 9
            pe_project(pe, 3, stage, m)
            pe.wait_ge(v_ready, 12)
            pe.wait_ge(q_ready, 8)

            def step(b, s):
                z = 1 - s
                if has(b, 0):
                    pe.wait_ge(ha_in, base("in", st) + b + 1)
                    waitfrom(pe, ha_less, base("less", st), b - 1)
                    for h in range(2):
                        last = mm(pe, bank(2 * s + h), still[:, s, 0:128], moving[:, s, 512 * h:512 * h + 512])
                    last.then_inc(ha_score, 1)
                if has(b, 1):
                    pe.wait_ge(ha_exp, base("exp", st) + b)
                    waitfrom(pe, ha_et, base("et", st), b - 1)
                    for i in range(8):
                        last = pe.transpose(bank(4 + i // 4)[:, i % 4 * 128:i % 4 * 128 + 128],
                                            exps[:, z, 128 * i:128 * i + 128], cst("ident"))
                    last.then_inc(ha_turn, 1)
                if has(b, 2):
                    pe.wait_ge(ha_et, base("et", st) + b - 1)
                    pe.wait_ge(ha_val, base("val", st) + b - 1)
                    waitfrom(pe, ha_at, base("at", st), b - 3)
                    for g in range(4):
                        o = bank(6 + s)[32 * g:32 * g + 32, :]
                        mm(pe, o[:, 0:256], values[:, s, 32 * g:32 * g + 32], exps_t[:, s, 256 * g:256 * g + 256])
                        last = mm(pe, o[:, 256:512], cst("ones")[:, 0:32], exps_t[:, s, 256 * g:256 * g + 256])
                    last.then_inc(ha_av, 1)
            rounds(pe, step, 2)
            pe_out_heads(pe, stage, "l3x_wo", 0)

        def act_l3x(act, m):
            st = 9
            act_project(act, 3, m)

            def step(b, s):
                z = 1 - s
                if has(b, 0):
                    act.wait_ge(ha_less, base("less", st) + b + 1)
                    act.activation(exps[:, s, :], exps[:, s, :], ACT.Exp, scale=SCALE).then_inc(ha_exp, 1)
                if has(b, 1):
                    act.wait_ge(ha_turn, base("turn", st) + b)
                    waitfrom(act, ha_av, base("av", st), b - 2)
                    act.copy(exps_t[:, z, :], ps[:, 4:6, :].rearrange("p b c -> p (b c)")).then_inc(ha_et, 1)
            rounds(act, step, 1)

        def dve_l3x(dve, norm):
            st = 9
            dve_norm(dve, norm, x, xn, 1e-5)
            dve_values(dve, 3)

            def step(b, s):
                top = small[:, s, 0:8]
                if has(b, 0):
                    dve.wait_ge(ha_score, base("score", st) + b + 1)
                    sc = banks(2 * s, 2, S)
                    dve.tensor_reduce(top, sc, AX.X, ALU.max)
                    dve.drain()
                    waitfrom(dve, ha_turn, base("turn", st), b - 1)
                    dve.tensor_tensor(exps[:, s, :].rearrange("p (i c) -> p i c", c=S), sc,
                                      top.unsqueeze(2).to_broadcast([128, 8, S]), ALU.subtract).then_inc(ha_less, 1)
                if has(b, 2):
                    dve.drain()
                    dve.wait_ge(ha_av, base("av", st) + b - 1)
                    dve_pick_heads(dve, bank(6 + s), [scratch[:, 1, 0:64], scratch[:, 1, 64:128]], 2)
                    dve.drain()
                    dve.reciprocal(scratch[:, 1, 128:192], scratch[:, 1, 64:128])
                    dve.drain()
                    dve.tensor_tensor(seq(at, b - 2, L), scratch[:, 1, 0:64], scratch[:, 1, 128:192],
                                      ALU.mult).then_inc(ha_at, 1)
            rounds(dve, step, 2)
            dve_out_heads(dve, 9, "l3x_bo")

        sa_dup = sem("sa_dup")
        sa_v = sem("sa_v")
        sa_vb = sem("sa_vb")
        sa_proj = sem("sa_proj")
        sa_rot = sem("sa_rot")
        SELF = {7: ("l2a", "rope2", True), 10: ("l3a", "rope3", False)}

        def act_duplicate(act, m, dst):
            for h in range(2):
                act.wait_ge(turned, 2 * m + h + 1)
                act.copy(xnt[:, 512 * h:512 * h + 512], bank(6 + h)).then_inc(xnt_ready, 1)
                act.activation(dst[:, 1024 * h:1024 * h + 1024].rearrange("p (b r l) -> p b r l", r=2, l=L),
                               bank(6 + h).rearrange("p (b l) -> p b l", l=L).unsqueeze(2).to_broadcast([128, 8, 2, L]),
                               ACT.Copy).then_inc(sa_dup, 1)

        def pe_self_values(pe, n, src, wname):
            for b in range(B):
                if b % 8 == 0:
                    pe.wait_ge(sa_dup, 2 * n + b // 8 + 1)
                last = mm(pe, bank(b // 4)[:, b % 4 * 128:b % 4 * 128 + 128], src[:, 128 * b:128 * b + 128], w(wname))
            last.then_inc(sa_v, 1)

        def pool_values(pool, b, s, mask):
            pool.tensor_tensor(values[:, s, :].rearrange("p (c g d) -> p c g d", c=2, g=4),
                               seq(v[:, :, :].rearrange("p b c -> p (b c)"), b, D)
                               .rearrange("p (g d) -> p g d", g=4).unsqueeze(1).to_broadcast([128, 2, 4, 32]),
                               cst(mask).rearrange("p (c d) -> p c d", c=2).unsqueeze(2).to_broadcast([128, 2, 4, 32]),
                               ALU.mult).then_inc(ha_val, 1)

        def pool_self(pool, st):
            n = {7: 1, 10: 2}[st]
            pool.wait_ge(sa_rot, 4 * n)
            pool.wait_ge(sa_vb, n + 1)

            def step(b, s):
                waitfrom(pool, ha_score, base("score", st), b - 1)
                pool.tensor_tensor(moving[:, s, 0:512].rearrange("p (i c) -> p i c", c=L),
                                   seq(k, b, L).unsqueeze(1).to_broadcast([128, 8, L]),
                                   cst("head_pair").unsqueeze(2).to_broadcast([128, 8, L]), ALU.mult)
                pool.tensor_tensor(still[:, s, 0:128].rearrange("p (j l) -> p j l", l=L),
                                   seq(q, b, L).unsqueeze(1).to_broadcast([128, 2, L]),
                                   cst("head_parity").unsqueeze(2).to_broadcast([128, 2, L]), ALU.mult).then_inc(ha_in, 1)
                waitfrom(pool, ha_av, base("av", st), b - 1)
                pool_values(pool, b, s, "value_soft")
            rounds(pool, step, 0)

        def pe_self(pe, st, m):
            name, _, _ = SELF[st]
            n = {7: 1, 10: 2}[st]
            pe_turn(pe, m, xn)
            pe.wait_ge(w_loaded[st], 16)
            pe_self_values(pe, n, e, name + "_wv")
            pe.wait_ge(sa_vb, n + 1)
            for h in range(2):
                pe.wait_ge(xnt_ready, 2 * m + h + 1)
                for j, part in enumerate(("_wq", "_wqr", "_wk", "_wkr")):
                    last = mm(pe, bank(4 * h + j), w(name + part), xnt[:, 512 * h:512 * h + 512])
                last.then_inc(sa_proj, 1)
            pe.wait_ge(sa_rot, 4 * n)

            def step(b, s):
                z = 1 - s
                if has(b, 0):
                    pe.wait_ge(ha_in, base("in", st) + b + 1)
                    waitfrom(pe, ha_less, base("less", st), b - 1)
                    mm(pe, bank(s), still[:, s, 0:128], moving[:, s, 0:512], start=True, stop=False)
                    mm(pe, bank(s), cstb("identb"), cstb("causal"), start=False, stop=True).then_inc(ha_score, 1)
                if has(b, 1):
                    pe.wait_ge(ha_exp, base("exp", st) + b)
                    waitfrom(pe, ha_et, base("et", st), b - 2)
                    for g in range(4):
                        last = pe.transpose(bank(2 + z)[:, 128 * g:128 * g + 128], exps[:, z, 128 * g:128 * g + 128],
                                            cst("ident"))
                    last.then_inc(ha_turn, 1)
                if has(b, 2):
                    pe.wait_ge(ha_et, base("et", st) + b - 1)
                    pe.wait_ge(ha_val, base("val", st) + b - 1)
                    waitfrom(pe, ha_at, base("at", st), b - 3)
                    for g in range(4):
                        for j in range(2):
                            mm(pe, bank(4 + s)[32 * g:32 * g + 32, 0:64], values[:, s, 128 * j + 32 * g:128 * j + 32 * g + 32],
                               exps_t[:, s, 128 * g + 64 * j:128 * g + 64 * j + 64], start=(j == 0), stop=(j == 1))
                        for j in range(2):
                            last = mm(pe, bank(4 + s)[32 * g:32 * g + 32, 64:128], cst("value_soft")[:, 32 * j:32 * j + 32],
                                      exps_t[:, s, 128 * g + 64 * j:128 * g + 64 * j + 64], start=(j == 0), stop=(j == 1))
                    last.then_inc(ha_av, 1)
            rounds(pe, step, 2)
            pe_out_heads(pe, st, name + "_wo", 0)

        def act_self(act, st, m):
            act_duplicate(act, m, e)

            def step(b, s):
                z = 1 - s
                if has(b, 0):
                    act.wait_ge(ha_less, base("less", st) + b + 1)
                    act.activation(exps[:, s, 0:512], exps[:, s, 0:512], ACT.Exp, scale=SCALE).then_inc(ha_exp, 1)
                if has(b, 1):
                    act.wait_ge(ha_turn, base("turn", st) + b)
                    waitfrom(act, ha_av, base("av", st), b - 2)
                    act.copy(exps_t[:, z, 0:512], bank(2 + z)).then_inc(ha_et, 1)
            rounds(act, step, 1)

        def dve_self(dve, st, norm):
            name, rope, biased = SELF[st]
            n = {7: 1, 10: 2}[st]
            dve_norm(dve, norm, x, xn, 1e-5)
            dve.wait_ge(sa_v, n + 1)
            if biased:
                dve.tensor_tensor(v[:, :, :], banks(0, 4, 128), rows_of(row(name + "_bv"), B), ALU.add).then_inc(sa_vb, 1)
            else:
                dve.tensor_copy(v[:, :, :], banks(0, 4, 128)).then_inc(sa_vb, 1)
            for h in range(2):
                dve.wait_ge(sa_proj, 2 * (n - 1) + h + 1)
                for j, (dst, bq) in enumerate(((q, "_bq"), (k, "_bk"))):
                    turn = scratch[:, j, :].rearrange("p (b l) -> p b l", l=L)
                    out = dst[:, 512 * h:512 * h + 512].rearrange("p (b l) -> p b l", l=L)
                    for o, bk, tab, sfx in ((out, 4 * h + 2 * j, "_cos", ""), (turn, 4 * h + 2 * j + 1, "_sin", "r")):
                        table = cst(rope + tab).unsqueeze(1).to_broadcast([128, 8, L])
                        src = bank(bk).rearrange("p (b l) -> p b l", l=L)
                        if biased:
                            dve.scalar_tensor_tensor(o, src, bias(name + bq + sfx), table, ALU.add, ALU.mult)
                        else:
                            dve.tensor_tensor(o, src, table, ALU.mult)
                dve.drain()
                for j, dst in enumerate((q, k)):
                    dve.tensor_tensor(dst[:, 512 * h:512 * h + 512], dst[:, 512 * h:512 * h + 512], scratch[:, j, :],
                                      ALU.add).then_inc(sa_rot, 1)
                dve.drain()

            def step(b, s):
                top = small[:, s, 0:8]
                if has(b, 0):
                    dve.wait_ge(ha_score, base("score", st) + b + 1)
                    sc = banks(s, 1, L)
                    dve.tensor_reduce(top, sc, AX.X, ALU.max)
                    dve.drain()
                    waitfrom(dve, ha_turn, base("turn", st), b - 1)
                    dve.tensor_tensor(exps[:, s, 0:512].rearrange("p (i c) -> p i c", c=L), sc,
                                      top.unsqueeze(2).to_broadcast([128, 8, L]), ALU.subtract).then_inc(ha_less, 1)
                if has(b, 2):
                    dve.wait_ge(ha_av, base("av", st) + b - 1)
                    dve.reciprocal(scratch[:, s, 0:64], bank(4 + s)[:, 64:128])
                    dve.drain()
                    dve.tensor_tensor(seq(at, b - 2, L), bank(4 + s)[:, 0:64], scratch[:, s, 0:64],
                                      ALU.mult).then_inc(ha_at, 1)
            rounds(dve, step, 2)
            dve_out_heads(dve, st, name + "_bo" if biased else None)

        wv_proj = sem("wv_proj")
        wv_arg = sem("wv_arg")
        wv_near = sem("wv_near")
        wv_frac = sem("wv_frac")
        wv_sin = sem("wv_sin")
        wv_sum = sem("wv_sum")
        wv_norm = sem("wv_norm")
        wv_unit = sem("wv_unit")
        wf_up = sem("wf_up")
        wf_arg = sem("wf_arg")
        wf_near = sem("wf_near")
        wf_frac = sem("wf_frac")
        wf_sin = sem("wf_sin")
        wf_h = sem("wf_h")
        wf_gelu = sem("wf_gelu")
        wf_out = sem("wf_out")
        MAGIC = 1.5 * 2.0 ** 23
        TURNS = float(np.float32(1.0 / (2.0 * np.pi)))
        ANGLE = float(np.float32(6.283185))
        waves = slots[:, :, :].rearrange("p a b -> p (a b)")[:, 0:4096].rearrange("p (c n) -> p c n", c=4)
        bigc = big[:, :].rearrange("p (c n) -> p c n", c=4)
        workc = work[:, :].rearrange("p (c n) -> p c n", c=4)

        def wholes(c):
            return (e if c < 2 else et)[:, 1024 * (c % 2):1024 * (c % 2) + 1024]

        def two(i):
            return ps[:, i:i + 2, :].rearrange("p b c -> p (b c)")

        def pool_wave(pool):
            st = 4
            pool.wait_ge(wv_unit, 4)
            pool.wait_ge(sa_vb, 1)

            def step(b, s):
                waitfrom(pool, ha_score, base("score", st), b - 1)
                for hf in range(2):
                    pool.tensor_tensor(moving[:, s, 256 * hf:256 * hf + 256].rearrange("p (i t) -> p i t", t=L),
                                       seq(waves[:, hf, :], b, L).unsqueeze(1).to_broadcast([128, 4, L]),
                                       cst("wave_pair").unsqueeze(2).to_broadcast([128, 4, L]), ALU.mult)
                    last = pool.tensor_tensor(still[:, s, 128 * hf:128 * hf + 128].rearrange("p (j t) -> p j t", t=L),
                                       seq(waves[:, 2 + hf, :], b, L).unsqueeze(1).to_broadcast([128, 2, L]),
                                       cst("wave_parity").unsqueeze(2).to_broadcast([128, 2, L]),
                                       ALU.mult)
                last.then_inc(ha_in, 1)
                waitfrom(pool, ha_av, base("av", st), b - 1)
                pool_values(pool, b, s, "value_wave")
            rounds(pool, step, 0)

        def pe_wave(pe, stage, m):
            st = 4
            pe_turn(pe, m, xn)
            pe.wait_ge(w_loaded[stage], 16)
            pe_self_values(pe, 0, k, "l1a_wv")
            for c in range(4):
                a = 0 if c % 2 else 4
                if c == 0:
                    pe.wait_ge(xnt_ready, 2 * m + 2)
                    pe.wait_ge(sa_dup, 2)
                if c == 1:
                    pe.wait_ge(sa_vb, 1)
                if c >= 2:
                    pe.wait_ge(wv_arg, c - 1)
                for j, part in enumerate(("f", "p")):
                    name = "l1a_w" + "qk"[c // 2] + part
                    for h in range(2):
                        last = mm(pe, bank(a + 2 * j + h), w(name, 128 * (c % 2), 128), xnt[:, 512 * h:512 * h + 512])
                last.then_inc(wv_proj, 1)
            for c in range(4):
                pe.wait_ge(wv_sin, c + 1)
                if c == 0:
                    pe.wait_ge(wv_arg, 4)
                for h in range(2):
                    last = mm(pe, bank(2 * c + h), cst("same_wave_head"), bigc[:, c, 512 * h:512 * h + 512])
                last.then_inc(wv_sum, 1)
            pe.wait_ge(wv_norm, 4)

            def step(b, s):
                z = 1 - s
                if has(b, 0):
                    pe.wait_ge(ha_in, base("in", st) + b + 1)
                    waitfrom(pe, ha_less, base("less", st), b - 1)
                    for hf in range(2):
                        last = mm(pe, bank(s)[:, 256 * hf:256 * hf + 256], still[:, s, 128 * hf:128 * hf + 128],
                                  moving[:, s, 256 * hf:256 * hf + 256])
                    last.then_inc(ha_score, 1)
                if has(b, 1):
                    pe.wait_ge(ha_less, base("less", st) + b)
                    pe.wait_ge(ha_val, base("val", st) + b)
                    waitfrom(pe, ha_at, base("at", st), b - 2)
                    for g in range(4):
                        for c in range(2):
                            i = 2 * g + c
                            last = mm(pe, bank(4 + z)[32 * g:32 * g + 32, 0:64],
                                      values[:, z, 128 * c + 32 * g:128 * c + 32 * g + 32],
                                      exps_t[:, z, 64 * i:64 * i + 64], start=(c == 0), stop=(c == 1))
                    last.then_inc(ha_av, 1)
            rounds(pe, step, 1)
            pe_out_heads(pe, st, "l1a_wo", 2)
            pe_turn(pe, m + 1, xn)
            for c in range(4):
                for h in range(2):
                    if c == 0:
                        pe.wait_ge(xnt_ready, 2 * m + 2 + h + 1)
                    last = mm(pe, bank(2 * c + h), w("l1a_w1", 128 * c, 128), xnt[:, 512 * h:512 * h + 512])
                last.then_inc(wf_up, 1)
            pe.wait_ge(wf_h, 4)
            for t in range(T):
                for c in range(4):
                    last = mm(pe, bank(t // 4)[:, t % 4 * 128:t % 4 * 128 + 128], bigc[:, c, 128 * t:128 * t + 128],
                              w("l1a_w2", 128 * c, 128), start=(c == 0), stop=(c == 3))
            last.then_inc(wf_out, 1)

        def act_wave(act, m):
            st = 4
            act_duplicate(act, m, k)
            for c in range(4):
                act.wait_ge(wv_arg, c + 1)
                act.activation(workc[:, c, :], bigc[:, c, :], ACT.Identity, scale=TURNS)
                act.activation(wholes(c), bigc[:, c, :], ACT.Copy, scale=TURNS, bias=MAGIC).then_inc(wv_near, 1)
            for c in range(4):
                act.wait_ge(wv_frac, c + 1)
                act.activation(waves[:, c, :], waves[:, c, :], ACT.Sin, scale=-ANGLE)
                act.drain()
                act.square(bigc[:, c, :], waves[:, c, :]).then_inc(wv_sin, 1)
            for c in range(4):
                act.wait_ge(wv_sum, c + 1)
                act.sqrt(workc[:, c, :], two(2 * c)).then_inc(wv_norm, 1)

            def step(b, s):
                act.wait_ge(ha_av, base("av", st) + b + 1)
                act.copy(seq(at, b, L), bank(4 + s)[:, 0:64]).then_inc(ha_at, 1)
            rounds(act, step, 0)
            act_turn(act, m + 1)
            for c in range(4):
                act.wait_ge(wf_up, c + 1)
                act.activation(bigc[:, c, :], two(2 * c), ACT.Gelu, bias=bias("l1a_b1", c)).then_inc(wf_gelu, 1)
            for c in range(4):
                act.wait_ge(wf_arg, c + 1)
                act.activation(waves[:, c, :], workc[:, c, :], ACT.Identity, scale=TURNS)
                act.activation(wholes(c), workc[:, c, :], ACT.Copy, scale=TURNS, bias=MAGIC).then_inc(wf_near, 1)
            for c in range(4):
                act.wait_ge(wf_frac, c + 1)
                act.activation(waves[:, c, :], waves[:, c, :], ACT.Sin, scale=-ANGLE).then_inc(wf_sin, 1)

        def dve_fraction(dve, near, turns, c, out_sem):
            dve.scalar_tensor_tensor(waves[:, c, :], near, MAGIC, turns, ALU.subtract, ALU.subtract)
            dve.drain()
            dve.tensor_scalar(waves[:, c, :], waves[:, c, :], -0.5, 0.5, ALU.max, ALU.min).then_inc(out_sem, 1)

        def dve_wave(dve, norm):
            st = 4
            dve_norm(dve, norm, x, xi, 1e-5, publish=False)
            dve.drain()
            dve_norm(dve, norm + 1, xi, xn, 1e-5, row("l1a_g1"), row("l1a_be1"))
            dve.wait_ge(sa_v, 1)
            dve.tensor_tensor(v[:, :, :], banks(0, 4, 128), rows_of(row("l1a_bv"), B), ALU.add).then_inc(sa_vb, 0 + 1)
            dve.drain()
            dve.tensor_tensor(v[:, :, :].rearrange("p b (h d) -> p b h d", d=HD),
                              v[:, :, :].rearrange("p b (h d) -> p b h d", d=HD),
                              row("l1a_iscale").unsqueeze(2).unsqueeze(1).to_broadcast([128, B, H, HD]), ALU.mult)
            for c in range(4):
                a = 0 if c % 2 else 4
                dve.wait_ge(wv_proj, c + 1)
                name = "l1a_b" + "qk"[c // 2]
                dve.scalar_tensor_tensor(bigc[:, c, :].rearrange("p (b l) -> p b l", l=L),
                                         two(a).rearrange("p (b l) -> p b l", l=L), bias(name + "f", c % 2),
                                         cst("position").unsqueeze(1).to_broadcast([128, B, L]), ALU.add, ALU.mult)
                dve.drain()
                dve.scalar_tensor_tensor(bigc[:, c, :], two(a + 2), bias(name + "p", c % 2), bigc[:, c, :],
                                         ALU.add, ALU.add).then_inc(wv_arg, 1)
            for c in range(4):
                dve.wait_ge(wv_near, c + 1)
                dve_fraction(dve, wholes(c), workc[:, c, :], c, wv_frac)
            for c in range(4):
                dve.wait_ge(wv_norm, c + 1)
                dve.tensor_scalar(workc[:, c, :], workc[:, c, :], 1e-12, None, ALU.max)
                dve.drain()
                dve.reciprocal(workc[:, c, :], workc[:, c, :])
                dve.drain()
                dve.tensor_tensor(waves[:, c, :], waves[:, c, :], workc[:, c, :], ALU.mult).then_inc(wv_unit, 1)

            def step(b, s):
                dve.wait_ge(ha_score, base("score", st) + b + 1)
                waitfrom(dve, ha_av, base("av", st), b - 1)
                dve.tensor_tensor(exps_t[:, s, 0:512].rearrange("p (i t) -> p i t", t=L), banks(s, 1, L),
                                  cst("wave_causal").unsqueeze(1).to_broadcast([128, 8, L]), ALU.mult).then_inc(ha_less, 1)
            rounds(dve, step, 0)
            dve.wait_ge(ha_out, base("at", st, 1) + 1)
            dve.tensor_tensor(xi[:, :, :], xi[:, :, :], banks(2, 2, 128), ALU.add)
            dve.drain()
            dve.tensor_tensor(xi[:, :, :], xi[:, :, :], rows_of(row("l1a_bo")), ALU.add)
            dve.drain()
            dve_norm(dve, norm + 2, xi, xn, 1e-5, row("l1a_g2"), row("l1a_be2"))
            for c in range(4):
                dve.wait_ge(wf_up, c + 1)
                dve.wait_ge(wf_gelu, c + 1)
                dve.tensor_scalar(workc[:, c, :], two(2 * c), bias("l1a_b1", c), None, ALU.add).then_inc(wf_arg, 1)
            for c in range(4):
                dve.wait_ge(wf_near, c + 1)
                dve_fraction(dve, wholes(c), waves[:, c, :], c, wf_frac)
            for c in range(4):
                dve.wait_ge(wf_sin, c + 1)
                dve.scalar_tensor_tensor(bigc[:, c, :], waves[:, c, :], 0.1, bigc[:, c, :], ALU.mult, ALU.add)\
                   .then_inc(wf_h, 1)
            dve.wait_ge(wf_out, 1)
            dve.tensor_tensor(xi[:, :, :], xi[:, :, :], banks(0, 2, 128), ALU.add)
            dve.drain()
            dve.tensor_tensor(xi[:, :, :], xi[:, :, :], rows_of(row("l1a_b2")), ALU.add)
            dve.drain()
            dve.tensor_tensor(x[:, :, :], x[:, :, :], xi[:, :, :], ALU.add).then_inc(x_done, 1)
            dve.drain()

        class Gated:

            def __init__(self, name, src, experts, chunks, slot, per, wide, slots_n):
                self.src, self.experts, self.chunks, self.slot, self.wide = src, experts, chunks, slot, wide
                self.per = per
                self.y_banks = 2 if wide > 128 else 1
                self.w = [sem(f"{name}_w{i}") for i in range(per)]
                self.up = sem(name + "_up")
                self.silu = sem(name + "_silu")
                self.h = sem(name + "_h")
                self.y = sem(name + "_y")
                self.acc = sem(name + "_acc")

        f1 = Gated("f1", l1f, 8, 4, L1F_SLOT, 2, 128, 2)
        f2 = Gated("f2", l2f, L2F_EXPERTS, 1, L2F_SLOT, 4, 128, 4)
        f3 = Gated("f3", l3f, L3F_PAIRS, 1, L3F_SLOT, 4, 256, 4)
        silus = work[:, 0:1024].rearrange("p (a c) -> p a c", a=2)

        def units(eng, f, step):
            n = 2 * f.per

            def body(i):
                for s in range(n):
                    step(n * i + s, s, i)
            rounds_n = f.experts // f.per
            peeled(eng, rounds_n, body)
            for u in range(rounds_n * n, 2 * f.experts + 1):
                step(u, u % n, rounds_n)

        def exists(f, u):
            return not isinstance(u, int) or 0 <= u < 2 * f.experts

        def pe_gated(pe, f):
            n = 2 * f.per

            def y(u, s):
                pe.wait_ge(f.h, f.chunks * (u + 1))
                waitfrom(pe, f.acc, 0, u - 1)
                yb = 4 + f.y_banks * (s % 2)
                per_bank = 512 // f.wide
                for t in range(4):
                    for c in range(f.chunks):
                        a = 256 * f.chunks + 128 * c
                        last = mm(pe, bank(yb + t // per_bank)[:, t % per_bank * f.wide:t % per_bank * f.wide + f.wide],
                                  h_at(s % 2, c)[:, 128 * t:128 * t + 128], slots[:, s // 2, a:a + f.wide],
                                  start=(c == 0), stop=(c == f.chunks - 1))
                last.then_inc(f.y, 1)

            def step(u, s, i):
                if exists(f, u):
                    if s % 2 == 0:
                        pe.wait_ge(f.w[s // 2], 16 * (i + 1))
                    for c in range(f.chunks):
                        kk = f.chunks * u + c
                        z = (f.chunks * s + c) % 2
                        waitfrom(pe, f.h, 0, kk - 1)
                        for part in range(2):
                            a = 128 * f.chunks * (1 - part) + 128 * c
                            last = mm(pe, bank(2 * z + part), slots[:, s // 2, a:a + 128],
                                      xnt[:, 512 * (s % 2):512 * (s % 2) + 512])
                        last.then_inc(f.up, 1)
                        if c == 0 and exists(f, u - 1):
                            y(u - 1, (s - 1) % n)
                else:
                    y(u - 1, (s - 1) % n)
            units(pe, f, step)

        def act_gated(act, f):
            def step(u, s, i):
                if exists(f, u):
                    for c in range(f.chunks):
                        kk = f.chunks * u + c
                        z = (f.chunks * s + c) % 2
                        act.wait_ge(f.up, kk + 1)
                        waitfrom(act, f.h, 0, kk - 1)
                        act.activation(silus[:, z, :], bank(2 * z), ACT.Silu).then_inc(f.silu, 1)
            units(act, f, step)

        def dve_gated(dve, f):
            n = 2 * f.per
            two_each = f.wide // 128

            def step(u, s, i):
                if exists(f, u):
                    if s % 2 == 0:
                        for j in range(two_each):
                            col = two_each * (f.per * i + s // 2) + j
                            src = gates[:, :, col] if isinstance(col, int) else gates[:, :, bass.ds(col, 1)].rearrange("p t o -> p (t o)")
                            dve.tensor_copy(gcol[:, s // 2, T * j:T * j + T], src)
                    for c in range(f.chunks):
                        kk = f.chunks * u + c
                        z = (f.chunks * s + c) % 2
                        dve.wait_ge(f.silu, kk + 1)
                        if c == 0:
                            waitfrom(dve, f.y, 0, u - 1)
                        dve.tensor_tensor(h_at(s % 2, c), silus[:, z, :], bank(2 * z + 1), ALU.mult).then_inc(f.h, 1)
                        if c == 0 and exists(f, u - 1):
                            add(u - 1, (s - 1) % n)
                else:
                    add(u - 1, (s - 1) % n)

            def add(u, s):
                dve.drain()
                dve.wait_ge(f.y, u + 1)
                yb = 4 + f.y_banks * (s % 2)
                per_bank = 512 // f.wide
                for j in range(two_each):
                    if j:
                        dve.drain()
                    for t in range(4):
                        tt = 4 * (s % 2) + t
                        a = t % per_bank * f.wide + 128 * j
                        last = dve_add_gated(dve, tt, bank(yb + t // per_bank)[:, a:a + 128],
                                             gcol[:, s // 2, T * j + tt:T * j + tt + 1])
                last.then_inc(f.acc, 1)
            units(dve, f, step)
            dve.drain()
            dve.nop().then_inc(x_done, 1)

        def sp_gated(sp, f):
            sp_experts(sp, f.src, f.slot, f.experts, f.per, f.w, f.y, 0)

        weigh_turn = sem("weigh_turn")
        weigh_cols = sem("weigh_cols")
        weigh_out = sem("weigh_out")
        weigh_in = sem("weigh_in")
        met = sem("met")
        met_sum = sem("met_sum")
        edge = sem("edge")
        edge_row = sem("edge_row")
        L1_CAPACITY = -(-5 * 2 * N // (4 * 8))
        weigh_dram = nc.dram_tensor("weigh_dram", (8, N), F32).ap()

        def pe_capacity(pe):
            pe.wait_ge(choice, 2)
            pe.transpose(bank(4)[0:64, 0:128], xi[:, 0, 0:64], cst("ident")).then_inc(weigh_turn, 1)
            for i in range(len(SHIFTS)):
                pe.wait_ge(met, i + 1)
                mm(pe, bank(4)[:, 128:129], cstb("same_expert"), metb[:, 0:1]).then_inc(met_sum, 1)
            pe.wait_ge(edge, 1)
            mm(pe, bank(4)[:, 256:272], cst("ones"), edges[:, :]).then_inc(edge_row, 1)
            pe.wait_ge(choice, 3)
            pe_prefix(pe, bank(6)[:, 0:64], picksb[:, 0:T, :].rearrange("p t e -> p (t e)"), T).then_inc(counted, 1)

        metb = sb("metb", [128, 1], BF16)
        edges = sb("edges", [128, 16])
        edger = sb("edger", [128, 16])
        found = sb("found", [128, 1], I32)
        trial = sb("trial", [128, 1], I32)
        step_i = sb("step_i", [128, 1], I32)
        count = sb("count", [128, 1])

        def dve_capacity(dve):
            sel, wt = picks[:, 2, :, 0:8], picks[:, 3, :, 0:8]
            dve.tensor_tensor(sel, picks[:, 0, :, 0:8], picks[:, 1, :, 0:8], ALU.add)
            dve.drain()
            dve.scalar_tensor_tensor(wt, sel, 1.0, gates[:, :, 0:8], ALU.subtract, ALU.add)
            dve.drain()
            dve.tensor_copy(xi[:, 0, 0:64].rearrange("p (e t) -> p t e", t=T), wt).then_inc(choice, 1)
            dve.memset(found[:, :], 0)
            dve.wait_ge(weigh_in, 256)
            row_w, hit = e[:, 0:N], e[:, N:2 * N]
            for i, shift in enumerate(SHIFTS):
                dve.drain()
                dve.tensor_tensor(trial[:, :], found[:, :], cis[:, i:i + 1], ALU.add)
                dve.drain()
                dve.tensor_scalar(hit, row_w, trial[:, :].bitcast(F32), 0.0, ALU.is_ge, ALU.add, accum_out=count[:, :])
                dve.drain()
                dve.tensor_scalar(metb[:, :], count[:, :], float(L1_CAPACITY), None, ALU.is_ge).then_inc(met, 1)
                dve.wait_ge(met_sum, i + 1)
                dve.tensor_scalar(count[:, :], bank(4)[:, 128:129], 1.0, 0.0, ALU.subtract, ALU.max)
                dve.drain()
                dve.tensor_scalar(step_i[:, :], count[:, :], float(1 << shift), None, ALU.mult)
                dve.drain()
                dve.tensor_tensor(found[:, :], found[:, :], step_i[:, :], ALU.add)
            dve.drain()
            dve.tensor_scalar(hit, row_w, found[:, :].bitcast(F32), 0.0, ALU.is_gt, ALU.add, accum_out=count[:, :])
            dve.tensor_scalar(edges[:, 0:8], cst("expert_row"), found[:, :].bitcast(F32), None, ALU.mult)
            dve.drain()
            dve.tensor_scalar(edges[:, 8:16], cst("expert_row"), count[:, :], None, ALU.mult).then_inc(edge, 1)
            dve.wait_ge(edge_row, 1)
            dve.tensor_copy(edger[:, :], bank(4)[:, 256:272])
            dve.drain()
            dve.tensor_scalar(edger[:, 8:16], edger[:, 8:16], -1.0, float(L1_CAPACITY), ALU.mult, ALU.add)
            over, same = picks[:, 0, :, 0:8], picks[:, 1, :, 0:8]
            dve.tensor_tensor(over, wt, rows_of(edger[:, 0:8]), ALU.is_gt)
            dve.tensor_tensor(same, wt, rows_of(edger[:, 0:8]), ALU.is_equal)
            dve.drain()
            dve.tensor_copy(picksb[:, 0:T, :], same).then_inc(choice, 1)
            dve.wait_ge(counted, 2)
            dve.tensor_tensor(sel, bank(6)[:, 0:64].rearrange("p (t e) -> p t e", e=8), rows_of(edger[:, 8:16]), ALU.is_lt)
            dve.drain()
            dve.tensor_tensor(same, same, sel, ALU.mult)
            dve.drain()
            dve.tensor_tensor(same, same, over, ALU.add)
            dve.drain()
            g8 = gates[:, :, 0:8]
            dve.tensor_tensor(g8, g8, same, ALU.mult)
            dve.drain()
            dve.tensor_reduce(tot[:, :], g8, AX.X, ALU.add)
            dve.drain()
            dve.tensor_scalar(tot[:, :], tot[:, :], 1.1920929e-07, None, ALU.max)
            dve.drain()
            dve.reciprocal(tot[:, :], tot[:, :])
            dve.drain()
            dve.tensor_tensor(g8, g8, per_token(tot[:, :], 8), ALU.mult)
            dve.drain()

        def sp_capacity(sp):
            sp.wait_ge(weigh_cols, 1)
            sp.dma_start(weigh_dram.rearrange("e (t p) -> (e t) p", p=128), et[0:64, 0:128]).then_inc(weigh_out, 16)
            sp.wait_ge(weigh_out, 16)
            for j in range(16):
                sp.dma_start(e[8 * j:8 * j + 8, 0:N], weigh_dram).then_inc(weigh_in, 16)

        def pe_f1(pe, m):
            pe_turn(pe, m, xn)
            pe_route(pe, m, 5, "l1f_wr", 8)
            pe_capacity(pe)
            pe_gated(pe, f1)

        def act_f1(act, m):
            act_turn(act, m)
            act_probs(act, 1, 8)
            act.wait_ge(weigh_turn, 1)
            act.copy(et[0:64, 0:128], bank(4)[0:64, 0:128]).then_inc(weigh_cols, 1)
            act_gated(act, f1)

        def dve_f1(dve, norm):
            dve_norm(dve, norm, x, xn, 1e-5)
            dve_probs(dve, 1, 8)
            dve_best(dve, 8, 2, 1.1920929e-07)
            dve_gates(dve, 8, 2)
            dve_capacity(dve)
            dve_gated(dve, f1)

        def pe_f2(pe, m):
            pe_turn(pe, m, xn)
            pe_route(pe, m, 8, "l2f_wr", 32)
            pe_gated(pe, f2)

        def act_f2(act, m):
            act_turn(act, m)
            act_probs(act, 2, 32)
            act_gated(act, f2)

        def dve_f2(dve, norm):
            dve_norm(dve, norm, x, xn, 1e-5)
            dve_probs(dve, 2, 32, "l2f_br")
            dve_best(dve, 32, 4, 1e-12)
            dve_gates(dve, 32, 4)
            dve.memset(gates[:, :, 32:36], 1.0)
            dve.drain()
            dve_gated(dve, f2)

        def pe_f3(pe, m):
            pe_turn(pe, m, xn)
            pe_route(pe, m, 11, "l3f_wg", 32)
            pe_gated(pe, f3)

        def act_f3(act, m):
            act_turn(act, m)
            act.wait_ge(route_less, 4)
            act.activation(probs[:, :, :], lg[:, :, :], ACT.Exp, scale=-1.0).then_inc(route_exp, 1)
            act_gated(act, f3)

        def dve_f3(dve, norm):
            LOW = -3.0e38
            dve_norm(dve, norm, x, xn, 1e-5)
            dve.wait_ge(route_logit, 4)
            dve.tensor_copy(lg[:, :, :], bank(5)[:, 0:256].rearrange("p (t e) -> p t e", e=32)).then_inc(route_less, 1)
            group = small[:, 0:8, 0:8]
            gmask = small[:, 8:16, 0:8]
            gbest = xi[:, 1, :].rearrange("p (t c) -> p t c", c=16)[:, :, 0:8]
            tops = xi[:, 2:4, :].rearrange("p a (n c) -> p (a n) c", c=8)
            dve.memset(group, LOW)
            dve.wait_ge(route_exp, 4)
            dve.tensor_scalar(probs[:, :, :], probs[:, :, :], 1.0, None, ALU.add)
            dve.drain()
            dve.reciprocal(probs[:, :, :], probs[:, :, :])
            dve.drain()
            dve.tensor_tensor(lg[:, :, :], probs[:, :, :], rows_of(row("l3f_bg")), ALU.add)
            dve.drain()
            for t in range(T):
                for g in range(4):
                    dve.max(tops[:, 4 * t + g, :], lg[:, t, 8 * g:8 * g + 8])
            dve.drain()
            dve.tensor_tensor(group[:, :, 0:4], tops[:, :, 0].rearrange("p (t g) -> p t g", g=4),
                              tops[:, :, 1].rearrange("p (t g) -> p t g", g=4), ALU.add)
            dve.drain()
            for t in range(T):
                dve.max(gbest[:, t, :], group[:, t, :])
            dve.drain()
            for t in range(T):
                dve.max_index(best_at[:, t, :], gbest[:, t, :], group[:, t, :])
            dve.drain()
            dve.tensor_copy(best_atf[:, :, :], best_at[:, :, :])
            dve.drain()
            dve.tensor_tensor(gmask[:, :, 0:4], rows_of(cst("iota")[:, 0:4]),
                              best_atf[:, :, 0:1].to_broadcast([128, T, 4]), ALU.is_equal)
            dve.tensor_tensor(gmask[:, :, 4:8], rows_of(cst("iota")[:, 0:4]),
                              best_atf[:, :, 1:2].to_broadcast([128, T, 4]), ALU.is_equal)
            dve.drain()
            dve.tensor_tensor(gmask[:, :, 0:4], gmask[:, :, 0:4], gmask[:, :, 4:8], ALU.add)
            dve.drain()
            dve.tensor_tensor(lg[:, :, :].rearrange("p t (g c) -> p t g c", c=8),
                              lg[:, :, :].rearrange("p t (g c) -> p t g c", c=8),
                              gmask[:, :, 0:4].unsqueeze(3).to_broadcast([128, T, 4, 8]), ALU.mult)
            dve.drain()
            for t in range(T):
                dve.max(best[:, t, :], lg[:, t, :])
            dve.drain()
            for t in range(T):
                dve.match_replace(tmp[:, t, :], best[:, t, :], lg[:, t, :], LOW)
            dve.drain()
            dve.tensor_scalar(tmp[:, :, :], tmp[:, :, :], LOW * 0.99, None, ALU.is_le)
            dve.drain()
            dve.tensor_tensor(gates[:, :, 0:32], tmp[:, :, :], probs[:, :, :], ALU.mult)
            dve.drain()
            dve.tensor_reduce(tot[:, :], gates[:, :, 0:32], AX.X, ALU.add)
            dve.drain()
            dve.tensor_scalar(tot[:, :], tot[:, :], 1e-20, None, ALU.add)
            dve.drain()
            dve.reciprocal(tot[:, :], tot[:, :])
            dve.drain()
            dve.tensor_tensor(gates[:, :, 0:32], gates[:, :, 0:32], per_token(tot[:, :], 32), ALU.mult)
            dve.drain()
            dve.tensor_scalar(gates[:, :, 0:32], gates[:, :, 0:32], 2.5, None, ALU.mult)
            dve.memset(gates[:, :, 32:34], 1.0)
            dve.drain()
            dve_gated(dve, f3)

        block = ctx.enter_context(nc.Block())

        @block.sync
        def _(sp):
            sp.dma_start(x[:, :, :], xin.rearrange("(t p) d -> p t d", p=128)).then_inc(x_loaded, 16)
            sp.dma_start(cfs[:, :], cf).then_inc(const_loaded, 16)
            sp.dma_start(work[:, 0:B_COLUMNS], cb).then_inc(const_loaded, 16)
            sp.dma_start(cis[:, :], ci).then_inc(const_loaded, 16)
            sp.dma_start(bsb[:, :], biases).then_inc(const_loaded, 16)
            sp.dma_start(rsb[:, :], rows.to_broadcast([128, ROW_COLUMNS])).then_inc(const_loaded, 16)
            sp.dma_start(ctxc[:, :], ctx_cols).then_inc(ctx_loaded, 16)
            sp.dma_start(ctxr[:, :, :], ctx_rows).then_inc(ctx_loaded, 16)
            for i in range(STAGES):
                a = WEIGHT_AT[WEIGHTS[i][0][0]][0]
                n = sum(width for _, width in WEIGHTS[i])
                sp.dma_start(wsb[:, a:a + n], weights[:, a:a + n]).then_inc(w_loaded[i], 16)
            sp.wait_ge(x_done, 2)
            sp_experts(sp, l0f, L0F_SLOT, 8, 2, f0_w, f0_y, 0)
            sp_capacity(sp)
            sp_gated(sp, f1)
            sp.wait_ge(x_done, 8)
            sp_gated(sp, f2)
            sp.wait_ge(x_done, 9)
            sp_gated(sp, f3)
            sp.wait_ge(x_done, STAGES)
            sp.dma_start(out.rearrange("(t p) d -> p t d", p=128), x[:, :, :]).then_inc(x_loaded, 16)
            sp.wait_ge(x_loaded, 32)

        @block.gpsimd
        def _(pool):
            pool.memset(minus_half[:, :], -0.5).then_inc(half_set, 1)
            pool.wait_ge(half_set, 1)
            pool_rstd(pool, 0)
            pool_rstd(pool, 1)
            pool_rstd(pool, 2)
            pool_rstd(pool, 3)
            for st in range(3, STAGES):
                if st == 4:
                    for n in range(5, 8):
                        if n == 7:
                            pool_wave(pool)
                        pool_rstd(pool, n)
                    continue
                pool_rstd(pool, 4 if st == 3 else st + 3)
                if st == 3:
                    pool_l1x(pool)
                if st in (7, 10):
                    pool_self(pool, st)
                if st == 9:
                    pool_l3x(pool)

        @block.scalar
        def _(act):
            act.wait_ge(const_loaded, 80)
            act_xs(act, 0, 0)
            act_la(act, 1)
            act_f0(act, 2)
            act_l1x(act, 3)
            act_wave(act, 4)
            act_f1(act, 6)
            act_xs(act, 1, 7)
            act_self(act, 7, 8)
            act_f2(act, 9)
            act_l3x(act, 10)
            act_self(act, 10, 11)
            act_f3(act, 12)

        @block.vector
        def _(dve):
            dve.wait_ge(x_loaded, 16)
            dve.wait_ge(const_loaded, 80)
            dve.tensor_copy(cbs[:, :], work[:, 0:B_COLUMNS])
            dve.drain()
            dve_xs(dve, 0, 0)
            dve_la(dve, 1)
            dve_f0(dve, 3)
            dve_l1x(dve, 4)
            dve_wave(dve, 5)
            dve_f1(dve, 8)
            dve_xs(dve, 1, 9)
            dve_self(dve, 7, 10)
            dve_f2(dve, 11)
            dve_l3x(dve, 12)
            dve_self(dve, 10, 13)
            dve_f3(dve, 14)

        @block.tensor
        def _(pe):
            pe_xs(pe, 0, 0, 0)
            pe_la(pe, 1, 1)
            pe_f0(pe, 2, 2)
            pe_l1x(pe, 3, 3)
            pe_wave(pe, 4, 4)
            pe_f1(pe, 6)
            pe_xs(pe, 1, 6, 7)
            pe_self(pe, 7, 8)
            pe_f2(pe, 9)
            pe_l3x(pe, 9, 10)
            pe_self(pe, 10, 11)
            pe_f3(pe, 12)



def laid_out(i):
    f = lambda a: np.asarray(a)
    t = lambda a: np.swapaxes(np.asarray(a), -1, -2)
    half = np.concatenate([np.arange(HD // 2, HD), np.arange(HD // 2)])
    swap = np.arange(HD) ^ 1
    by_half = (np.arange(H)[:, None] * HD + half[None, :]).ravel()
    by_two = (np.arange(H)[:, None] * HD + swap[None, :]).ravel()
    b2 = np.zeros((128, T, D), np.float32)
    for tt in range(T):
        b2[8 * tt:8 * tt + 8, tt] = f(i["L0_ffn_b2"])
    wt = {
        "l0x_w": t(i["L0_xattn_W"]),
        "l0a_wq": t(i["L0_attn_Wq"]), "l0a_wkv": np.concatenate([t(i["L0_attn_Wk"]), t(i["L0_attn_Wv"])], 1),
        "l0a_wd": t(i["L0_attn_Wd"]),
        "l0f_wg": f(i["L0_ffn_wg"]), "l0f_b2": b2.reshape(128, T * D),
        "l1x_wq": f(i["L1_xattn_Wq"]), "l1x_wk": f(i["L1_xattn_Wk"]), "l1x_wv": f(i["L1_xattn_Wv"]),
        "l1x_wo": f(i["L1_xattn_Wo"]),
        "l1a_wqf": f(i["L1_attn_Wqf"]), "l1a_wqp": f(i["L1_attn_Wqp"]), "l1a_wkf": f(i["L1_attn_Wkf"]),
        "l1a_wkp": f(i["L1_attn_Wkp"]), "l1a_wv": f(i["L1_attn_Wv"]), "l1a_wo": f(i["L1_attn_Wo"]),
        "l1a_w1": f(i["L1_attn_W1"]),
        "l1a_w2": f(i["L1_attn_W2"]).reshape(4, 128, 128).transpose(1, 0, 2).reshape(128, 512),
        "l1f_wr": t(i["L1_ffn_router_weight"]),
        "l2x_wq": f(i["L2_xattn_W_q"]), "l2x_wk": f(i["L2_xattn_W_k"]), "l2x_wv": f(i["L2_xattn_W_v"]),
        "l2a_wq": t(i["L2_attn_Wq"]), "l2a_wqr": t(i["L2_attn_Wq"])[:, by_half],
        "l2a_wk": t(i["L2_attn_Wk"]), "l2a_wkr": t(i["L2_attn_Wk"])[:, by_half],
        "l2a_wv": t(i["L2_attn_Wv"]), "l2a_wo": t(i["L2_attn_Wo"]),
        "l2f_wr": t(i["L2_ffn_router_w"]),
        "l3x_wq": f(i["L3_xattn_W_Q"]), "l3x_wk": f(i["L3_xattn_W_K"]), "l3x_wv": f(i["L3_xattn_W_V"]),
        "l3x_wo": f(i["L3_xattn_W_O"]),
        "l3a_wq": t(i["L3_attn_Wq"]), "l3a_wqr": t(i["L3_attn_Wq"])[:, by_two],
        "l3a_wk": t(i["L3_attn_Wk"]), "l3a_wkr": t(i["L3_attn_Wk"])[:, by_two],
        "l3a_wv": t(i["L3_attn_Wv"]), "l3a_wo": t(i["L3_attn_Wo"]),
        "l3f_wg": t(i["L3_ffn_gate_w"]),
    }
    rw = {
        "l0a_bkv": np.concatenate([f(i["L0_attn_bk"]), f(i["L0_attn_bv"])]), "l0a_bd": i["L0_attn_bd"],
        "l0a_gamma": i["L0_attn_gamma"], "l0a_beta": i["L0_attn_beta"], "l1x_bv": i["L1_xattn_bv"],
        "l1x_bo": i["L1_xattn_bo"], "l1a_g1": i["L1_attn_ln1_g"], "l1a_be1": i["L1_attn_ln1_b"],
        "l1a_bv": i["L1_attn_bv"], "l1a_bo": i["L1_attn_bo"], "l1a_iscale": f(i["L1_attn_iscale"]).reshape(-1),
        "l1a_g2": i["L1_attn_ln2_g"], "l1a_be2": i["L1_attn_ln2_b"], "l1a_b2": i["L1_attn_b2"],
        "l2x_bv": i["L2_xattn_b_v"], "l2a_bv": i["L2_attn_bv"], "l2a_bo": i["L2_attn_bo"],
        "l2f_br": i["L2_ffn_router_bias"], "l3x_bv": i["L3_xattn_b_V"], "l3x_bo": i["L3_xattn_b_O"],
        "l3f_bg": i["L3_ffn_gate_bias"],
    }
    two = lambda a: f(a).reshape(-1, 128).T
    bs = {
        "l0x_b": two(i["L0_xattn_b"]), "l0a_bq": two(i["L0_attn_bq"]), "l1x_bq": two(i["L1_xattn_bq"]),
        "l1x_bk": two(i["L1_xattn_bk"]), "l1a_bqf": two(i["L1_attn_bqf"]), "l1a_bqp": two(i["L1_attn_bqp"]),
        "l1a_bkf": two(i["L1_attn_bkf"]), "l1a_bkp": two(i["L1_attn_bkp"]), "l1a_b1": two(i["L1_attn_b1"]),
        "l2x_bq": two(i["L2_xattn_b_q"]), "l2x_bk": two(i["L2_xattn_b_k"]), "l2a_bq": two(i["L2_attn_bq"]),
        "l2a_bqr": two(f(i["L2_attn_bq"])[by_half]), "l2a_bk": two(i["L2_attn_bk"]),
        "l2a_bkr": two(f(i["L2_attn_bk"])[by_half]), "l3x_bq": two(i["L3_xattn_b_Q"]), "l3x_bk": two(i["L3_xattn_b_K"]),
    }
    chunks = lambda a: a.reshape(a.shape[0], -1, 128, 128).transpose(0, 2, 1, 3).reshape(a.shape[0], 128, -1)
    l0f = np.concatenate([f(i["L0_ffn_w1"]), chunks(f(i["L0_ffn_w2"])),
                          f(i["L0_ffn_b1"]).reshape(8, 4, 128).transpose(0, 2, 1)], 2)
    l1f = np.concatenate([t(i["L1_ffn_ff_pre_act_weight"]), t(i["L1_ffn_gate_weight"]),
                          chunks(t(i["L1_ffn_ff_post_act_weight"]))], 2)
    shared = lambda a: t(a).reshape(128, 4, 128).transpose(1, 0, 2)
    l2f = np.concatenate([
        np.concatenate([t(i["L2_ffn_up_w"]), shared(i["L2_ffn_sup_w"])], 0),
        np.concatenate([t(i["L2_ffn_gate_w"]), shared(i["L2_ffn_sgate_w"])], 0),
        np.concatenate([t(i["L2_ffn_down_w"]), t(i["L2_ffn_sdown_w"]).reshape(4, 128, 128)], 0)], 2)
    pair = lambda a, s: np.concatenate([t(a).reshape(16, 2, 128, 64).transpose(0, 2, 1, 3).reshape(16, 128, 128),
                                        t(s)[None]], 0)
    down = np.concatenate([t(i["L3_ffn_expert_down"]).reshape(16, 128, 128), t(i["L3_ffn_shared_down"])[None]], 0)
    apart = np.zeros((17, 128, 256), np.float32)
    apart[:, 0:64, 0:128] = down[:, 0:64]
    apart[:, 64:128, 128:256] = down[:, 64:128]
    l3f = np.concatenate([pair(i["L3_ffn_expert_up"], i["L3_ffn_shared_up"]),
                          pair(i["L3_ffn_expert_gate"], i["L3_ffn_shared_gate"]), apart], 2)
    ctxs = f(i["ctx_1024"])
    return {
        "xin": f(i["x"]).reshape(N, D),
        "ctx_cols": ctxs.reshape(B * S, D).T,
        "ctx_rows": ctxs.transpose(1, 0, 2),
        "weights": np.concatenate([wt[n] for n, _ in [w for g in WEIGHTS for w in g]], 1),
        "rows": np.concatenate([f(rw[n]) for n, _ in ROWS])[None, :],
        "biases": np.concatenate([bs[n] for n, _ in BIASES], 1),
        "l0f": l0f, "l1f": l1f, "l2f": l2f, "l3f": l3f,
        "cf": np.concatenate(list(const_columns().values()), 1),
        "cb": np.concatenate(list(const_bf_columns().values()), 1),
        "ci": const_int_columns(),
    }


def kernel(**inputs):
    import concourse.bacc as bacc
    from concourse.bass_utils import run_bass_kernel_spmd as run

    nc = bacc.Bacc("TRN2", target_bir_lowering=False, num_devices=1)
    arrays = {f"in_{k}": np.ascontiguousarray(v) for k, v in laid_out(inputs).items()}
    args = {k[3:]: nc.dram_tensor(k, a.shape, mybir.dt.from_np(a.dtype), kind="ExternalInput").ap()
            for k, a in arrays.items()}
    out = nc.dram_tensor("out_0", (N, D), F32, kind="ExternalOutput").ap()
    perceiver(nc, out=out, **args)
    r = run(nc, [arrays], core_ids=[0])
    return r.results[0]["out_0"].reshape(B, L, D)
```

```python
from contextlib import ExitStack

import numpy as np
import concourse.bass as bass
from concourse import mybir

F32 = mybir.dt.float32
BF16 = mybir.dt.bfloat16
I32 = mybir.dt.int32
U32 = mybir.dt.uint32
ALU = mybir.AluOpType
ACT = mybir.ActivationFunctionType
AX = mybir.AxisListType

D = 128
B = 16
L = 64
S = 128
N = B * L
T = N // 128
H = 16
HD = D // H
W = 16
L0_CAPACITY = 2 * N // 8
L1_CAPACITY = -(-5 * 2 * N // (4 * 8))
STAGES = 12



def const_columns():
    p = np.arange(128)
    c = {}
    c["ident"] = np.eye(128)
    c["ones"] = np.ones((128, 128))
    c["same_head"] = (p[:, None] // HD == p[None, :] // HD)
    c["head"] = (p[:, None] // HD == np.arange(H)[None, :])
    c["head_eps"] = c["head"] * 1e-6
    c["head_pair"] = (p[:, None] // (2 * HD) == np.arange(H // 2)[None, :])
    c["head_parity"] = (p[:, None] // HD % 2 == np.arange(2)[None, :])
    c["head_of_four"] = (p[:, None] // HD % 4 == np.arange(4)[None, :])
    c["wave_pair"] = (p[:, None] // (2 * W) == np.arange(4)[None, :])
    c["wave_parity"] = (p[:, None] // W % 2 == np.arange(2)[None, :])
    c["same_wave_head"] = (p[:, None] // W == p[None, :] // W)
    col = np.arange(32)
    ii, j = col // 16, col // 8 % 2
    r = p[:, None, None] // L
    k = np.arange(2)[None, :, None]
    c["value_soft"] = ((ii == r) & (j == k)).reshape(128, 64)
    c["value_wave"] = ((j == r) & (ii == k)).reshape(128, 64)
    s, t = p[:, None] % L, np.arange(L)[None, :]
    c["wave_causal"] = (s <= t) / np.sqrt(t + 1.0)
    c["position"] = np.broadcast_to(t, (128, L))
    f32 = np.float32
    d = p[:, None] % HD
    theta = f32(1250) ** (f32(-2.0) * (d % (HD // 2)).astype(f32) / f32(HD))
    ang = (t + 1).astype(f32) * theta.astype(f32)
    c["rope2_cos"] = np.cos(ang.astype(f32))
    c["rope2_sin"] = np.sin(ang.astype(f32)) * np.where(d < HD // 2, -1.0, 1.0)
    freq = f32(1.0) / f32(10000.0) ** ((2 * (d % (HD // 2))).astype(f32) / f32(HD))
    ang = t.astype(f32) * freq.astype(f32)
    c["rope3_cos"] = np.cos(ang.astype(f32))
    c["rope3_sin"] = np.sin(ang.astype(f32)) * np.where(d % 2 == 0, -1.0, 1.0)
    c["iota"] = np.broadcast_to(np.arange(32)[None, :], (128, 32))
    c["first_slot0"] = np.broadcast_to(L0_CAPACITY * np.arange(8)[None, :], (128, 8))
    c["first_slot1"] = np.broadcast_to(L1_CAPACITY * np.arange(8)[None, :], (128, 8))
    c["spare_row"] = np.arange(2 * T)[None, :] * 128 + p[:, None]
    c["expert_row"] = (p[:, None] == np.arange(8)[None, :])
    return {k: np.asarray(v, np.float32) for k, v in c.items()}


def const_bf_columns():
    p = np.arange(128)
    c = {}
    c["identb"] = np.eye(128)
    c["earlier"] = (p[:, None] < p[None, :])
    c["onesb"] = np.ones((128, 128))
    c["same_expert"] = (p[:, None] % 8 == p[None, :] % 8)
    c["causal"] = np.where(np.arange(L)[None, None, :] <= p[:, None, None] % L, 0.0, -1e30) * np.ones((1, 8, 1))
    return {k: np.asarray(v, np.float32).reshape(128, -1) for k, v in c.items()}


SHIFTS = [26, 22, 18, 14, 10, 6, 2, 0]


def const_int_columns():
    return (np.arange(128)[:, None] // 8 << np.array(SHIFTS)[None, :]).astype(np.int32)



WEIGHTS = [
    [("l0x_w", 128)],
    [("l0a_wq", 128), ("l0a_wkv", 256), ("l0a_wd", 128)],
    [("l0f_wg", 8), ("l0f_b2", 1024)],
    [("l1x_wq", 128), ("l1x_wk", 128), ("l1x_wv", 128), ("l1x_wo", 128)],
    [("l1a_wqf", 256), ("l1a_wqp", 256), ("l1a_wkf", 256), ("l1a_wkp", 256), ("l1a_wv", 128),
     ("l1a_wo", 128), ("l1a_w1", 512), ("l1a_w2", 512)],
    [("l1f_wr", 8)],
    [("l2x_wq", 128), ("l2x_wk", 128), ("l2x_wv", 128)],
    [("l2a_wq", 128), ("l2a_wqr", 128), ("l2a_wk", 128), ("l2a_wkr", 128), ("l2a_wv", 128), ("l2a_wo", 128)],
    [("l2f_wr", 32)],
    [("l3x_wq", 128), ("l3x_wk", 128), ("l3x_wv", 128), ("l3x_wo", 128)],
    [("l3a_wq", 128), ("l3a_wqr", 128), ("l3a_wk", 128), ("l3a_wkr", 128), ("l3a_wv", 128), ("l3a_wo", 128)],
    [("l3f_wg", 32)],
]
ROWS = [("l0a_bkv", 256), ("l0a_bd", 128), ("l0a_gamma", 128), ("l0a_beta", 128), ("l1x_bv", 128), ("l1x_bo", 128),
        ("l1a_g1", 128), ("l1a_be1", 128), ("l1a_bv", 128), ("l1a_bo", 128), ("l1a_iscale", 16), ("l1a_g2", 128),
        ("l1a_be2", 128), ("l1a_b2", 128), ("l2x_bv", 128), ("l2a_bv", 128), ("l2a_bo", 128), ("l2f_br", 32),
        ("l3x_bv", 128), ("l3x_bo", 128), ("l3f_bg", 32)]
BIASES = [("l0x_b", 1), ("l0a_bq", 1), ("l1x_bq", 1), ("l1x_bk", 1), ("l1a_bqf", 2), ("l1a_bqp", 2), ("l1a_bkf", 2),
          ("l1a_bkp", 2), ("l1a_b1", 4), ("l2x_bq", 1), ("l2x_bk", 1), ("l2a_bq", 1), ("l2a_bqr", 1), ("l2a_bk", 1),
          ("l2a_bkr", 1), ("l3x_bq", 1), ("l3x_bk", 1)]


def places(items):
    at, out = 0, {}
    for name, width in items:
        out[name] = (at, width)
        at += width
    return out, at


WEIGHT_AT, WEIGHT_COLUMNS = places([w for group in WEIGHTS for w in group])
ROW_AT, ROW_COLUMNS = places(ROWS)
BIAS_AT, BIAS_COLUMNS = places(BIASES)
L0F_SLOT = 512 + 512 + 4
L1F_SLOT = 512 + 512 + 512
L2F_SLOT = 128 + 128 + 128
L3F_SLOT = 128 + 128 + 256
L2F_EXPERTS = 32 + 4
L3F_PAIRS = 16 + 1


def perceiver(nc, xin, ctx_cols, ctx_rows, weights, rows, biases, l0f, l1f, l2f, l3f, cf, cb, ci, out):
    F_AT, F_COLUMNS = places([(k, v.shape[1]) for k, v in const_columns().items()])
    B_AT, B_COLUMNS = places([(k, v.shape[1]) for k, v in const_bf_columns().items()])
    with ExitStack() as ctx:
        def sb(name, shape, dt=F32):
            return ctx.enter_context(nc.sbuf_tensor(name, shape, dt))

        def sem(name):
            return ctx.enter_context(nc.semaphore(name))

        x = sb("x", [128, T, D])
        xn = sb("xn", [128, T, D])
        xi = sb("xi", [128, T, D])
        xnt = sb("xnt", [128, N])
        ctxc = sb("ctxc", [128, B * S])
        ctxr = sb("ctxr", [128, B, D])
        wsb = sb("wsb", [128, WEIGHT_COLUMNS])
        rsb = sb("rsb", [128, ROW_COLUMNS])
        bsb = sb("bsb", [128, BIAS_COLUMNS])
        cfs = sb("cfs", [128, F_COLUMNS])
        cbs = sb("cbs", [128, B_COLUMNS], BF16)
        cis = sb("cis", [128, len(SHIFTS)], I32)
        minus_half = sb("minus_half", [128, T])
        stats = sb("stats", [128, T, 6])
        moments = sb("moments", [128, T, 2])
        variance = sb("variance", [128, T])
        rstd = sb("rstd", [128, T])
        q = sb("q", [128, N])
        k = sb("k", [128, B * S])
        v = sb("v", [128, B, S])
        e = sb("e", [128, B * S])
        et = sb("et", [128, B * S])
        at = sb("at", [128, N])
        big = sb("big", [128, 4096])
        work = sb("work", [128, 4096])
        slots = sb("slots", [128, 4, L1F_SLOT])
        small = sb("small", [128, 32, 16])
        ps = ctx.enter_context(nc.psum_tensor("ps", [128, 8, 512], F32))

        def w(name, a=0, n=None):
            at0, width = WEIGHT_AT[name]
            return wsb[:, at0 + a:at0 + a + (width if n is None else n)]

        def row(name):
            at0, width = ROW_AT[name]
            return rsb[:, at0:at0 + width]

        def bias(name, i=0):
            return bsb[:, BIAS_AT[name][0] + i:BIAS_AT[name][0] + i + 1]

        def cst(name):
            at0, width = F_AT[name]
            return cfs[:, at0:at0 + width]

        def cstb(name):
            at0, width = B_AT[name]
            return cbs[:, at0:at0 + width]

        def rows_of(ap, n=T):
            return ap.unsqueeze(1).to_broadcast([128, n, ap.shape[1]])

        def bank(i):
            return ps[:, i, :]

        def banks(i, n, width):
            return ps[:, i:i + n, :].rearrange("p b (c w) -> p (b c) w", w=width)

        const_loaded = sem("const_loaded")
        x_loaded = sem("x_loaded")
        ctx_loaded = sem("ctx_loaded")
        w_loaded = [sem(f"w_loaded{i}") for i in range(STAGES)]
        half_set = sem("half_set")
        ones_set = sem("ones_set")
        x_done = sem("x_done")
        stats_ready = sem("stats_ready")
        rstd_ready = sem("rstd_ready")
        rows_ready = sem("rows_ready")
        turned = sem("turned")
        xnt_ready = sem("xnt_ready")


        def dve_norm(dve, n, src, dst, eps, gain=None, shift=None, publish=True):
            for t in range(T):
                dve.bn_stats(stats[:, t, :], src[:, t, :])
            dve.drain()
            for t in range(T):
                dve.bn_aggr(moments[:, t, :], stats[:, t, :])
            dve.drain()
            dve.tensor_scalar(variance[:, :], moments[:, :, 1], eps, None, ALU.add).then_inc(stats_ready, 1)
            dve.wait_ge(rstd_ready, n + 1)
            for t in range(T):
                last = dve.tensor_scalar(dst[:, t, :], src[:, t, :], moments[:, t, 0:1], rstd[:, t:t + 1],
                                         ALU.subtract, ALU.mult)
                if publish and gain is None:
                    last.then_inc(rows_ready, 1)
            if gain is not None:
                dve.drain()
                dve.tensor_tensor(dst[:, :, :], dst[:, :, :], rows_of(gain), ALU.mult)
                dve.drain()
                last = dve.tensor_tensor(dst[:, :, :], dst[:, :, :], rows_of(shift), ALU.add)
                if publish:
                    last.then_inc(rows_ready, T)

        def pool_rstd(pool, n):
            pool.wait_ge(stats_ready, n + 1)
            pool.tensor_tensor(rstd[:, :], variance[:, :], minus_half[:, :], ALU.pow).then_inc(rstd_ready, 1)

        def pe_turn(pe, m, src):
            for t in range(T):
                pe.wait_ge(rows_ready, T * m + t + 1)
                last = pe.transpose(bank(6 + t // 4)[:, t % 4 * 128:t % 4 * 128 + 128], src[:, t, :], cst("ident"))
                if t % 4 == 3:
                    last.then_inc(turned, 1)

        def act_turn(act, m):
            for h in range(2):
                act.wait_ge(turned, 2 * m + h + 1)
                act.copy(xnt[:, 512 * h:512 * h + 512], bank(6 + h)).then_inc(xnt_ready, 1)

        def mm(pe, o, lhs, rhs, start=True, stop=True):
            return pe.matmul(o, lhs, rhs, start=start, stop=stop)

        def peeled(eng, n, body, first=1):
            for i in range(first):
                body(i)
            with eng.Fori(first, n) as i:
                body(i)

        def wait(eng, s, value):
            if not isinstance(value, int) or value > 0:
                eng.wait_ge(s, value)

        def waitfrom(eng, s, base, more):
            if not isinstance(more, int) or more > 0:
                eng.wait_ge(s, base + more)

        kproj = sem("kproj")
        k_ready = sem("k_ready")
        vproj = sem("vproj")
        v_ready = sem("v_ready")
        qproj = sem("qproj")
        q_ready = sem("q_ready")
        VBANK = [4, 5, 0, 1]
        CROSS = [("l0x_w", "l0x_b", "l0x_w", "l0x_b", None, None)] + [
            (f"l{i}x_wq", f"l{i}x_bq", f"l{i}x_wk", f"l{i}x_bk", f"l{i}x_wv", f"l{i}x_bv") for i in (1, 2, 3)]

        def pe_project(pe, n, stage, m):
            wq, _, wk, _, wv, _ = CROSS[n]
            if stage:
                pe.wait_ge(x_done, stage)
            else:
                pe.wait_ge(ctx_loaded, 32)
                pe.wait_ge(const_loaded, 80)
            pe.wait_ge(w_loaded[stage], 16)
            for c in range(4):
                mm(pe, bank(c), w(wk), ctxc[:, 512 * c:512 * c + 512]).then_inc(kproj, 1)
            if n:
                for c in range(4):
                    if c >= 2:
                        pe.wait_ge(k_ready, 4 * n + c - 1)
                    for i in range(4):
                        b = 4 * c + i
                        last = mm(pe, bank(VBANK[c])[:, 128 * i:128 * i + 128], ctxc[:, 128 * b:128 * b + 128], w(wv))
                    last.then_inc(vproj, 1)
            pe_turn(pe, m, xn)
            pe.wait_ge(k_ready, 4 * n + 4)
            for h in range(2):
                pe.wait_ge(xnt_ready, 2 * m + h + 1)
                mm(pe, bank(2 + h), w(wq), xnt[:, 512 * h:512 * h + 512]).then_inc(qproj, 1)

        def act_project(act, n, m):
            _, bq, _, bk, _, _ = CROSS[n]
            for c in range(4):
                act.wait_ge(kproj, 4 * n + c + 1)
                act.activation(k[:, 512 * c:512 * c + 512], bank(c), ACT.Identity, bias=bias(bk)).then_inc(k_ready, 1)
            act_turn(act, m)
            for h in range(2):
                act.wait_ge(qproj, 2 * n + h + 1)
                act.activation(q[:, 512 * h:512 * h + 512], bank(2 + h), ACT.Identity, bias=bias(bq)).then_inc(q_ready, 1)

        def dve_values(dve, n):
            for c in range(4):
                dve.wait_ge(vproj, 4 * (n - 1) + c + 1)
                dve.tensor_tensor(v[:, 4 * c:4 * c + 4, :], banks(VBANK[c], 1, 128), rows_of(row(CROSS[n][5]), 4),
                                  ALU.add).then_inc(v_ready, 1)

        xs_score = sem("xs_score")
        xs_less = sem("xs_less")
        xs_exp = sem("xs_exp")
        xs_turn = sem("xs_turn")
        xs_et = sem("xs_et")
        xs_out = sem("xs_out")

        def pe_xs(pe, n, stage, m):
            c = 2 * n
            pe_project(pe, c, stage, m)
            if n:
                pe.wait_ge(v_ready, 4 * c)
            for h in range(2):
                pe.wait_ge(q_ready, 2 * c + h + 1)
                for i in range(8):
                    b = 8 * h + i
                    o = bank(h)[64 * (b % 2):64 * (b % 2) + 64, i // 2 * 128:i // 2 * 128 + 128]
                    last = mm(pe, o, q[:, L * b:L * b + L], k[:, S * b:S * b + S])
                last.then_inc(xs_score, 1)
            for h in range(2):
                pe.wait_ge(xs_exp, 2 * n + h + 1)
                for i in range(4):
                    t = 4 * h + i
                    last = pe.transpose(bank(2 + h)[:, 128 * i:128 * i + 128], e[:, 128 * t:128 * t + 128], cst("ident"))
                last.then_inc(xs_turn, 1)
            for h in range(2):
                pe.wait_ge(xs_et, 2 * n + h + 1)
                for i in range(8):
                    b = 8 * h + i
                    o = bank(4 + h)[64 * (b % 2):64 * (b % 2) + 64, i // 2 * 128:i // 2 * 128 + 128]
                    last = mm(pe, o, et[:, L * b:L * b + L], v[:, b, :] if n else ctxr[:, b, :])
                last.then_inc(xs_out, 1)

        def act_xs(act, n, m):
            act_project(act, 2 * n, m)
            for h in range(2):
                act.wait_ge(xs_less, 2 * n + h + 1)
                act.activation(e[:, 512 * h:512 * h + 512], big[:, 512 * h:512 * h + 512], ACT.Exp,
                               scale=float(D) ** -0.5 if n else 1.0).then_inc(xs_exp, 1)
            for h in range(2):
                act.wait_ge(xs_turn, 2 * n + h + 1)
                act.copy(et[:, 512 * h:512 * h + 512], bank(2 + h)).then_inc(xs_et, 1)

        def dve_xs(dve, n, norm):
            dve_norm(dve, norm, x, xn, 1e-5)
            if n:
                dve_values(dve, 2 * n)
            top, total, inverse = small[:, 0, 0:8], small[:, 1, 0:8], small[:, 2, 0:8]
            for h in range(2):
                dve.wait_ge(xs_score, 2 * n + h + 1)
                dve.tensor_reduce(top[:, 4 * h:4 * h + 4], banks(h, 1, 128), AX.X, ALU.max)
                dve.drain()
                dve.tensor_tensor(big[:, 512 * h:512 * h + 512].rearrange("p (t s) -> p t s", s=S), banks(h, 1, 128),
                                  top[:, 4 * h:4 * h + 4].unsqueeze(2).to_broadcast([128, 4, S]),
                                  ALU.subtract).then_inc(xs_less, 1)
            for h in range(2):
                dve.wait_ge(xs_exp, 2 * n + h + 1)
                dve.tensor_reduce(total[:, 4 * h:4 * h + 4], e[:, 512 * h:512 * h + 512].rearrange("p (t s) -> p t s", s=S),
                                  AX.X, ALU.add)
            dve.drain()
            dve.reciprocal(inverse, total)
            dve.drain()
            for h in range(2):
                dve.wait_ge(xs_out, 2 * n + h + 1)
                for i in range(4):
                    t = 4 * h + i
                    last = dve.scalar_tensor_tensor(x[:, t, :], bank(4 + h)[:, 128 * i:128 * i + 128],
                                                    inverse[:, t:t + 1], x[:, t, :], ALU.mult, ALU.add)
            last.then_inc(x_done, 1)
            dve.drain()

        la_q = sem("la_q")
        la_kv = sem("la_kv")
        la_neg = sem("la_neg")
        la_exp = sem("la_exp")
        la_feat = sem("la_feat")
        la_sum = sem("la_sum")
        la_kvm = sem("la_kvm")
        la_ctx = sem("la_ctx")
        la_div = sem("la_div")
        la_turn = sem("la_turn")
        la_cols = sem("la_cols")
        la_out = sem("la_out")
        KV = D + 1
        KVH = D + H
        vone = work[:, 0:T * KV].rearrange("p (t c) -> p t c", c=KV)
        kfeat = big[:, 0:N].rearrange("p (t c) -> p t c", c=D)
        kvm = slots[:, 0:2, :].rearrange("p a b -> p (a b)")[:, 0:B * KVH].rearrange("p (b c) -> p b c", c=KVH)

        def pe_la(pe, stage, m):
            pe_turn(pe, m, xn)
            pe.wait_ge(w_loaded[stage], 16)
            for h in range(2):
                pe.wait_ge(xnt_ready, 2 * m + h + 1)
                mm(pe, bank(4 + h), w("l0a_wq"), xnt[:, 512 * h:512 * h + 512]).then_inc(la_q, 1)
            for t in range(T):
                last = mm(pe, bank(t // 2)[:, 256 * (t % 2):256 * (t % 2) + 256], xnt[:, 128 * t:128 * t + 128],
                          w("l0a_wkv"))
                if t % 2:
                    last.then_inc(la_kv, 1)
            pe.wait_ge(la_feat, 3)
            for b in range(B):
                p = 64 * (b % 2)
                t = b // 2
                last = mm(pe, bank(3 * (b % 2) + t // 3)[:, KV * (t % 3):KV * (t % 3) + KV], kfeat[p:p + 64, t, :],
                          vone[p:p + 64, t, :])
            last.then_inc(la_sum, 1)
            pe.wait_ge(la_kvm, 1)
            for b in range(B):
                t, p = b // 2, 64 * (b % 2)
                last = mm(pe, bank(t // 3)[p:p + 64, KVH * (t % 3):KVH * (t % 3) + KVH], q[:, L * b:L * b + L],
                          kvm[:, T * (b % 2) + t, :])
            last.then_inc(la_ctx, 1)
            pe.wait_ge(la_div, 1)
            for t in range(T):
                last = pe.transpose(bank(6 + t // 4)[:, t % 4 * 128:t % 4 * 128 + 128], xi[:, t, :], cst("ident"))
                if t % 4 == 3:
                    last.then_inc(la_turn, 1)
            for t in range(T):
                pe.wait_ge(la_cols, t // 4 + 1)
                last = mm(pe, bank(3 + t // 4)[:, t % 4 * 128:t % 4 * 128 + 128], at[:, 128 * t:128 * t + 128],
                          w("l0a_wd"))
            last.then_inc(la_out, 1)

        def act_la(act, m):
            act_turn(act, m)
            act.wait_ge(la_neg, 1)
            act.activation(e[:, 0:N], e[:, 0:N], ACT.Exp).then_inc(la_exp, 1)
            act.wait_ge(la_neg, 2)
            act.activation(et[:, 0:N], et[:, 0:N], ACT.Exp).then_inc(la_exp, 1)
            for h in range(2):
                act.wait_ge(la_turn, h + 1)
                act.copy(at[:, 512 * h:512 * h + 512], bank(6 + h)).then_inc(la_cols, 1)

        def dve_la(dve, norm):
            dve_norm(dve, norm, x, xn, 1e-5)
            dve.wait_ge(la_q, 2)
            dve.tensor_scalar(e[:, 0:N], ps[:, 4:6, :].rearrange("p b c -> p (b c)"), bias("l0a_bq"), 0.0,
                              ALU.add, ALU.min).then_inc(la_neg, 1)
            dve.tensor_scalar(q[:, :], ps[:, 4:6, :].rearrange("p b c -> p (b c)"), bias("l0a_bq"), 0.0,
                              ALU.add, ALU.max)
            dve.wait_ge(la_kv, 4)
            kv = banks(0, 4, 256)
            krow = rows_of(row("l0a_bkv")[:, 0:128])
            vrow = rows_of(row("l0a_bkv")[:, 128:256])
            dve.tensor_tensor(kfeat, kv[:, :, 0:128], krow, ALU.add)
            dve.memset(vone[:, :, 128:129], 1.0)
            dve.tensor_tensor(vone[:, :, 0:128], kv[:, :, 128:256], vrow, ALU.add).then_inc(la_feat, 1)
            dve.drain()
            dve.tensor_scalar(et[:, 0:N], big[:, 0:N], 0.0, None, ALU.min).then_inc(la_neg, 1)
            dve.wait_ge(la_exp, 1)
            dve.tensor_tensor(q[:, :], q[:, :], e[:, 0:N], ALU.add).then_inc(la_feat, 1)
            dve.wait_ge(la_exp, 2)
            dve.scalar_tensor_tensor(big[:, 0:N], big[:, 0:N], 0.0, et[:, 0:N], ALU.max,
                                     ALU.add).then_inc(la_feat, 1)
            dve.wait_ge(la_sum, 1)
            for g in range(6):
                nb, a = min(3, T - 3 * (g % 3)), T * (g // 3) + 3 * (g % 3)
                src = bank(g)[:, 0:nb * KV].rearrange("p (b c) -> p b c", c=KV)
                dve.tensor_tensor(kvm[:, a:a + nb, 0:128], src[:, :, 0:128], rows_of(cst("same_head"), nb), ALU.mult)
                dve.tensor_tensor(kvm[:, a:a + nb, 128:KVH], rows_of(cst("head"), nb),
                                  src[:, :, 128:129].to_broadcast([128, nb, H]), ALU.mult)
            dve.drain()
            dve.tensor_tensor(kvm[:, :, 128:KVH], kvm[:, :, 128:KVH], rows_of(cst("head_eps"), B), ALU.add)\
               .then_inc(la_kvm, 1)
            dve.wait_ge(la_ctx, 1)
            z = small[:, 0:8, :]
            for g in range(3):
                nt = min(3, T - 3 * g)
                src = bank(g)[:, 0:nt * KVH].rearrange("p (t c) -> p t c", c=KVH)
                dve.reciprocal(z[:, 3 * g:3 * g + nt, :], src[:, :, 128:KVH])
            dve.drain()
            for t in range(T):
                src = bank(t // 3)[:, KVH * (t % 3):KVH * (t % 3) + 128].rearrange("p (h d) -> p h d", d=HD)
                last = dve.tensor_tensor(xi[:, t, :].rearrange("p (h d) -> p h d", d=HD), src,
                                         z[:, t, :].unsqueeze(2).to_broadcast([128, H, HD]), ALU.mult)
            last.then_inc(la_div, 1)
            dve.wait_ge(la_out, 1)
            dve.tensor_tensor(xi[:, :, :], banks(3, 2, 128), rows_of(row("l0a_bd")), ALU.add)
            dve.drain()
            dve.tensor_tensor(xi[:, :, :], xi[:, :, :], xn[:, :, :], ALU.add)
            dve.drain()
            dve_norm(dve, norm + 1, xi, xi, 1e-12, row("l0a_gamma"), row("l0a_beta"), publish=False)
            dve.drain()
            dve.tensor_tensor(x[:, :, :], x[:, :, :], xi[:, :, :], ALU.add).then_inc(x_done, 1)
            dve.drain()

        route_logit = sem("route_logit")
        route_less = sem("route_less")
        route_exp = sem("route_exp")
        choice = sem("choice")
        counted = sem("counted")
        NB = 36
        lg = sb("lg", [128, T, 32])
        probs = sb("probs", [128, T, 32])
        best = sb("best", [128, T, 8])
        best_at = sb("best_at", [128, T, 8], U32)
        best_atf = sb("best_atf", [128, T, 8])
        picks = sb("picks", [128, 4, T, 32])
        share = sb("share", [128, T, 8])
        tot = sb("tot", [128, T])
        gates = sb("gates", [128, T, NB])
        picksb = sb("picksb", [128, 2 * T, 8], BF16)
        tmp = sb("tmp", [128, T, 32])
        silus = work[:, 0:1024].rearrange("p (a c) -> p a c", a=2)
        gcol = sb("gcol", [128, 4, 2 * T])

        def pe_route(pe, m, stage, wname, E):
            pe.wait_ge(w_loaded[stage], 16)
            for t in range(T):
                pe.wait_ge(xnt_ready, 2 * m + t // 4 + 1)
                last = mm(pe, bank(5)[:, E * t:E * t + E], xnt[:, 128 * t:128 * t + 128], w(wname))
            last.then_inc(route_logit, 1)

        def per_token(ap, E):
            return ap.unsqueeze(2).to_broadcast([128, T, E])

        def dve_probs(dve, n, E, brow=None):
            lgE, pr = lg[:, :, 0:E], probs[:, :, 0:E]
            dve.wait_ge(route_logit, n + 1)
            src = bank(5)[:, 0:T * E].rearrange("p (t e) -> p t e", e=E)
            if brow is None:
                dve.tensor_copy(lgE, src)
            else:
                dve.tensor_tensor(lgE, src, rows_of(row(brow)), ALU.add)
            dve.drain()
            dve.tensor_reduce(tot[:, :], lgE, AX.X, ALU.max)
            dve.drain()
            dve.tensor_tensor(lgE, lgE, per_token(tot[:, :], E), ALU.subtract).then_inc(route_less, 1)
            dve.wait_ge(route_exp, n + 1)
            dve.tensor_reduce(tot[:, :], pr, AX.X, ALU.add)
            dve.drain()
            dve.reciprocal(tot[:, :], tot[:, :])
            dve.drain()
            dve.tensor_tensor(pr, pr, per_token(tot[:, :], E), ALU.mult)
            dve.drain()

        def act_probs(act, n, E, scale=1.0):
            act.wait_ge(route_less, n + 1)
            act.activation(probs[:, :, 0:E], lg[:, :, 0:E], ACT.Exp, scale=scale).then_inc(route_exp, 1)

        def dve_best(dve, E, K, floor):
            for t in range(T):
                dve.max(best[:, t, :], probs[:, t, 0:E])
            dve.drain()
            for t in range(T):
                dve.max_index(best_at[:, t, :], best[:, t, :], probs[:, t, 0:E])
            dve.tensor_reduce(tot[:, :], best[:, :, 0:K], AX.X, ALU.add)
            dve.drain()
            dve.tensor_copy(best_atf[:, :, :], best_at[:, :, :])
            if floor:
                dve.tensor_scalar(tot[:, :], tot[:, :], floor, None, ALU.max)
            dve.drain()
            for j in range(K):
                dve.tensor_tensor(picks[:, j, :, 0:E], rows_of(cst("iota")[:, 0:E]),
                                  best_atf[:, :, j:j + 1].to_broadcast([128, T, E]), ALU.is_equal)
            dve.reciprocal(tot[:, :], tot[:, :])
            dve.drain()
            dve.tensor_tensor(share[:, :, 0:K], best[:, :, 0:K], per_token(tot[:, :], K), ALU.mult)
            dve.drain()

        def dve_gates(dve, E, K):
            dve.tensor_tensor(gates[:, :, 0:E], picks[:, 0, :, 0:E], share[:, :, 0:1].to_broadcast([128, T, E]), ALU.mult)
            for j in range(1, K):
                if j > 1:
                    dve.drain()
                dve.tensor_tensor(tmp[:, :, 0:E], picks[:, j, :, 0:E], share[:, :, j:j + 1].to_broadcast([128, T, E]),
                                  ALU.mult)
                dve.drain()
                dve.tensor_tensor(gates[:, :, 0:E], gates[:, :, 0:E], tmp[:, :, 0:E], ALU.add)
            dve.drain()

        def pe_prefix(pe, o, src, n):
            pe.matmul(o, cstb("earlier"), src, start=True, stop=False)
            for d in range(1, n):
                last = pe.matmul(o[:, 8 * d:8 * n], cstb("onesb"), src[:, 0:8 * (n - d)], start=False, stop=(d == n - 1))
            return last

        f0_b = sem("f0_b")

        def h_at(u, c):
            return big[:, 2048 * (u % 2) + 512 * c:2048 * (u % 2) + 512 * c + 512]

        def sp_experts(sp, src, width, n, per, sems, y_done, units_back):
            def body(i):
                for s in range(per):
                    wait(sp, y_done, 2 * (per * (i - 1) + s) + 2)
                    sp.dma_start(slots[:, s, 0:width], src[per * i + s]).then_inc(sems[s], 16)
            peeled(sp, n // per, body)
            for s in range(n % per):
                i = n // per
                wait(sp, y_done, 2 * (per * (i - 1) + s) + 2)
                sp.dma_start(slots[:, s, 0:width], src[per * i + s]).then_inc(sems[s], 16)

        class Routed:

            def __init__(self, n, src, capacity, slot, gated):
                self.n, self.src, self.capacity, self.slot, self.gated = n, src, capacity, slot, gated
                self.slots = 8 * capacity
                self.groups = self.slots // 512
                self.tiles = [min(128, capacity - a) for a in range(0, capacity, 128)]
                self.stores = 1 if capacity % 128 == 0 else 2
                self.sent = nc.dram_tensor(f"sent{n}", (self.slots + 2 * N, D), F32).ap()
                self.made = nc.dram_tensor(f"made{n}", (self.slots + 1, D), F32).ap()

        r0 = Routed(0, l0f, L0_CAPACITY, L0F_SLOT, False)
        r1 = Routed(1, l1f, L1_CAPACITY, L1F_SLOT, True)
        zeros_set = sem("zeros_set")
        cleared = sem("cleared")
        rt_slots = sem("rt_slots")
        rt_sent = sem("rt_sent")
        rt_back = [sem(f"rt_back{g}") for g in range(5)]
        rt_turn = sem("rt_turn")
        rt_cols = sem("rt_cols")
        rt_w = [sem(f"rt_w{i}") for i in range(4)]
        rt_up = sem("rt_up")
        rt_silu = sem("rt_silu")
        rt_h = sem("rt_h")
        rt_y = sem("rt_y")
        rt_rows = sem("rt_rows")
        rt_made = [sem(f"rt_made{i}") for i in range(4)]
        rt_got = [sem(f"rt_got{g}") for g in range(4)]
        slot_at = sb("slot_at", [128, 2 * T])
        kept = sb("kept", [128, 2 * T])
        row_to = sb("row_to", [128, 2 * T], U32)
        row_from = sb("row_from", [128, 2 * T], U32)
        slot_cols = work[:, 1024:1024 + r1.slots]

        def slot_rows(g):
            return v[:, 4 * g:4 * g + 4, :] if g < 4 else q[:, 0:512].rearrange("p (n d) -> p n d", d=D)

        def hidden(s, c, r):
            at0 = 2048 * (s % 2) + r.capacity * c
            return big[:, at0:at0 + r.capacity]

        def pool_clear(pool):
            pool.memset(slots[:, 2:4, :], 0.0).then_inc(zeros_set, 1)

        def sp_clear(sp):
            zeros = slots[:, 2:4, :].rearrange("p a b -> p (a b)")
            sp.wait_ge(zeros_set, 1)
            for r in (r0, r1):
                width = r.slots * D // 128
                sp.dma_start(r.sent[0:r.slots, :].rearrange("(p a) d -> p (a d)", p=128), zeros[:, 0:width]).then_inc(cleared, 16)
                sp.dma_start(r.made[r.slots:r.slots + 1, :], zeros[0:1, 0:D]).then_inc(cleared, 16)

        def sp_routed(sp, r):
            n = r.n

            def load(e, s):
                sp.dma_start(slots[:, s, 0:r.slot], r.src[e]).then_inc(rt_w[s], 16)

            for s in range(4):
                load(s, s)
            sp.wait_ge(rt_sent, 256 * (n + 1))
            for g in range(r.groups):
                sp.dma_start(slot_rows(g), r.sent[512 * g:512 * g + 512, :].rearrange("(n p) d -> p n d", p=128))\
                    .then_inc(rt_back[g], 16)
            for e in range(8):
                s = e % 4
                if e < 4:
                    sp.wait_ge(rt_y, 8 * r.n + e + 1)
                    load(e + 4, s)
                sp.wait_ge(rt_rows, 8 * r.n + e + 1)
                a = r.capacity * e
                full = r.capacity // 128
                sp.dma_start(r.made[a:a + 128 * full, :].rearrange("(n p) d -> p n d", p=128),
                             result(s)[:, 0:128 * full].rearrange("p (n d) -> p n d", d=D)).then_inc(rt_made[s], 16)
                if r.stores == 2:
                    m = r.tiles[-1]
                    sp.dma_start(r.made[a + 128 * full:a + r.capacity, :],
                                 result(s)[0:m, 128 * full:128 * full + 128]).then_inc(rt_made[s], 16)

        def result(s):
            return e[:, 512 * s:512 * s + 512]

        def stored(r, experts):
            return 32 * r.n + 16 * r.stores * experts

        def pool_routed(pool, r):
            if r.n == 0:
                pool.wait_ge(cleared, 64)
            pool.wait_ge(rt_slots, r.n + 1)
            for c in range(2 * T):
                pool.indirect_dma_start(r.sent, bass.IndirectOffsetOnAxis(ap=row_to[:, c:c + 1], axis=0),
                                        xn[:, c % T, :], None).then_inc(rt_sent, 16)
            for s in range(4):
                pool.wait_ge(rt_made[s], stored(r, 2))
            for g in range(4):
                for c in (2 * g, 2 * g + 1, T + 2 * g, T + 2 * g + 1):
                    pool.indirect_dma_start(et[:, 128 * c:128 * c + 128], None, r.made,
                                            bass.IndirectOffsetOnAxis(ap=row_from[:, c:c + 1], axis=0)).then_inc(rt_got[g], 16)

        def pe_routed(pe, r):
            n = r.n
            for g in range(r.groups):
                pe.wait_ge(rt_back[g], 16 * (n + 1) if g < 4 else 16)
                if g >= 2:
                    pe.wait_ge(rt_cols, 4 * n + g - 1)
                for i in range(4):
                    last = pe.transpose(bank(6 + g % 2)[:, 128 * i:128 * i + 128], slot_rows(g)[:, i, :], cst("ident"))
                last.then_inc(rt_turn, 1)
            pe.wait_ge(rt_cols, 4 * n + r.groups)

            def y(e, s):
                pe.wait_ge(rt_h, 32 * n + 4 * (e + 1))
                waitfrom(pe, rt_rows, 8 * n, e - 1)
                for i, m in enumerate(r.tiles):
                    for c in range(4):
                        a = 512 * (1 + r.gated) + 128 * c
                        last = mm(pe, bank(4 + s % 2)[0:m, 128 * i:128 * i + 128], hidden(s, c, r)[:, 128 * i:128 * i + m],
                                  slots[:, s, a:a + 128], start=(c == 0), stop=(c == 3))
                last.then_inc(rt_y, 1)

            def body(i):
                for s in range(4):
                    e = 4 * i + s
                    pe.wait_ge(rt_w[s], 32 * n + 16 * (i + 1))
                    cols = slot_cols[:, bass.ds(e * r.capacity, r.capacity)] if not isinstance(e, int) else \
                        slot_cols[:, e * r.capacity:(e + 1) * r.capacity]
                    for c in range(4):
                        if r.gated:
                            waitfrom(pe, rt_h, 32 * n, 4 * e + c - 1)
                            for part in range(2):
                                a = 512 * (1 - part) + 128 * c
                                last = mm(pe, bank(2 * (c % 2) + part)[:, 0:r.capacity], slots[:, s, a:a + 128], cols)
                        else:
                            waitfrom(pe, rt_h, 32 * n, 4 * e + c - 3)
                            last = mm(pe, bank(c)[:, 0:r.capacity], slots[:, s, 128 * c:128 * c + 128], cols)
                        last.then_inc(rt_up, 1)
                        if c == 1 and (s or not isinstance(i, int) or i > 0):
                            y(e - 1, (s - 1) % 4)
            peeled(pe, 2, body)
            y(7, 3)

        def act_routed(act, r):
            n = r.n
            for g in range(r.groups):
                act.wait_ge(rt_turn, 4 * n + g + 1)
                act.copy(slot_cols[:, 512 * g:512 * g + 512], bank(6 + g % 2)).then_inc(rt_cols, 1)

            def body(i):
                for s in range(4):
                    e = 4 * i + s
                    for c in range(4):
                        act.wait_ge(rt_up, 32 * n + 4 * e + c + 1)
                        if r.gated:
                            waitfrom(act, rt_h, 32 * n, 4 * e + c - 1)
                            act.activation(silus[:, c % 2, 0:r.capacity], bank(2 * (c % 2))[:, 0:r.capacity],
                                           ACT.Silu).then_inc(rt_silu, 1)
                        else:
                            if c == 0:
                                waitfrom(act, rt_y, 8 * n, e - 1)
                            act.activation(hidden(s, c, r), bank(c)[:, 0:r.capacity], ACT.Relu,
                                           bias=slots[:, s, 1024 + c:1025 + c]).then_inc(rt_h, 1)
            peeled(act, 2, body)

        def dve_slots(dve, r, pick, place):
            for j in range(2):
                dve.tensor_tensor(tmp[:, :, 8 * j:8 * j + 8], place[j], rows_of(cst(f"first_slot{r.n}")), ALU.add)
                dve.tensor_tensor(tmp[:, :, 16 + 8 * j:24 + 8 * j], pick[j], gates[:, :, 0:8], ALU.mult)
                dve.tensor_reduce(kept[:, T * j:T * j + T], pick[j], AX.X, ALU.add)
            dve.drain()
            for j in range(2):
                dve.tensor_tensor(tmp[:, :, 8 * j:8 * j + 8], tmp[:, :, 8 * j:8 * j + 8], pick[j], ALU.mult)
                dve.tensor_reduce(gcol[:, j, 0:T], tmp[:, :, 16 + 8 * j:24 + 8 * j], AX.X, ALU.add)
            dve.tensor_scalar(kept[:, :], kept[:, :], -1.0, 1.0, ALU.mult, ALU.add)
            dve.drain()
            for j in range(2):
                dve.tensor_reduce(slot_at[:, T * j:T * j + T], tmp[:, :, 8 * j:8 * j + 8], AX.X, ALU.add)
            dve.drain()
            dve.scalar_tensor_tensor(slot_at[:, :], kept[:, :], float(r.slots), slot_at[:, :], ALU.mult, ALU.add)
            dve.drain()
            dve.tensor_copy(row_from[:, :], slot_at[:, :])
            dve.tensor_tensor(kept[:, :], kept[:, :], cst("spare_row"), ALU.mult)
            dve.drain()
            dve.tensor_tensor(kept[:, :], kept[:, :], slot_at[:, :], ALU.add)
            dve.drain()
            dve.tensor_copy(row_to[:, :], kept[:, :]).then_inc(rt_slots, 1)

        def dve_routed(dve, r):
            n = r.n

            def rows_out(e, s, i):
                dve.wait_ge(rt_y, 8 * n + e + 1)
                if not isinstance(i, int) or i > 0:
                    dve.wait_ge(rt_made[s], stored(r, i))
                full = r.capacity // 128
                last = dve.tensor_copy(result(s)[:, 0:128 * full], bank(4 + s % 2)[:, 0:128 * full])
                if r.stores == 2:
                    m = r.tiles[-1]
                    last = dve.tensor_copy(result(s)[0:m, 128 * full:128 * full + 128],
                                           bank(4 + s % 2)[0:m, 128 * full:128 * full + 128])
                last.then_inc(rt_rows, 1)

            def body(i):
                for s in range(4):
                    e = 4 * i + s
                    if r.gated:
                        for c in range(4):
                            dve.wait_ge(rt_silu, 4 * e + c + 1)
                            if c == 0:
                                waitfrom(dve, rt_y, 8 * n, e - 1)
                            dve.tensor_tensor(hidden(s, c, r), silus[:, c % 2, 0:r.capacity],
                                              bank(2 * (c % 2) + 1)[:, 0:r.capacity], ALU.mult).then_inc(rt_h, 1)
                            if c == 2 and (s or not isinstance(i, int) or i > 0):
                                rows_out(e - 1, (s - 1) % 4, i if s else i - 1)
                    else:
                        rows_out(e, s, i)
            peeled(dve, 2, body)
            if r.gated:
                rows_out(7, 3, 1)
            dve.drain()
            for g in range(4):
                dve.wait_ge(rt_got[g], 64 * (n + 1))
                for j in range(2):
                    for t in (2 * g, 2 * g + 1):
                        c = T * j + t
                        last = dve.scalar_tensor_tensor(x[:, t, :], et[:, 128 * c:128 * c + 128], gcol[:, j, t:t + 1],
                                                        x[:, t, :], ALU.mult, ALU.add)
                    dve.drain()
            dve.nop().then_inc(x_done, 1)

        def pe_f0(pe, stage, m):
            pe_turn(pe, m, xn)
            pe_route(pe, m, stage, "l0f_wg", 8)
            pe.wait_ge(choice, 1)
            pe_prefix(pe, bank(6)[:, 0:16 * 8], picksb[:, :, :].rearrange("p t e -> p (t e)"), 2 * T).then_inc(counted, 1)
            pe.wait_ge(f0_b, 1)
            pe.transpose(bank(7)[0:64, 0:128], xi[:, 0, 0:64], cst("ident")).then_inc(f0_b, 1)
            pe.wait_ge(f0_b, 3)
            for t in range(T):
                last = mm(pe, bank(t // 4)[:, t % 4 * 128:t % 4 * 128 + 128], et[0:64, 0:128],
                          w("l0f_b2", 128 * t, 128)[0:64, :])
            last.then_inc(f0_b, 1)
            pe.wait_ge(f0_b, 5)
            pe_routed(pe, r0)

        def act_f0(act, m):
            act_turn(act, m)
            act_probs(act, 0, 8)
            act.wait_ge(f0_b, 2)
            act.copy(et[0:64, 0:128], bank(7)[0:64, 0:128]).then_inc(f0_b, 1)
            act_routed(act, r0)

        def dve_add_gated(dve, t, src, gate):
            return dve.scalar_tensor_tensor(x[:, t, :], src, gate, x[:, t, :], ALU.mult, ALU.add)

        def dve_f0(dve, norm):
            dve_norm(dve, norm, x, xn, 1e-5)
            dve_probs(dve, 0, 8)
            dve_best(dve, 8, 2, None)
            for j in range(2):
                last = dve.tensor_copy(picksb[:, T * j:T * j + T, :], picks[:, j, :, 0:8])
            last.then_inc(choice, 1)
            dve.wait_ge(counted, 1)
            place = bank(6)[:, 0:128].rearrange("p (t e) -> p t e", e=8)
            for j in range(2):
                dve.scalar_tensor_tensor(picks[:, j, :, 0:8], place[:, T * j:T * j + T, :], float(L0_CAPACITY),
                                         picks[:, j, :, 0:8], ALU.is_lt, ALU.mult)
            dve.drain()
            dve_gates(dve, 8, 2)
            dve_slots(dve, r0, [picks[:, j, :, 0:8] for j in range(2)], [place[:, T * j:T * j + T, :] for j in range(2)])
            dve.tensor_copy(xi[:, 0, 0:64].rearrange("p (t e) -> p t e", e=8), gates[:, :, 0:8]).then_inc(f0_b, 1)
            dve.wait_ge(f0_b, 4)
            dve.tensor_tensor(x[:, :, :], x[:, :, :], banks(0, 2, 128), ALU.add).then_inc(f0_b, 1)
            dve.drain()
            dve_routed(dve, r0)

        ha_in = sem("ha_in")
        ha_val = sem("ha_val")
        ha_score = sem("ha_score")
        ha_less = sem("ha_less")
        ha_exp = sem("ha_exp")
        ha_v = sem("ha_v")
        ha_turn = sem("ha_turn")
        ha_et = sem("ha_et")
        ha_av = sem("ha_av")
        ha_at = sem("ha_at")
        ha_out = sem("ha_out")
        USES = {3: "in score less exp v av at", 4: "in val score less av at", 7: "in val score less exp turn et av at",
                9: "in val score less exp turn et av at", 10: "in val score less exp turn et av at"}

        def base(name, stage, per=B):
            return per * sum(name in uses.split() for st, uses in USES.items() if st < stage)

        moving = big[:, 0:2048].rearrange("p (a c) -> p a c", a=2)
        less = big[:, 2048:4096].rearrange("p (a c) -> p a c", a=2)
        exps = e[:, :].rearrange("p (a c) -> p a c", a=2)
        still = work[:, 0:512].rearrange("p (a c) -> p a c", a=2)
        values = work[:, 512:1024].rearrange("p (a c) -> p a c", a=2)
        scratch = work[:, 1024:2048].rearrange("p (a c) -> p a c", a=2)
        exps_t = et[:, :].rearrange("p (a c) -> p a c", a=2)
        SCALE = float(HD) ** -0.5

        def rounds(eng, step, lags):
            def body(i):
                for s in range(2):
                    step(2 * i + s, s)
            peeled(eng, B // 2, body, 2)
            for b in range(B, B + lags):
                step(b, b % 2)

        def has(b, lag):
            return not isinstance(b, int) or 0 <= b - lag < B

        def seq(ap, b, n):
            return ap[:, bass.ds(b * n, n)] if not isinstance(b, int) else ap[:, b * n:b * n + n]

        def pe_out_heads(pe, stage, wname, wo_banks):
            pe.wait_ge(ha_at, base("at", stage) + B)
            for t in range(T):
                last = mm(pe, bank(wo_banks + t // 4)[:, t % 4 * 128:t % 4 * 128 + 128], at[:, 128 * t:128 * t + 128],
                          w(wname))
            last.then_inc(ha_out, 1)

        def dve_out_heads(dve, stage, brow):
            dve.wait_ge(ha_out, base("at", stage, 1) + 1)
            dve.tensor_tensor(x[:, :, :], x[:, :, :], banks(0, 2, 128), ALU.add)
            dve.drain()
            if brow:
                dve.tensor_tensor(x[:, :, :], x[:, :, :], rows_of(row(brow)), ALU.add)
                dve.drain()
            dve.nop().then_inc(x_done, 1)

        def dve_pick_heads(dve, src, dst, parts):
            for n in range(parts):
                dve.tensor_tensor(scratch[:, 0, 256 * n:256 * n + 256].rearrange("p (j l) -> p j l", l=L),
                                  src[:, 256 * n:256 * n + 256].rearrange("p (j l) -> p j l", l=L),
                                  cst("head_of_four").unsqueeze(2).to_broadcast([128, 4, L]), ALU.mult)
            dve.drain()
            for n in range(parts):
                last = dve.tensor_reduce(dst[n], scratch[:, 0, 256 * n:256 * n + 256].rearrange("p (j l) -> p l j", l=L),
                                         AX.X, ALU.add)
            return last


        def pool_l1x(pool):
            st = 3
            pool.wait_ge(q_ready, 2 * 1 + 2)
            pool.wait_ge(k_ready, 4 * 1 + 4)

            def step(b, s):
                waitfrom(pool, ha_score, base("score", st), b - 1)
                pool.tensor_tensor(moving[:, s, :].rearrange("p (h l) -> p h l", l=L),
                                   seq(q, b, L).unsqueeze(1).to_broadcast([128, H, L]),
                                   cst("head").unsqueeze(2).to_broadcast([128, H, L]), ALU.mult)
                pool.tensor_copy(still[:, s, 0:128], seq(k, b, S)).then_inc(ha_in, 1)
            rounds(pool, step, 0)

        def pe_l1x(pe, stage, m):
            st = 3
            pe_project(pe, 1, stage, m)
            pe.wait_ge(v_ready, 4)
            pe.wait_ge(q_ready, 4)

            def step(b, s):
                if has(b, 0):
                    pe.wait_ge(ha_in, base("in", st) + b + 1)
                    waitfrom(pe, ha_less, base("less", st), b - 1)
                    for h in range(2):
                        last = mm(pe, bank(2 * s + h), still[:, s, 0:128], moving[:, s, 512 * h:512 * h + 512])
                    last.then_inc(ha_score, 1)
                if has(b, 2):
                    pe.wait_ge(ha_v, base("v", st) + b - 1)
                    waitfrom(pe, ha_at, base("at", st), b - 3)
                    for g in range(4):
                        last = mm(pe, bank(4 + s)[32 * g:32 * g + 32, 0:256], values[:, s, 32 * g:32 * g + 32],
                                  exps[:, s, 256 * g:256 * g + 256])
                    last.then_inc(ha_av, 1)
            rounds(pe, step, 2)
            pe_out_heads(pe, stage, "l1x_wo", 0)

        def act_l1x(act, m):
            st = 3
            act_project(act, 1, m)

            def step(b, s):
                act.wait_ge(ha_less, base("less", st) + b + 1)
                waitfrom(act, ha_av, base("av", st), b - 1)
                act.activation(exps[:, s, :], less[:, s, :], ACT.Exp, scale=SCALE).then_inc(ha_exp, 1)
            rounds(act, step, 0)

        def dve_l1x(dve, norm):
            st = 3
            dve_norm(dve, norm, x, xn, 1e-5)
            dve_values(dve, 1)

            def step(b, s):
                top, total, z = small[:, s, :], small[:, 2 + s, :], 1 - s
                if has(b, 0):
                    dve.wait_ge(ha_score, base("score", st) + b + 1)
                    sc = banks(2 * s, 2, L)
                    dve.tensor_reduce(top, sc, AX.X, ALU.max)
                    dve.drain()
                    waitfrom(dve, ha_exp, base("exp", st), b - 1)
                    dve.tensor_tensor(less[:, s, :].rearrange("p (h l) -> p h l", l=L), sc,
                                      top.unsqueeze(2).to_broadcast([128, H, L]), ALU.subtract).then_inc(ha_less, 1)
                if has(b, 1):
                    total = small[:, 2 + z, :]
                    dve.wait_ge(ha_exp, base("exp", st) + b)
                    dve.tensor_reduce(total, exps[:, z, :].rearrange("p (h l) -> p h l", l=L), AX.X, ALU.add)
                    dve.drain()
                    dve.reciprocal(total, total)
                    dve.drain()
                    waitfrom(dve, ha_av, base("av", st), b - 2)
                    vb = seq(v[:, :, :].rearrange("p b c -> p (b c)"), b - 1, D)
                    dve.tensor_tensor(values[:, z, 0:128].rearrange("p (h d) -> p h d", d=HD),
                                      vb.rearrange("p (h d) -> p h d", d=HD),
                                      total.unsqueeze(2).to_broadcast([128, H, HD]), ALU.mult).then_inc(ha_v, 1)
                if has(b, 2):
                    dve.drain()
                    dve.wait_ge(ha_av, base("av", st) + b - 1)
                    dve_pick_heads(dve, bank(4 + s), [seq(at, b - 2, L)], 1).then_inc(ha_at, 1)
            rounds(dve, step, 2)
            dve_out_heads(dve, 3, "l1x_bo")


        def pool_l3x(pool):
            st = 9
            pool.wait_ge(q_ready, 2 * 3 + 2)
            pool.wait_ge(k_ready, 4 * 3 + 4)
            pool.wait_ge(v_ready, 12)

            def step(b, s):
                if has(b, 0):
                    waitfrom(pool, ha_score, base("score", st), b - 1)
                    pool.tensor_tensor(moving[:, s, :].rearrange("p (i c) -> p i c", c=S),
                                       seq(k, b, S).unsqueeze(1).to_broadcast([128, 8, S]),
                                       cst("head_pair").unsqueeze(2).to_broadcast([128, 8, S]), ALU.mult)
                    pool.tensor_tensor(still[:, s, 0:128].rearrange("p (j l) -> p j l", l=L),
                                       seq(q, b, L).unsqueeze(1).to_broadcast([128, 2, L]),
                                       cst("head_parity").unsqueeze(2).to_broadcast([128, 2, L]), ALU.mult).then_inc(ha_in, 1)
                if has(b, 2):
                    waitfrom(pool, ha_av, base("av", st), b - 3)
                    pool.tensor_copy(values[:, s, 0:128],
                                     seq(v[:, :, :].rearrange("p b c -> p (b c)"), b - 2, D)).then_inc(ha_val, 1)
            rounds(pool, step, 2)

        def pe_l3x(pe, stage, m):
            st = 9
            pe_project(pe, 3, stage, m)
            pe.wait_ge(v_ready, 12)
            pe.wait_ge(q_ready, 8)

            def step(b, s):
                z = 1 - s
                if has(b, 0):
                    pe.wait_ge(ha_in, base("in", st) + b + 1)
                    waitfrom(pe, ha_less, base("less", st), b - 1)
                    for h in range(2):
                        last = mm(pe, bank(2 * s + h), still[:, s, 0:128], moving[:, s, 512 * h:512 * h + 512])
                    last.then_inc(ha_score, 1)
                if has(b, 2):
                    pe.wait_ge(ha_exp, base("exp", st) + b - 1)
                    waitfrom(pe, ha_et, base("et", st), b - 2)
                    for i in range(8):
                        last = pe.transpose(bank(4 + i // 4)[:, i % 4 * 128:i % 4 * 128 + 128],
                                            exps[:, s, 128 * i:128 * i + 128], cst("ident"))
                    last.then_inc(ha_turn, 1)
                if has(b, 3):
                    pe.wait_ge(ha_et, base("et", st) + b - 2)
                    pe.wait_ge(ha_val, base("val", st) + b - 2)
                    waitfrom(pe, ha_at, base("at", st), b - 4)
                    for g in range(4):
                        o = bank(6 + z)[32 * g:32 * g + 32, :]
                        mm(pe, o[:, 0:256], values[:, z, 32 * g:32 * g + 32], exps_t[:, z, 256 * g:256 * g + 256])
                        last = mm(pe, o[:, 256:512], cst("ones")[:, 0:32], exps_t[:, z, 256 * g:256 * g + 256])
                    last.then_inc(ha_av, 1)
            rounds(pe, step, 3)
            pe_out_heads(pe, stage, "l3x_wo", 0)

        def act_l3x(act, m):
            st = 9
            act_project(act, 3, m)

            def step(b, s):
                if has(b, 0):
                    act.wait_ge(ha_less, base("less", st) + b + 1)
                    waitfrom(act, ha_turn, base("turn", st), b - 1)
                    act.activation(exps[:, s, :], less[:, s, :], ACT.Exp, scale=SCALE).then_inc(ha_exp, 1)
                if has(b, 2):
                    act.wait_ge(ha_turn, base("turn", st) + b - 1)
                    waitfrom(act, ha_av, base("av", st), b - 3)
                    act.copy(exps_t[:, s, :], ps[:, 4:6, :].rearrange("p b c -> p (b c)")).then_inc(ha_et, 1)
            rounds(act, step, 2)

        def dve_l3x(dve, norm):
            st = 9
            dve_norm(dve, norm, x, xn, 1e-5)
            dve_values(dve, 3)

            def step(b, s):
                top = small[:, s, 0:8]
                if has(b, 0):
                    dve.wait_ge(ha_score, base("score", st) + b + 1)
                    sc = banks(2 * s, 2, S)
                    dve.tensor_reduce(top, sc, AX.X, ALU.max)
                    dve.drain()
                    waitfrom(dve, ha_exp, base("exp", st), b - 1)
                    dve.tensor_tensor(less[:, s, :].rearrange("p (i c) -> p i c", c=S), sc,
                                      top.unsqueeze(2).to_broadcast([128, 8, S]), ALU.subtract).then_inc(ha_less, 1)
                if has(b, 3):
                    dve.drain()
                    dve.wait_ge(ha_av, base("av", st) + b - 2)
                    dve_pick_heads(dve, bank(7 - s), [scratch[:, 1, 0:64], scratch[:, 1, 64:128]], 2)
                    dve.drain()
                    dve.reciprocal(scratch[:, 1, 128:192], scratch[:, 1, 64:128])
                    dve.drain()
                    dve.tensor_tensor(seq(at, b - 3, L), scratch[:, 1, 0:64], scratch[:, 1, 128:192],
                                      ALU.mult).then_inc(ha_at, 1)
            rounds(dve, step, 3)
            dve_out_heads(dve, 9, "l3x_bo")

        sa_dup = sem("sa_dup")
        sa_v = sem("sa_v")
        sa_vb = sem("sa_vb")
        sa_proj = sem("sa_proj")
        sa_rot = sem("sa_rot")
        SELF = {7: ("l2a", "rope2", True), 10: ("l3a", "rope3", False)}

        def act_duplicate(act, m, dst):
            for h in range(2):
                act.wait_ge(turned, 2 * m + h + 1)
                act.copy(xnt[:, 512 * h:512 * h + 512], bank(6 + h)).then_inc(xnt_ready, 1)
                act.activation(dst[:, 1024 * h:1024 * h + 1024].rearrange("p (b r l) -> p b r l", r=2, l=L),
                               bank(6 + h).rearrange("p (b l) -> p b l", l=L).unsqueeze(2).to_broadcast([128, 8, 2, L]),
                               ACT.Copy).then_inc(sa_dup, 1)

        def pe_self_values(pe, n, src, wname):
            for b in range(B):
                if b % 8 == 0:
                    pe.wait_ge(sa_dup, 2 * n + b // 8 + 1)
                last = mm(pe, bank(b // 4)[:, b % 4 * 128:b % 4 * 128 + 128], src[:, 128 * b:128 * b + 128], w(wname))
            last.then_inc(sa_v, 1)

        def pool_values(pool, b, s, mask):
            pool.tensor_tensor(values[:, s, :].rearrange("p (c g d) -> p c g d", c=2, g=4),
                               seq(v[:, :, :].rearrange("p b c -> p (b c)"), b, D)
                               .rearrange("p (g d) -> p g d", g=4).unsqueeze(1).to_broadcast([128, 2, 4, 32]),
                               cst(mask).rearrange("p (c d) -> p c d", c=2).unsqueeze(2).to_broadcast([128, 2, 4, 32]),
                               ALU.mult).then_inc(ha_val, 1)

        def pool_self(pool, st):
            n = {7: 1, 10: 2}[st]
            pool.wait_ge(sa_rot, 4 * n)
            pool.wait_ge(sa_vb, n + 1)

            def step(b, s):
                if has(b, 0):
                    waitfrom(pool, ha_score, base("score", st), b - 1)
                    pool.tensor_tensor(moving[:, s, 0:512].rearrange("p (i c) -> p i c", c=L),
                                       seq(k, b, L).unsqueeze(1).to_broadcast([128, 8, L]),
                                       cst("head_pair").unsqueeze(2).to_broadcast([128, 8, L]), ALU.mult)
                    pool.tensor_tensor(still[:, s, 0:128].rearrange("p (j l) -> p j l", l=L),
                                       seq(q, b, L).unsqueeze(1).to_broadcast([128, 2, L]),
                                       cst("head_parity").unsqueeze(2).to_broadcast([128, 2, L]), ALU.mult).then_inc(ha_in, 1)
                if has(b, 2):
                    waitfrom(pool, ha_av, base("av", st), b - 3)
                    pool_values(pool, b - 2, s, "value_soft")
            rounds(pool, step, 2)

        def pe_self(pe, st, m):
            name, _, _ = SELF[st]
            n = {7: 1, 10: 2}[st]
            pe_turn(pe, m, xn)
            pe.wait_ge(w_loaded[st], 16)
            pe_self_values(pe, n, e, name + "_wv")
            pe.wait_ge(sa_vb, n + 1)
            for h in range(2):
                pe.wait_ge(xnt_ready, 2 * m + h + 1)
                for j, part in enumerate(("_wq", "_wqr", "_wk", "_wkr")):
                    last = mm(pe, bank(4 * h + j), w(name + part), xnt[:, 512 * h:512 * h + 512])
                last.then_inc(sa_proj, 1)
            pe.wait_ge(sa_rot, 4 * n)

            def step(b, s):
                z = 1 - s
                if has(b, 0):
                    pe.wait_ge(ha_in, base("in", st) + b + 1)
                    waitfrom(pe, ha_less, base("less", st), b - 1)
                    mm(pe, bank(s), still[:, s, 0:128], moving[:, s, 0:512], start=True, stop=False)
                    mm(pe, bank(s), cstb("identb"), cstb("causal"), start=False, stop=True).then_inc(ha_score, 1)
                if has(b, 2):
                    pe.wait_ge(ha_exp, base("exp", st) + b - 1)
                    waitfrom(pe, ha_et, base("et", st), b - 3)
                    for g in range(4):
                        last = pe.transpose(bank(2 + s)[:, 128 * g:128 * g + 128], exps[:, s, 128 * g:128 * g + 128],
                                            cst("ident"))
                    last.then_inc(ha_turn, 1)
                if has(b, 3):
                    pe.wait_ge(ha_et, base("et", st) + b - 2)
                    pe.wait_ge(ha_val, base("val", st) + b - 2)
                    waitfrom(pe, ha_at, base("at", st), b - 4)
                    for g in range(4):
                        for j in range(2):
                            mm(pe, bank(4 + z)[32 * g:32 * g + 32, 0:64], values[:, z, 128 * j + 32 * g:128 * j + 32 * g + 32],
                               exps_t[:, z, 128 * g + 64 * j:128 * g + 64 * j + 64], start=(j == 0), stop=(j == 1))
                        for j in range(2):
                            last = mm(pe, bank(4 + z)[32 * g:32 * g + 32, 64:128], cst("value_soft")[:, 32 * j:32 * j + 32],
                                      exps_t[:, z, 128 * g + 64 * j:128 * g + 64 * j + 64], start=(j == 0), stop=(j == 1))
                    last.then_inc(ha_av, 1)
            rounds(pe, step, 3)
            pe_out_heads(pe, st, name + "_wo", 0)

        def act_self(act, st, m):
            act_duplicate(act, m, e)

            def step(b, s):
                if has(b, 0):
                    act.wait_ge(ha_less, base("less", st) + b + 1)
                    waitfrom(act, ha_turn, base("turn", st), b - 1)
                    act.activation(exps[:, s, 0:512], less[:, s, 0:512], ACT.Exp, scale=SCALE).then_inc(ha_exp, 1)
                if has(b, 2):
                    act.wait_ge(ha_turn, base("turn", st) + b - 1)
                    waitfrom(act, ha_av, base("av", st), b - 3)
                    act.copy(exps_t[:, s, 0:512], bank(2 + s)).then_inc(ha_et, 1)
            rounds(act, step, 2)

        def dve_self(dve, st, norm):
            name, rope, biased = SELF[st]
            n = {7: 1, 10: 2}[st]
            dve_norm(dve, norm, x, xn, 1e-5)
            dve.wait_ge(sa_v, n + 1)
            if biased:
                dve.tensor_tensor(v[:, :, :], banks(0, 4, 128), rows_of(row(name + "_bv"), B), ALU.add).then_inc(sa_vb, 1)
            else:
                dve.tensor_copy(v[:, :, :], banks(0, 4, 128)).then_inc(sa_vb, 1)
            for h in range(2):
                dve.wait_ge(sa_proj, 2 * (n - 1) + h + 1)
                for j, (dst, bq) in enumerate(((q, "_bq"), (k, "_bk"))):
                    turn = scratch[:, j, :].rearrange("p (b l) -> p b l", l=L)
                    out = dst[:, 512 * h:512 * h + 512].rearrange("p (b l) -> p b l", l=L)
                    for o, bk, tab, sfx in ((out, 4 * h + 2 * j, "_cos", ""), (turn, 4 * h + 2 * j + 1, "_sin", "r")):
                        table = cst(rope + tab).unsqueeze(1).to_broadcast([128, 8, L])
                        src = bank(bk).rearrange("p (b l) -> p b l", l=L)
                        if biased:
                            dve.scalar_tensor_tensor(o, src, bias(name + bq + sfx), table, ALU.add, ALU.mult)
                        else:
                            dve.tensor_tensor(o, src, table, ALU.mult)
                dve.drain()
                for j, dst in enumerate((q, k)):
                    dve.tensor_tensor(dst[:, 512 * h:512 * h + 512], dst[:, 512 * h:512 * h + 512], scratch[:, j, :],
                                      ALU.add).then_inc(sa_rot, 1)
                dve.drain()

            def step(b, s):
                top = small[:, s, 0:8]
                if has(b, 0):
                    dve.wait_ge(ha_score, base("score", st) + b + 1)
                    sc = banks(s, 1, L)
                    dve.tensor_reduce(top, sc, AX.X, ALU.max)
                    dve.drain()
                    waitfrom(dve, ha_exp, base("exp", st), b - 1)
                    dve.tensor_tensor(less[:, s, 0:512].rearrange("p (i c) -> p i c", c=L), sc,
                                      top.unsqueeze(2).to_broadcast([128, 8, L]), ALU.subtract).then_inc(ha_less, 1)
                if has(b, 3):
                    dve.wait_ge(ha_av, base("av", st) + b - 2)
                    dve.reciprocal(scratch[:, s, 0:64], bank(5 - s)[:, 64:128])
                    dve.drain()
                    dve.tensor_tensor(seq(at, b - 3, L), bank(5 - s)[:, 0:64], scratch[:, s, 0:64],
                                      ALU.mult).then_inc(ha_at, 1)
            rounds(dve, step, 3)
            dve_out_heads(dve, st, name + "_bo" if biased else None)

        wv_proj = sem("wv_proj")
        wv_arg = sem("wv_arg")
        wv_near = sem("wv_near")
        wv_frac = sem("wv_frac")
        wv_sin = sem("wv_sin")
        wv_sum = sem("wv_sum")
        wv_norm = sem("wv_norm")
        wv_unit = sem("wv_unit")
        wf_up = sem("wf_up")
        wf_arg = sem("wf_arg")
        wf_near = sem("wf_near")
        wf_frac = sem("wf_frac")
        wf_sin = sem("wf_sin")
        wf_h = sem("wf_h")
        wf_gelu = sem("wf_gelu")
        wf_out = sem("wf_out")
        MAGIC = 1.5 * 2.0 ** 23
        TURNS = float(np.float32(1.0 / (2.0 * np.pi)))
        ANGLE = float(np.float32(6.283185))
        waves = slots[:, :, :].rearrange("p a b -> p (a b)")[:, 0:4096].rearrange("p (c n) -> p c n", c=4)
        bigc = big[:, :].rearrange("p (c n) -> p c n", c=4)
        workc = work[:, :].rearrange("p (c n) -> p c n", c=4)

        def wholes(c):
            return (e if c < 2 else et)[:, 1024 * (c % 2):1024 * (c % 2) + 1024]

        def two(i):
            return ps[:, i:i + 2, :].rearrange("p b c -> p (b c)")

        def pool_wave(pool):
            st = 4
            pool.wait_ge(wv_unit, 4)
            pool.wait_ge(sa_vb, 1)

            def step(b, s):
                if has(b, 0):
                    waitfrom(pool, ha_score, base("score", st), b - 1)
                    for hf in range(2):
                        pool.tensor_tensor(moving[:, s, 256 * hf:256 * hf + 256].rearrange("p (i t) -> p i t", t=L),
                                           seq(waves[:, hf, :], b, L).unsqueeze(1).to_broadcast([128, 4, L]),
                                           cst("wave_pair").unsqueeze(2).to_broadcast([128, 4, L]), ALU.mult)
                        last = pool.tensor_tensor(still[:, s, 128 * hf:128 * hf + 128].rearrange("p (j t) -> p j t", t=L),
                                           seq(waves[:, 2 + hf, :], b, L).unsqueeze(1).to_broadcast([128, 2, L]),
                                           cst("wave_parity").unsqueeze(2).to_broadcast([128, 2, L]),
                                           ALU.mult)
                    last.then_inc(ha_in, 1)
                if has(b, 1):
                    waitfrom(pool, ha_av, base("av", st), b - 2)
                    pool_values(pool, b - 1, 1 - s, "value_wave")
            rounds(pool, step, 1)

        def pe_wave(pe, stage, m):
            st = 4
            pe_turn(pe, m, xn)
            pe.wait_ge(w_loaded[stage], 16)
            pe_self_values(pe, 0, k, "l1a_wv")
            for c in range(4):
                a = 0 if c % 2 else 4
                if c == 0:
                    pe.wait_ge(xnt_ready, 2 * m + 2)
                    pe.wait_ge(sa_dup, 2)
                if c == 1:
                    pe.wait_ge(sa_vb, 1)
                if c >= 2:
                    pe.wait_ge(wv_arg, c - 1)
                for j, part in enumerate(("f", "p")):
                    name = "l1a_w" + "qk"[c // 2] + part
                    for h in range(2):
                        last = mm(pe, bank(a + 2 * j + h), w(name, 128 * (c % 2), 128), xnt[:, 512 * h:512 * h + 512])
                last.then_inc(wv_proj, 1)
            for c in range(4):
                pe.wait_ge(wv_sin, c + 1)
                if c == 0:
                    pe.wait_ge(wv_arg, 4)
                for h in range(2):
                    last = mm(pe, bank(2 * c + h), cst("same_wave_head"), bigc[:, c, 512 * h:512 * h + 512])
                last.then_inc(wv_sum, 1)
            pe.wait_ge(wv_norm, 4)

            def step(b, s):
                if has(b, 0):
                    pe.wait_ge(ha_in, base("in", st) + b + 1)
                    waitfrom(pe, ha_less, base("less", st), b - 1)
                    for hf in range(2):
                        last = mm(pe, bank(s)[:, 256 * hf:256 * hf + 256], still[:, s, 128 * hf:128 * hf + 128],
                                  moving[:, s, 256 * hf:256 * hf + 256])
                    last.then_inc(ha_score, 1)
                if has(b, 2):
                    pe.wait_ge(ha_less, base("less", st) + b - 1)
                    pe.wait_ge(ha_val, base("val", st) + b - 1)
                    waitfrom(pe, ha_at, base("at", st), b - 3)
                    for g in range(4):
                        for c in range(2):
                            i = 2 * g + c
                            last = mm(pe, bank(4 + s)[32 * g:32 * g + 32, 0:64],
                                      values[:, s, 128 * c + 32 * g:128 * c + 32 * g + 32],
                                      exps_t[:, s, 64 * i:64 * i + 64], start=(c == 0), stop=(c == 1))
                    last.then_inc(ha_av, 1)
            rounds(pe, step, 2)
            pe_out_heads(pe, st, "l1a_wo", 2)
            pe_turn(pe, m + 1, xn)
            for c in range(4):
                for h in range(2):
                    if c == 0:
                        pe.wait_ge(xnt_ready, 2 * m + 2 + h + 1)
                    last = mm(pe, bank(2 * c + h), w("l1a_w1", 128 * c, 128), xnt[:, 512 * h:512 * h + 512])
                last.then_inc(wf_up, 1)
            pe.wait_ge(wf_h, 4)
            for t in range(T):
                for c in range(4):
                    last = mm(pe, bank(t // 4)[:, t % 4 * 128:t % 4 * 128 + 128], bigc[:, c, 128 * t:128 * t + 128],
                              w("l1a_w2", 128 * c, 128), start=(c == 0), stop=(c == 3))
            last.then_inc(wf_out, 1)

        def act_wave(act, m):
            st = 4
            act_duplicate(act, m, k)
            for c in range(4):
                act.wait_ge(wv_arg, c + 1)
                act.activation(workc[:, c, :], bigc[:, c, :], ACT.Identity, scale=TURNS)
                act.activation(wholes(c), bigc[:, c, :], ACT.Copy, scale=TURNS, bias=MAGIC).then_inc(wv_near, 1)
            for c in range(4):
                act.wait_ge(wv_frac, c + 1)
                act.activation(waves[:, c, :], waves[:, c, :], ACT.Sin, scale=-ANGLE)
                act.drain()
                act.square(bigc[:, c, :], waves[:, c, :]).then_inc(wv_sin, 1)
            for c in range(4):
                act.wait_ge(wv_sum, c + 1)
                act.sqrt(workc[:, c, :], two(2 * c)).then_inc(wv_norm, 1)

            def step(b, s):
                act.wait_ge(ha_av, base("av", st) + b + 1)
                act.copy(seq(at, b, L), bank(4 + s)[:, 0:64]).then_inc(ha_at, 1)
            rounds(act, step, 0)
            act_turn(act, m + 1)
            for c in range(4):
                act.wait_ge(wf_up, c + 1)
                act.activation(bigc[:, c, :], two(2 * c), ACT.Gelu, bias=bias("l1a_b1", c)).then_inc(wf_gelu, 1)
            for c in range(4):
                act.wait_ge(wf_arg, c + 1)
                act.activation(waves[:, c, :], workc[:, c, :], ACT.Identity, scale=TURNS)
                act.activation(wholes(c), workc[:, c, :], ACT.Copy, scale=TURNS, bias=MAGIC).then_inc(wf_near, 1)
            for c in range(4):
                act.wait_ge(wf_frac, c + 1)
                act.activation(waves[:, c, :], waves[:, c, :], ACT.Sin, scale=-ANGLE).then_inc(wf_sin, 1)

        def dve_fraction(dve, near, turns, c, out_sem):
            dve.scalar_tensor_tensor(waves[:, c, :], near, MAGIC, turns, ALU.subtract, ALU.subtract)
            dve.drain()
            dve.tensor_scalar(waves[:, c, :], waves[:, c, :], -0.5, 0.5, ALU.max, ALU.min).then_inc(out_sem, 1)

        def dve_wave(dve, norm):
            st = 4
            dve_norm(dve, norm, x, xi, 1e-5, publish=False)
            dve.drain()
            dve_norm(dve, norm + 1, xi, xn, 1e-5, row("l1a_g1"), row("l1a_be1"))
            dve.wait_ge(sa_v, 1)
            dve.tensor_tensor(v[:, :, :], banks(0, 4, 128), rows_of(row("l1a_bv"), B), ALU.add).then_inc(sa_vb, 0 + 1)
            dve.drain()
            dve.tensor_tensor(v[:, :, :].rearrange("p b (h d) -> p b h d", d=HD),
                              v[:, :, :].rearrange("p b (h d) -> p b h d", d=HD),
                              row("l1a_iscale").unsqueeze(2).unsqueeze(1).to_broadcast([128, B, H, HD]), ALU.mult)
            for c in range(4):
                a = 0 if c % 2 else 4
                dve.wait_ge(wv_proj, c + 1)
                name = "l1a_b" + "qk"[c // 2]
                dve.scalar_tensor_tensor(bigc[:, c, :].rearrange("p (b l) -> p b l", l=L),
                                         two(a).rearrange("p (b l) -> p b l", l=L), bias(name + "f", c % 2),
                                         cst("position").unsqueeze(1).to_broadcast([128, B, L]), ALU.add, ALU.mult)
                dve.drain()
                dve.scalar_tensor_tensor(bigc[:, c, :], two(a + 2), bias(name + "p", c % 2), bigc[:, c, :],
                                         ALU.add, ALU.add).then_inc(wv_arg, 1)
            for c in range(4):
                dve.wait_ge(wv_near, c + 1)
                dve_fraction(dve, wholes(c), workc[:, c, :], c, wv_frac)
            for c in range(4):
                dve.wait_ge(wv_norm, c + 1)
                dve.tensor_scalar(workc[:, c, :], workc[:, c, :], 1e-12, None, ALU.max)
                dve.drain()
                dve.reciprocal(workc[:, c, :], workc[:, c, :])
                dve.drain()
                dve.tensor_tensor(waves[:, c, :], waves[:, c, :], workc[:, c, :], ALU.mult).then_inc(wv_unit, 1)

            def step(b, s):
                dve.wait_ge(ha_score, base("score", st) + b + 1)
                waitfrom(dve, ha_av, base("av", st), b - 1)
                dve.tensor_tensor(exps_t[:, s, 0:512].rearrange("p (i t) -> p i t", t=L), banks(s, 1, L),
                                  cst("wave_causal").unsqueeze(1).to_broadcast([128, 8, L]), ALU.mult).then_inc(ha_less, 1)
            rounds(dve, step, 0)
            dve.wait_ge(ha_out, base("at", st, 1) + 1)
            dve.tensor_tensor(xi[:, :, :], xi[:, :, :], banks(2, 2, 128), ALU.add)
            dve.drain()
            dve.tensor_tensor(xi[:, :, :], xi[:, :, :], rows_of(row("l1a_bo")), ALU.add)
            dve.drain()
            dve_norm(dve, norm + 2, xi, xn, 1e-5, row("l1a_g2"), row("l1a_be2"))
            for c in range(4):
                dve.wait_ge(wf_up, c + 1)
                dve.wait_ge(wf_gelu, c + 1)
                dve.tensor_scalar(workc[:, c, :], two(2 * c), bias("l1a_b1", c), None, ALU.add).then_inc(wf_arg, 1)
            for c in range(4):
                dve.wait_ge(wf_near, c + 1)
                dve_fraction(dve, wholes(c), waves[:, c, :], c, wf_frac)
            for c in range(4):
                dve.wait_ge(wf_sin, c + 1)
                dve.scalar_tensor_tensor(bigc[:, c, :], waves[:, c, :], 0.1, bigc[:, c, :], ALU.mult, ALU.add)\
                   .then_inc(wf_h, 1)
            dve.wait_ge(wf_out, 1)
            dve.tensor_tensor(xi[:, :, :], xi[:, :, :], banks(0, 2, 128), ALU.add)
            dve.drain()
            dve.tensor_tensor(xi[:, :, :], xi[:, :, :], rows_of(row("l1a_b2")), ALU.add)
            dve.drain()
            dve.tensor_tensor(x[:, :, :], x[:, :, :], xi[:, :, :], ALU.add).then_inc(x_done, 1)
            dve.drain()

        class Gated:

            def __init__(self, name, src, experts, chunks, slot, per, wide, slots_n):
                self.src, self.experts, self.chunks, self.slot, self.wide = src, experts, chunks, slot, wide
                self.per = per
                self.y_banks = 2 if wide > 128 else 1
                self.w = [sem(f"{name}_w{i}") for i in range(per)]
                self.up = sem(name + "_up")
                self.silu = sem(name + "_silu")
                self.h = sem(name + "_h")
                self.y = sem(name + "_y")
                self.acc = sem(name + "_acc")

        f2 = Gated("f2", l2f, L2F_EXPERTS, 1, L2F_SLOT, 4, 128, 4)
        f3 = Gated("f3", l3f, L3F_PAIRS, 1, L3F_SLOT, 4, 256, 4)

        def units(eng, f, step):
            n = 2 * f.per

            def body(i):
                for s in range(n):
                    step(n * i + s, s, i)
            rounds_n = f.experts // f.per
            peeled(eng, rounds_n, body)
            for u in range(rounds_n * n, 2 * f.experts + 1):
                step(u, u % n, rounds_n)

        def exists(f, u):
            return not isinstance(u, int) or 0 <= u < 2 * f.experts

        def pe_gated(pe, f):
            n = 2 * f.per

            def y(u, s):
                pe.wait_ge(f.h, f.chunks * (u + 1))
                waitfrom(pe, f.acc, 0, u - 1)
                yb = 4 + f.y_banks * (s % 2)
                per_bank = 512 // f.wide
                for t in range(4):
                    for c in range(f.chunks):
                        a = 256 * f.chunks + 128 * c
                        last = mm(pe, bank(yb + t // per_bank)[:, t % per_bank * f.wide:t % per_bank * f.wide + f.wide],
                                  h_at(s % 2, c)[:, 128 * t:128 * t + 128], slots[:, s // 2, a:a + f.wide],
                                  start=(c == 0), stop=(c == f.chunks - 1))
                last.then_inc(f.y, 1)

            def step(u, s, i):
                if exists(f, u):
                    if s % 2 == 0:
                        pe.wait_ge(f.w[s // 2], 16 * (i + 1))
                    for c in range(f.chunks):
                        kk = f.chunks * u + c
                        z = (f.chunks * s + c) % 2
                        waitfrom(pe, f.h, 0, kk - 1)
                        for part in range(2):
                            a = 128 * f.chunks * (1 - part) + 128 * c
                            last = mm(pe, bank(2 * z + part), slots[:, s // 2, a:a + 128],
                                      xnt[:, 512 * (s % 2):512 * (s % 2) + 512])
                        last.then_inc(f.up, 1)
                        if c == 0 and exists(f, u - 1):
                            y(u - 1, (s - 1) % n)
                else:
                    y(u - 1, (s - 1) % n)
            units(pe, f, step)

        def act_gated(act, f):
            def step(u, s, i):
                if exists(f, u):
                    for c in range(f.chunks):
                        kk = f.chunks * u + c
                        z = (f.chunks * s + c) % 2
                        act.wait_ge(f.up, kk + 1)
                        waitfrom(act, f.h, 0, kk - 1)
                        act.activation(silus[:, z, :], bank(2 * z), ACT.Silu).then_inc(f.silu, 1)
            units(act, f, step)

        def dve_gated(dve, f):
            n = 2 * f.per
            two_each = f.wide // 128

            def step(u, s, i):
                if exists(f, u):
                    if s % 2 == 0:
                        for j in range(two_each):
                            col = two_each * (f.per * i + s // 2) + j
                            src = gates[:, :, col] if isinstance(col, int) else gates[:, :, bass.ds(col, 1)].rearrange("p t o -> p (t o)")
                            dve.tensor_copy(gcol[:, s // 2, T * j:T * j + T], src)
                    for c in range(f.chunks):
                        kk = f.chunks * u + c
                        z = (f.chunks * s + c) % 2
                        dve.wait_ge(f.silu, kk + 1)
                        if c == 0:
                            waitfrom(dve, f.y, 0, u - 1)
                        dve.tensor_tensor(h_at(s % 2, c), silus[:, z, :], bank(2 * z + 1), ALU.mult).then_inc(f.h, 1)
                        if c == 0 and exists(f, u - 1):
                            add(u - 1, (s - 1) % n)
                else:
                    add(u - 1, (s - 1) % n)

            def add(u, s):
                dve.drain()
                dve.wait_ge(f.y, u + 1)
                yb = 4 + f.y_banks * (s % 2)
                per_bank = 512 // f.wide
                for j in range(two_each):
                    if j:
                        dve.drain()
                    for t in range(4):
                        tt = 4 * (s % 2) + t
                        a = t % per_bank * f.wide + 128 * j
                        last = dve_add_gated(dve, tt, bank(yb + t // per_bank)[:, a:a + 128],
                                             gcol[:, s // 2, T * j + tt:T * j + tt + 1])
                last.then_inc(f.acc, 1)
            units(dve, f, step)
            dve.drain()
            dve.nop().then_inc(x_done, 1)

        def sp_gated(sp, f):
            sp_experts(sp, f.src, f.slot, f.experts, f.per, f.w, f.y, 0)

        weigh_turn = sem("weigh_turn")
        weigh_cols = sem("weigh_cols")
        weigh_out = sem("weigh_out")
        weigh_in = sem("weigh_in")
        met = sem("met")
        met_sum = sem("met_sum")
        edge = sem("edge")
        edge_row = sem("edge_row")
        weigh_dram = nc.dram_tensor("weigh_dram", (8, N), F32).ap()

        def pe_capacity(pe):
            pe.wait_ge(choice, 2)
            pe.transpose(bank(4)[0:64, 0:128], xi[:, 0, 0:64], cst("ident")).then_inc(weigh_turn, 1)
            for i in range(len(SHIFTS)):
                pe.wait_ge(met, i + 1)
                mm(pe, bank(4)[:, 128:129], cstb("same_expert"), metb[:, 0:1]).then_inc(met_sum, 1)
            pe.wait_ge(edge, 1)
            mm(pe, bank(4)[:, 256:272], cst("ones"), edges[:, :]).then_inc(edge_row, 1)
            pe.wait_ge(choice, 3)
            pe_prefix(pe, bank(6)[:, 0:64], picksb[:, 0:T, :].rearrange("p t e -> p (t e)"), T).then_inc(counted, 1)
            pe.wait_ge(choice, 4)
            pe_prefix(pe, bank(6)[:, 64:128], picksb[:, T:2 * T, :].rearrange("p t e -> p (t e)"), T).then_inc(counted, 1)

        metb = sb("metb", [128, 1], BF16)
        edges = sb("edges", [128, 16])
        edger = sb("edger", [128, 16])
        found = sb("found", [128, 1], I32)
        trial = sb("trial", [128, 1], I32)
        step_i = sb("step_i", [128, 1], I32)
        count = sb("count", [128, 1])

        def dve_capacity(dve):
            sel, wt = picks[:, 2, :, 0:8], picks[:, 3, :, 0:8]
            mine = [picks[:, j, :, 8:16] for j in range(2)]
            for j in range(2):
                dve.tensor_copy(mine[j], picks[:, j, :, 0:8])
            dve.tensor_tensor(sel, picks[:, 0, :, 0:8], picks[:, 1, :, 0:8], ALU.add)
            dve.drain()
            dve.scalar_tensor_tensor(wt, sel, 1.0, gates[:, :, 0:8], ALU.subtract, ALU.add)
            dve.drain()
            dve.tensor_copy(xi[:, 0, 0:64].rearrange("p (e t) -> p t e", t=T), wt).then_inc(choice, 1)
            dve.memset(found[:, :], 0)
            dve.wait_ge(weigh_in, 256)
            row_w, hit = e[:, 0:N], e[:, N:2 * N]
            for i, shift in enumerate(SHIFTS):
                dve.drain()
                dve.tensor_tensor(trial[:, :], found[:, :], cis[:, i:i + 1], ALU.add)
                dve.drain()
                dve.tensor_scalar(hit, row_w, trial[:, :].bitcast(F32), 0.0, ALU.is_ge, ALU.add, accum_out=count[:, :])
                dve.drain()
                dve.tensor_scalar(metb[:, :], count[:, :], float(L1_CAPACITY), None, ALU.is_ge).then_inc(met, 1)
                dve.wait_ge(met_sum, i + 1)
                dve.tensor_scalar(count[:, :], bank(4)[:, 128:129], 1.0, 0.0, ALU.subtract, ALU.max)
                dve.drain()
                dve.tensor_scalar(step_i[:, :], count[:, :], float(1 << shift), None, ALU.mult)
                dve.drain()
                dve.tensor_tensor(found[:, :], found[:, :], step_i[:, :], ALU.add)
            dve.drain()
            dve.tensor_scalar(hit, row_w, found[:, :].bitcast(F32), 0.0, ALU.is_gt, ALU.add, accum_out=count[:, :])
            dve.tensor_scalar(edges[:, 0:8], cst("expert_row"), found[:, :].bitcast(F32), None, ALU.mult)
            dve.drain()
            dve.tensor_scalar(edges[:, 8:16], cst("expert_row"), count[:, :], None, ALU.mult).then_inc(edge, 1)
            dve.wait_ge(edge_row, 1)
            dve.tensor_copy(edger[:, :], bank(4)[:, 256:272])
            dve.drain()
            dve.tensor_scalar(edger[:, 8:16], edger[:, 8:16], -1.0, float(L1_CAPACITY), ALU.mult, ALU.add)
            over, same = picks[:, 0, :, 0:8], picks[:, 1, :, 0:8]
            dve.tensor_tensor(over, wt, rows_of(edger[:, 0:8]), ALU.is_gt)
            dve.tensor_tensor(same, wt, rows_of(edger[:, 0:8]), ALU.is_equal)
            dve.drain()
            dve.tensor_copy(picksb[:, 0:T, :], same).then_inc(choice, 1)
            dve.wait_ge(counted, 2)
            dve.tensor_tensor(sel, bank(6)[:, 0:64].rearrange("p (t e) -> p t e", e=8), rows_of(edger[:, 8:16]), ALU.is_lt)
            dve.drain()
            dve.tensor_tensor(same, same, sel, ALU.mult)
            dve.drain()
            dve.tensor_tensor(same, same, over, ALU.add)
            dve.drain()
            g8 = gates[:, :, 0:8]
            dve.tensor_copy(picksb[:, T:2 * T, :], same).then_inc(choice, 1)
            for j in range(2):
                dve.tensor_tensor(mine[j], mine[j], same, ALU.mult)
            dve.tensor_tensor(g8, g8, same, ALU.mult)
            dve.drain()
            dve.tensor_reduce(tot[:, :], g8, AX.X, ALU.add)
            dve.drain()
            dve.tensor_scalar(tot[:, :], tot[:, :], 1.1920929e-07, None, ALU.max)
            dve.drain()
            dve.reciprocal(tot[:, :], tot[:, :])
            dve.drain()
            dve.tensor_tensor(g8, g8, per_token(tot[:, :], 8), ALU.mult)
            dve.drain()
            dve.wait_ge(counted, 3)
            dve_slots(dve, r1, mine, [bank(6)[:, 64:128].rearrange("p (t e) -> p t e", e=8)] * 2)

        def sp_capacity(sp):
            sp.wait_ge(weigh_cols, 1)
            sp.dma_start(weigh_dram.rearrange("e (t p) -> (e t) p", p=128), et[0:64, 0:128]).then_inc(weigh_out, 16)
            sp.wait_ge(weigh_out, 16)
            for j in range(16):
                sp.dma_start(e[8 * j:8 * j + 8, 0:N], weigh_dram).then_inc(weigh_in, 16)

        def pe_f1(pe, m):
            pe_turn(pe, m, xn)
            pe_route(pe, m, 5, "l1f_wr", 8)
            pe_capacity(pe)
            pe_routed(pe, r1)

        def act_f1(act, m):
            act_turn(act, m)
            act_probs(act, 1, 8)
            act.wait_ge(weigh_turn, 1)
            act.copy(et[0:64, 0:128], bank(4)[0:64, 0:128]).then_inc(weigh_cols, 1)
            act_routed(act, r1)

        def dve_f1(dve, norm):
            dve_norm(dve, norm, x, xn, 1e-5)
            dve_probs(dve, 1, 8)
            dve_best(dve, 8, 2, 1.1920929e-07)
            dve_gates(dve, 8, 2)
            dve_capacity(dve)
            dve_routed(dve, r1)

        def pe_f2(pe, m):
            pe_turn(pe, m, xn)
            pe_route(pe, m, 8, "l2f_wr", 32)
            pe_gated(pe, f2)

        def act_f2(act, m):
            act_turn(act, m)
            act_probs(act, 2, 32)
            act_gated(act, f2)

        def dve_f2(dve, norm):
            dve_norm(dve, norm, x, xn, 1e-5)
            dve_probs(dve, 2, 32, "l2f_br")
            dve_best(dve, 32, 4, 1e-12)
            dve_gates(dve, 32, 4)
            dve.memset(gates[:, :, 32:36], 1.0)
            dve.drain()
            dve_gated(dve, f2)

        def pe_f3(pe, m):
            pe_turn(pe, m, xn)
            pe_route(pe, m, 11, "l3f_wg", 32)
            pe_gated(pe, f3)

        def act_f3(act, m):
            act_turn(act, m)
            act.wait_ge(route_less, 4)
            act.activation(probs[:, :, :], lg[:, :, :], ACT.Exp, scale=-1.0).then_inc(route_exp, 1)
            act_gated(act, f3)

        def dve_f3(dve, norm):
            LOW = -3.0e38
            dve_norm(dve, norm, x, xn, 1e-5)
            dve.wait_ge(route_logit, 4)
            dve.tensor_copy(lg[:, :, :], bank(5)[:, 0:256].rearrange("p (t e) -> p t e", e=32)).then_inc(route_less, 1)
            group = small[:, 0:8, 0:8]
            gmask = small[:, 8:16, 0:8]
            gbest = xi[:, 1, :].rearrange("p (t c) -> p t c", c=16)[:, :, 0:8]
            tops = xi[:, 2:4, :].rearrange("p a (n c) -> p (a n) c", c=8)
            dve.memset(group, LOW)
            dve.wait_ge(route_exp, 4)
            dve.tensor_scalar(probs[:, :, :], probs[:, :, :], 1.0, None, ALU.add)
            dve.drain()
            dve.reciprocal(probs[:, :, :], probs[:, :, :])
            dve.drain()
            dve.tensor_tensor(lg[:, :, :], probs[:, :, :], rows_of(row("l3f_bg")), ALU.add)
            dve.drain()
            for t in range(T):
                for g in range(4):
                    dve.max(tops[:, 4 * t + g, :], lg[:, t, 8 * g:8 * g + 8])
            dve.drain()
            dve.tensor_tensor(group[:, :, 0:4], tops[:, :, 0].rearrange("p (t g) -> p t g", g=4),
                              tops[:, :, 1].rearrange("p (t g) -> p t g", g=4), ALU.add)
            dve.drain()
            for t in range(T):
                dve.max(gbest[:, t, :], group[:, t, :])
            dve.drain()
            for t in range(T):
                dve.max_index(best_at[:, t, :], gbest[:, t, :], group[:, t, :])
            dve.drain()
            dve.tensor_copy(best_atf[:, :, :], best_at[:, :, :])
            dve.drain()
            dve.tensor_tensor(gmask[:, :, 0:4], rows_of(cst("iota")[:, 0:4]),
                              best_atf[:, :, 0:1].to_broadcast([128, T, 4]), ALU.is_equal)
            dve.tensor_tensor(gmask[:, :, 4:8], rows_of(cst("iota")[:, 0:4]),
                              best_atf[:, :, 1:2].to_broadcast([128, T, 4]), ALU.is_equal)
            dve.drain()
            dve.tensor_tensor(gmask[:, :, 0:4], gmask[:, :, 0:4], gmask[:, :, 4:8], ALU.add)
            dve.drain()
            dve.tensor_tensor(lg[:, :, :].rearrange("p t (g c) -> p t g c", c=8),
                              lg[:, :, :].rearrange("p t (g c) -> p t g c", c=8),
                              gmask[:, :, 0:4].unsqueeze(3).to_broadcast([128, T, 4, 8]), ALU.mult)
            dve.drain()
            for t in range(T):
                dve.max(best[:, t, :], lg[:, t, :])
            dve.drain()
            for t in range(T):
                dve.match_replace(tmp[:, t, :], best[:, t, :], lg[:, t, :], LOW)
            dve.drain()
            dve.tensor_scalar(tmp[:, :, :], tmp[:, :, :], LOW * 0.99, None, ALU.is_le)
            dve.drain()
            dve.tensor_tensor(gates[:, :, 0:32], tmp[:, :, :], probs[:, :, :], ALU.mult)
            dve.drain()
            dve.tensor_reduce(tot[:, :], gates[:, :, 0:32], AX.X, ALU.add)
            dve.drain()
            dve.tensor_scalar(tot[:, :], tot[:, :], 1e-20, None, ALU.add)
            dve.drain()
            dve.reciprocal(tot[:, :], tot[:, :])
            dve.drain()
            dve.tensor_tensor(gates[:, :, 0:32], gates[:, :, 0:32], per_token(tot[:, :], 32), ALU.mult)
            dve.drain()
            dve.tensor_scalar(gates[:, :, 0:32], gates[:, :, 0:32], 2.5, None, ALU.mult)
            dve.memset(gates[:, :, 32:34], 1.0)
            dve.drain()
            dve_gated(dve, f3)

        block = ctx.enter_context(nc.Block())

        @block.sync
        def _(sp):
            sp.dma_start(x[:, :, :], xin.rearrange("(t p) d -> p t d", p=128)).then_inc(x_loaded, 16)
            sp.dma_start(cfs[:, :], cf).then_inc(const_loaded, 16)
            sp.dma_start(work[:, 0:B_COLUMNS], cb).then_inc(const_loaded, 16)
            sp.dma_start(cis[:, :], ci).then_inc(const_loaded, 16)
            sp.dma_start(bsb[:, :], biases).then_inc(const_loaded, 16)
            sp.dma_start(rsb[:, :], rows.to_broadcast([128, ROW_COLUMNS])).then_inc(const_loaded, 16)
            sp.dma_start(ctxc[:, :], ctx_cols).then_inc(ctx_loaded, 16)
            sp.dma_start(ctxr[:, :, :], ctx_rows).then_inc(ctx_loaded, 16)
            for i in range(STAGES):
                a = WEIGHT_AT[WEIGHTS[i][0][0]][0]
                n = sum(width for _, width in WEIGHTS[i])
                sp.dma_start(wsb[:, a:a + n], weights[:, a:a + n]).then_inc(w_loaded[i], 16)
            sp_clear(sp)
            sp.wait_ge(cleared, 64)
            sp.wait_ge(x_done, 2)
            sp_routed(sp, r0)
            sp_capacity(sp)
            sp_routed(sp, r1)
            sp.wait_ge(x_done, 8)
            sp_gated(sp, f2)
            sp.wait_ge(x_done, 9)
            sp_gated(sp, f3)
            sp.wait_ge(x_done, STAGES)
            sp.dma_start(out.rearrange("(t p) d -> p t d", p=128), x[:, :, :]).then_inc(x_loaded, 16)
            sp.wait_ge(x_loaded, 32)

        @block.gpsimd
        def _(pool):
            pool.memset(minus_half[:, :], -0.5).then_inc(half_set, 1)
            pool.wait_ge(half_set, 1)
            pool_clear(pool)
            pool_rstd(pool, 0)
            pool_rstd(pool, 1)
            pool_rstd(pool, 2)
            pool_rstd(pool, 3)
            pool_routed(pool, r0)
            for st in range(3, STAGES):
                if st == 4:
                    for n in range(5, 8):
                        if n == 7:
                            pool_wave(pool)
                        pool_rstd(pool, n)
                    continue
                pool_rstd(pool, 4 if st == 3 else st + 3)
                if st == 3:
                    pool_l1x(pool)
                if st == 5:
                    pool_routed(pool, r1)
                if st in (7, 10):
                    pool_self(pool, st)
                if st == 9:
                    pool_l3x(pool)

        @block.scalar
        def _(act):
            act.wait_ge(const_loaded, 80)
            act_xs(act, 0, 0)
            act_la(act, 1)
            act_f0(act, 2)
            act_l1x(act, 3)
            act_wave(act, 4)
            act_f1(act, 6)
            act_xs(act, 1, 7)
            act_self(act, 7, 8)
            act_f2(act, 9)
            act_l3x(act, 10)
            act_self(act, 10, 11)
            act_f3(act, 12)

        @block.vector
        def _(dve):
            dve.wait_ge(x_loaded, 16)
            dve.wait_ge(const_loaded, 80)
            dve.tensor_copy(cbs[:, :], work[:, 0:B_COLUMNS])
            dve.drain()
            dve_xs(dve, 0, 0)
            dve_la(dve, 1)
            dve_f0(dve, 3)
            dve_l1x(dve, 4)
            dve_wave(dve, 5)
            dve_f1(dve, 8)
            dve_xs(dve, 1, 9)
            dve_self(dve, 7, 10)
            dve_f2(dve, 11)
            dve_l3x(dve, 12)
            dve_self(dve, 10, 13)
            dve_f3(dve, 14)

        @block.tensor
        def _(pe):
            pe_xs(pe, 0, 0, 0)
            pe_la(pe, 1, 1)
            pe_f0(pe, 2, 2)
            pe_l1x(pe, 3, 3)
            pe_wave(pe, 4, 4)
            pe_f1(pe, 6)
            pe_xs(pe, 1, 6, 7)
            pe_self(pe, 7, 8)
            pe_f2(pe, 9)
            pe_l3x(pe, 9, 10)
            pe_self(pe, 10, 11)
            pe_f3(pe, 12)



def laid_out(i):
    f = lambda a: np.asarray(a)
    t = lambda a: np.swapaxes(np.asarray(a), -1, -2)
    half = np.concatenate([np.arange(HD // 2, HD), np.arange(HD // 2)])
    swap = np.arange(HD) ^ 1
    by_half = (np.arange(H)[:, None] * HD + half[None, :]).ravel()
    by_two = (np.arange(H)[:, None] * HD + swap[None, :]).ravel()
    b2 = np.zeros((128, T, D), np.float32)
    for tt in range(T):
        b2[8 * tt:8 * tt + 8, tt] = f(i["L0_ffn_b2"])
    wt = {
        "l0x_w": t(i["L0_xattn_W"]),
        "l0a_wq": t(i["L0_attn_Wq"]), "l0a_wkv": np.concatenate([t(i["L0_attn_Wk"]), t(i["L0_attn_Wv"])], 1),
        "l0a_wd": t(i["L0_attn_Wd"]),
        "l0f_wg": f(i["L0_ffn_wg"]), "l0f_b2": b2.reshape(128, T * D),
        "l1x_wq": f(i["L1_xattn_Wq"]), "l1x_wk": f(i["L1_xattn_Wk"]), "l1x_wv": f(i["L1_xattn_Wv"]),
        "l1x_wo": f(i["L1_xattn_Wo"]),
        "l1a_wqf": f(i["L1_attn_Wqf"]), "l1a_wqp": f(i["L1_attn_Wqp"]), "l1a_wkf": f(i["L1_attn_Wkf"]),
        "l1a_wkp": f(i["L1_attn_Wkp"]), "l1a_wv": f(i["L1_attn_Wv"]), "l1a_wo": f(i["L1_attn_Wo"]),
        "l1a_w1": f(i["L1_attn_W1"]),
        "l1a_w2": f(i["L1_attn_W2"]).reshape(4, 128, 128).transpose(1, 0, 2).reshape(128, 512),
        "l1f_wr": t(i["L1_ffn_router_weight"]),
        "l2x_wq": f(i["L2_xattn_W_q"]), "l2x_wk": f(i["L2_xattn_W_k"]), "l2x_wv": f(i["L2_xattn_W_v"]),
        "l2a_wq": t(i["L2_attn_Wq"]), "l2a_wqr": t(i["L2_attn_Wq"])[:, by_half],
        "l2a_wk": t(i["L2_attn_Wk"]), "l2a_wkr": t(i["L2_attn_Wk"])[:, by_half],
        "l2a_wv": t(i["L2_attn_Wv"]), "l2a_wo": t(i["L2_attn_Wo"]),
        "l2f_wr": t(i["L2_ffn_router_w"]),
        "l3x_wq": f(i["L3_xattn_W_Q"]), "l3x_wk": f(i["L3_xattn_W_K"]), "l3x_wv": f(i["L3_xattn_W_V"]),
        "l3x_wo": f(i["L3_xattn_W_O"]),
        "l3a_wq": t(i["L3_attn_Wq"]), "l3a_wqr": t(i["L3_attn_Wq"])[:, by_two],
        "l3a_wk": t(i["L3_attn_Wk"]), "l3a_wkr": t(i["L3_attn_Wk"])[:, by_two],
        "l3a_wv": t(i["L3_attn_Wv"]), "l3a_wo": t(i["L3_attn_Wo"]),
        "l3f_wg": t(i["L3_ffn_gate_w"]),
    }
    rw = {
        "l0a_bkv": np.concatenate([f(i["L0_attn_bk"]), f(i["L0_attn_bv"])]), "l0a_bd": i["L0_attn_bd"],
        "l0a_gamma": i["L0_attn_gamma"], "l0a_beta": i["L0_attn_beta"], "l1x_bv": i["L1_xattn_bv"],
        "l1x_bo": i["L1_xattn_bo"], "l1a_g1": i["L1_attn_ln1_g"], "l1a_be1": i["L1_attn_ln1_b"],
        "l1a_bv": i["L1_attn_bv"], "l1a_bo": i["L1_attn_bo"], "l1a_iscale": f(i["L1_attn_iscale"]).reshape(-1),
        "l1a_g2": i["L1_attn_ln2_g"], "l1a_be2": i["L1_attn_ln2_b"], "l1a_b2": i["L1_attn_b2"],
        "l2x_bv": i["L2_xattn_b_v"], "l2a_bv": i["L2_attn_bv"], "l2a_bo": i["L2_attn_bo"],
        "l2f_br": i["L2_ffn_router_bias"], "l3x_bv": i["L3_xattn_b_V"], "l3x_bo": i["L3_xattn_b_O"],
        "l3f_bg": i["L3_ffn_gate_bias"],
    }
    two = lambda a: f(a).reshape(-1, 128).T
    bs = {
        "l0x_b": two(i["L0_xattn_b"]), "l0a_bq": two(i["L0_attn_bq"]), "l1x_bq": two(i["L1_xattn_bq"]),
        "l1x_bk": two(i["L1_xattn_bk"]), "l1a_bqf": two(i["L1_attn_bqf"]), "l1a_bqp": two(i["L1_attn_bqp"]),
        "l1a_bkf": two(i["L1_attn_bkf"]), "l1a_bkp": two(i["L1_attn_bkp"]), "l1a_b1": two(i["L1_attn_b1"]),
        "l2x_bq": two(i["L2_xattn_b_q"]), "l2x_bk": two(i["L2_xattn_b_k"]), "l2a_bq": two(i["L2_attn_bq"]),
        "l2a_bqr": two(f(i["L2_attn_bq"])[by_half]), "l2a_bk": two(i["L2_attn_bk"]),
        "l2a_bkr": two(f(i["L2_attn_bk"])[by_half]), "l3x_bq": two(i["L3_xattn_b_Q"]), "l3x_bk": two(i["L3_xattn_b_K"]),
    }
    chunks = lambda a: a.reshape(a.shape[0], -1, 128, 128).transpose(0, 2, 1, 3).reshape(a.shape[0], 128, -1)
    l0f = np.concatenate([f(i["L0_ffn_w1"]), chunks(f(i["L0_ffn_w2"])),
                          f(i["L0_ffn_b1"]).reshape(8, 4, 128).transpose(0, 2, 1)], 2)
    l1f = np.concatenate([t(i["L1_ffn_ff_pre_act_weight"]), t(i["L1_ffn_gate_weight"]),
                          chunks(t(i["L1_ffn_ff_post_act_weight"]))], 2)
    shared = lambda a: t(a).reshape(128, 4, 128).transpose(1, 0, 2)
    l2f = np.concatenate([
        np.concatenate([t(i["L2_ffn_up_w"]), shared(i["L2_ffn_sup_w"])], 0),
        np.concatenate([t(i["L2_ffn_gate_w"]), shared(i["L2_ffn_sgate_w"])], 0),
        np.concatenate([t(i["L2_ffn_down_w"]), t(i["L2_ffn_sdown_w"]).reshape(4, 128, 128)], 0)], 2)
    pair = lambda a, s: np.concatenate([t(a).reshape(16, 2, 128, 64).transpose(0, 2, 1, 3).reshape(16, 128, 128),
                                        t(s)[None]], 0)
    down = np.concatenate([t(i["L3_ffn_expert_down"]).reshape(16, 128, 128), t(i["L3_ffn_shared_down"])[None]], 0)
    apart = np.zeros((17, 128, 256), np.float32)
    apart[:, 0:64, 0:128] = down[:, 0:64]
    apart[:, 64:128, 128:256] = down[:, 64:128]
    l3f = np.concatenate([pair(i["L3_ffn_expert_up"], i["L3_ffn_shared_up"]),
                          pair(i["L3_ffn_expert_gate"], i["L3_ffn_shared_gate"]), apart], 2)
    ctxs = f(i["ctx_1024"])
    return {
        "xin": f(i["x"]).reshape(N, D),
        "ctx_cols": ctxs.reshape(B * S, D).T,
        "ctx_rows": ctxs.transpose(1, 0, 2),
        "weights": np.concatenate([wt[n] for n, _ in [w for g in WEIGHTS for w in g]], 1),
        "rows": np.concatenate([f(rw[n]) for n, _ in ROWS])[None, :],
        "biases": np.concatenate([bs[n] for n, _ in BIASES], 1),
        "l0f": l0f, "l1f": l1f, "l2f": l2f, "l3f": l3f,
        "cf": np.concatenate(list(const_columns().values()), 1),
        "cb": np.concatenate(list(const_bf_columns().values()), 1),
        "ci": const_int_columns(),
    }


def kernel(**inputs):
    import concourse.bacc as bacc
    from concourse.bass_utils import run_bass_kernel_spmd as run

    nc = bacc.Bacc("TRN2", target_bir_lowering=False, num_devices=1)
    arrays = {f"in_{k}": np.ascontiguousarray(v) for k, v in laid_out(inputs).items()}
    args = {k[3:]: nc.dram_tensor(k, a.shape, mybir.dt.from_np(a.dtype), kind="ExternalInput").ap()
            for k, a in arrays.items()}
    out = nc.dram_tensor("out_0", (N, D), F32, kind="ExternalOutput").ap()
    perceiver(nc, out=out, **args)
    r = run(nc, [arrays], core_ids=[0])
    return r.results[0]["out_0"].reshape(B, L, D)
```

```python
from contextlib import ExitStack

import numpy as np
import concourse.bass as bass
from concourse import mybir

F32 = mybir.dt.float32
BF16 = mybir.dt.bfloat16
I32 = mybir.dt.int32
U32 = mybir.dt.uint32
ALU = mybir.AluOpType
ACT = mybir.ActivationFunctionType
AX = mybir.AxisListType

D = 128
B = 16
L = 64
S = 128
N = B * L
T = N // 128
H = 16
HD = D // H
W = 16
L3F_GATES = 32 + 2
L0_CAPACITY = 2 * N // 8
L1_CAPACITY = -(-5 * 2 * N // (4 * 8))
STAGES = 12



def const_columns():
    p = np.arange(128)
    c = {}
    c["ident"] = np.eye(128)
    c["ones"] = np.ones((128, 128))
    c["same_head"] = (p[:, None] // HD == p[None, :] // HD)
    c["head"] = (p[:, None] // HD == np.arange(H)[None, :])
    c["head_eps"] = c["head"] * 1e-6
    c["head_pair"] = (p[:, None] // (2 * HD) == np.arange(H // 2)[None, :])
    c["head_parity"] = (p[:, None] // HD % 2 == np.arange(2)[None, :])
    c["head_of_four"] = (p[:, None] // HD % 4 == np.arange(4)[None, :])
    c["wave_pair"] = (p[:, None] // (2 * W) == np.arange(4)[None, :])
    c["wave_parity"] = (p[:, None] // W % 2 == np.arange(2)[None, :])
    half = np.arange(2)[None, :, None]
    c["wave_sum"] = (8 * half + p[:, None, None] // W == np.arange(32)[None, None, :]).reshape(128, 64)
    at = 32 * np.arange(4)[:, None, None] + 8 * np.arange(2)[None, :, None] + (p // W)[None, None, :]
    c["wave_spread"] = (p[:, None, None, None] == at[None]).reshape(128, 1024)
    col = np.arange(32)
    ii, j = col // 16, col // 8 % 2
    r = p[:, None, None] // L
    k = np.arange(2)[None, :, None]
    c["value_soft"] = ((ii == r) & (j == k)).reshape(128, 64)
    c["value_wave"] = ((j == r) & (ii == k)).reshape(128, 64)
    s, t = p[:, None] % L, np.arange(L)[None, :]
    c["wave_causal"] = (s <= t) / np.sqrt(t + 1.0)
    c["position"] = np.broadcast_to(t, (128, L))
    f32 = np.float32
    d = p[:, None] % HD
    theta = f32(1250) ** (f32(-2.0) * (d % (HD // 2)).astype(f32) / f32(HD))
    ang = (t + 1).astype(f32) * theta.astype(f32)
    c["rope2_cos"] = np.cos(ang.astype(f32))
    c["rope2_sin"] = np.sin(ang.astype(f32)) * np.where(d < HD // 2, -1.0, 1.0)
    freq = f32(1.0) / f32(10000.0) ** ((2 * (d % (HD // 2))).astype(f32) / f32(HD))
    ang = t.astype(f32) * freq.astype(f32)
    c["rope3_cos"] = np.cos(ang.astype(f32))
    c["rope3_sin"] = np.sin(ang.astype(f32)) * np.where(d % 2 == 0, -1.0, 1.0)
    c["iota"] = np.broadcast_to(np.arange(32)[None, :], (128, 32))
    c["first_slot0"] = np.broadcast_to(L0_CAPACITY * np.arange(8)[None, :], (128, 8))
    c["first_slot1"] = np.broadcast_to(L1_CAPACITY * np.arange(8)[None, :], (128, 8))
    c["spare_row"] = np.arange(2 * T)[None, :] * 128 + p[:, None]
    c["gate_row"] = (p[:, None] % L3F_GATES == np.arange(L3F_GATES)[None, :]) & (p[:, None] < 3 * L3F_GATES)
    c["needed"] = L1_CAPACITY * (p[:, None] >= 8)
    c["expert_row"] = (p[:, None] == np.arange(8)[None, :])
    return {k: np.asarray(v, np.float32) for k, v in c.items()}


def const_bf_columns():
    p = np.arange(128)
    c = {}
    c["identb"] = np.eye(128)
    c["earlier"] = (p[:, None] < p[None, :])
    c["onesb"] = np.ones((128, 128))
    c["same_expert"] = (p[:, None] % 8 == p[None, :] % 8)
    c["causal"] = np.where(np.arange(L)[None, None, :] <= p[:, None, None] % L, 0.0, -1e30) * np.ones((1, 8, 1))
    return {k: np.asarray(v, np.float32).reshape(128, -1) for k, v in c.items()}


SHIFTS = [26, 22, 18, 14, 10, 6, 2, 0]


def const_int_columns():
    return (np.arange(128)[:, None] // 8 << np.array(SHIFTS)[None, :]).astype(np.int32)



WEIGHTS = [
    [("l0x_w", 128)],
    [("l0a_wq", 128), ("l0a_wkv", 256), ("l0a_wd", 128)],
    [("l0f_wg", 8), ("l0f_b2", 1024)],
    [("l1x_wq", 128), ("l1x_wk", 128), ("l1x_wv", 128), ("l1x_wo", 128)],
    [("l1a_wqf", 256), ("l1a_wqp", 256), ("l1a_wkf", 256), ("l1a_wkp", 256), ("l1a_wv", 128),
     ("l1a_wo", 128), ("l1a_w1", 512), ("l1a_w2", 512)],
    [("l1f_wr", 8)],
    [("l2x_wq", 128), ("l2x_wk", 128), ("l2x_wv", 128)],
    [("l2a_wq", 128), ("l2a_wqr", 128), ("l2a_wk", 128), ("l2a_wkr", 128), ("l2a_wv", 128), ("l2a_wo", 128)],
    [("l2f_wr", 32)],
    [("l3x_wq", 128), ("l3x_wk", 128), ("l3x_wv", 128), ("l3x_wo", 128)],
    [("l3a_wq", 128), ("l3a_wqr", 128), ("l3a_wk", 128), ("l3a_wkr", 128), ("l3a_wv", 128), ("l3a_wo", 128)],
    [("l3f_wg", 32)],
]
ROWS = [("l0a_bkv", 256), ("l0a_bd", 128), ("l0a_gamma", 128), ("l0a_beta", 128), ("l1x_bv", 128), ("l1x_bo", 128),
        ("l1a_bv", 128), ("l1a_bo", 128), ("l1a_iscale", 16), ("l1a_b2", 128), ("l2x_bv", 128), ("l2a_bv", 128), ("l2a_bo", 128), ("l2f_br", 32),
        ("l3x_bv", 128), ("l3x_bo", 128), ("l3f_bg", 32)]
BIASES = [("l0x_b", 1), ("l0a_bq", 1), ("l1x_bq", 1), ("l1x_bk", 1), ("l1a_bqf", 2), ("l1a_bqp", 2), ("l1a_bkf", 2),
          ("l1a_bkp", 2), ("l1a_b1", 4), ("l1a_g1", 1), ("l1a_be1", 1), ("l1a_g2", 1),
          ("l1a_be2", 1), ("l2x_bq", 1), ("l2x_bk", 1), ("l2a_bq", 1), ("l2a_bqr", 1), ("l2a_bk", 1),
          ("l2a_bkr", 1), ("l3x_bq", 1), ("l3x_bk", 1)]


def places(items):
    at, out = 0, {}
    for name, width in items:
        out[name] = (at, width)
        at += width
    return out, at


WEIGHT_AT, WEIGHT_COLUMNS = places([w for group in WEIGHTS for w in group])
ROW_AT, ROW_COLUMNS = places(ROWS)
BIAS_AT, BIAS_COLUMNS = places(BIASES)
L0F_SLOT = 512 + 512 + 4
L1F_SLOT = 512 + 512 + 512
L2F_SLOT = 128 + 128 + 128
L3F_SLOT = 128 + 128 + 128
L2F_EXPERTS = 4 + 32
L3F_PAIRS = 16 + 1


def perceiver(nc, xin, ctx_cols, ctx_rows, weights, rows, biases, l0f, l1f, l2f, l3f, cf, cb, ci, out):
    F_AT, F_COLUMNS = places([(k, v.shape[1]) for k, v in const_columns().items()])
    B_AT, B_COLUMNS = places([(k, v.shape[1]) for k, v in const_bf_columns().items()])
    with ExitStack() as ctx:
        def sb(name, shape, dt=F32):
            return ctx.enter_context(nc.sbuf_tensor(name, shape, dt))

        def sem(name):
            return ctx.enter_context(nc.semaphore(name))

        x = sb("x", [128, T, D])
        xn = sb("xn", [128, T, D])
        xi = sb("xi", [128, T, D])
        xnt = sb("xnt", [128, N])
        ctxc = sb("ctxc", [128, B * S])
        ctxr = sb("ctxr", [128, B, D])
        wsb = sb("wsb", [128, WEIGHT_COLUMNS])
        rsb = sb("rsb", [128, ROW_COLUMNS])
        bsb = sb("bsb", [128, BIAS_COLUMNS])
        cfs = sb("cfs", [128, F_COLUMNS])
        cbs = sb("cbs", [128, B_COLUMNS], BF16)
        cis = sb("cis", [128, len(SHIFTS)], I32)
        minus_half = sb("minus_half", [128, T])
        stats = sb("stats", [128, T, 6])
        moments = sb("moments", [128, T, 2])
        variance = sb("variance", [128, T])
        rstd = sb("rstd", [128, T])
        q = sb("q", [128, N])
        k = sb("k", [128, B * S])
        v = sb("v", [128, B, S])
        e = sb("e", [128, B * S])
        et = sb("et", [128, B * S])
        at = sb("at", [128, N])
        big = sb("big", [128, 4096])
        work = sb("work", [128, 4096])
        slots = sb("slots", [128, 4, L1F_SLOT])
        small = sb("small", [128, 32, 16])
        ps = ctx.enter_context(nc.psum_tensor("ps", [128, 8, 512], F32))

        def w(name, a=0, n=None):
            at0, width = WEIGHT_AT[name]
            return wsb[:, at0 + a:at0 + a + (width if n is None else n)]

        def row(name):
            at0, width = ROW_AT[name]
            return rsb[:, at0:at0 + width]

        def bias(name, i=0):
            return bsb[:, BIAS_AT[name][0] + i:BIAS_AT[name][0] + i + 1]

        def cst(name):
            at0, width = F_AT[name]
            return cfs[:, at0:at0 + width]

        def cstb(name):
            at0, width = B_AT[name]
            return cbs[:, at0:at0 + width]

        def rows_of(ap, n=T):
            return ap.unsqueeze(1).to_broadcast([128, n, ap.shape[1]])

        def bank(i):
            return ps[:, i, :]

        def banks(i, n, width):
            return ps[:, i:i + n, :].rearrange("p b (c w) -> p (b c) w", w=width)

        const_loaded = sem("const_loaded")
        bias_loaded = sem("bias_loaded")
        other_loaded = sem("other_loaded")
        ctxr_loaded = sem("ctxr_loaded")
        x_loaded = sem("x_loaded")
        ctx_loaded = sem("ctx_loaded")
        w_loaded = [sem(f"w_loaded{i}") for i in range(STAGES)]
        half_set = sem("half_set")
        x_done = sem("x_done")
        stats_ready = sem("stats_ready")
        rstd_ready = sem("rstd_ready")
        rows_ready = sem("rows_ready")
        turned = sem("turned")
        xnt_ready = sem("xnt_ready")


        def dve_norm(dve, n, src, dst, eps, publish=True):
            for h in range(2):
                for t in range(4 * h, 4 * h + 4):
                    dve.bn_stats(stats[:, t, :], src[:, t, :])
                dve.drain()
                for t in range(4 * h, 4 * h + 4):
                    last = dve.bn_aggr(moments[:, t, :], stats[:, t, :])
                dve.drain()
                dve.tensor_scalar(variance[:, 4 * h:4 * h + 4], moments[:, 4 * h:4 * h + 4, 1], eps, None,
                                  ALU.add).then_inc(stats_ready, 1)
            for h in range(2):
                dve.wait_ge(rstd_ready, 2 * n + h + 1)
                for t in range(4 * h, 4 * h + 4):
                    last = dve.tensor_scalar(dst[:, t, :], src[:, t, :], moments[:, t, 0:1], rstd[:, t:t + 1],
                                             ALU.subtract, ALU.mult)
                    if publish:
                        last.then_inc(rows_ready, 1)

        def pool_rstd(pool, n):
            for h in range(2):
                pool.wait_ge(stats_ready, 2 * n + h + 1)
                pool.tensor_tensor(rstd[:, 4 * h:4 * h + 4], variance[:, 4 * h:4 * h + 4], minus_half[:, 4 * h:4 * h + 4],
                                   ALU.pow).then_inc(rstd_ready, 1)

        def pe_turn(pe, m, src):
            for t in range(T):
                pe.wait_ge(rows_ready, T * m + t + 1)
                last = pe.transpose(bank(6 + t // 4)[:, t % 4 * 128:t % 4 * 128 + 128], src[:, t, :], cst("ident"))
                if t % 4 == 3:
                    last.then_inc(turned, 1)

        def act_turn(act, m, gain=None, shift=None):
            for h in range(2):
                act.wait_ge(turned, 2 * m + h + 1)
                dst, src = xnt[:, 512 * h:512 * h + 512], bank(6 + h)
                if gain is None:
                    act.copy(dst, src).then_inc(xnt_ready, 1)
                else:
                    act.activation(dst, src, ACT.Identity, scale=gain, bias=shift).then_inc(xnt_ready, 1)

        def mm(pe, o, lhs, rhs, start=True, stop=True):
            return pe.matmul(o, lhs, rhs, start=start, stop=stop)

        def peeled(eng, n, body, first=1):
            for i in range(first):
                body(i)
            with eng.Fori(first, n) as i:
                body(i)

        def wait(eng, s, value):
            if not isinstance(value, int) or value > 0:
                eng.wait_ge(s, value)

        def waitfrom(eng, s, base, more):
            if not isinstance(more, int) or more > 0:
                eng.wait_ge(s, base + more)

        kproj = sem("kproj")
        k_ready = sem("k_ready")
        vproj = sem("vproj")
        v_ready = sem("v_ready")
        qproj = sem("qproj")
        q_ready = sem("q_ready")
        VBANK = [4, 5, 0, 1]
        CROSS = [("l0x_w", "l0x_b", "l0x_w", "l0x_b", None, None)] + [
            (f"l{i}x_wq", f"l{i}x_bq", f"l{i}x_wk", f"l{i}x_bk", f"l{i}x_wv", f"l{i}x_bv") for i in (1, 2, 3)]

        def pe_keys(pe, n, stage):
            wq, _, wk, _, wv, _ = CROSS[n]
            pe.wait_ge(w_loaded[stage], 16)
            for c in range(4):
                mm(pe, bank(c), w(wk), ctxc[:, 512 * c:512 * c + 512]).then_inc(kproj, 1)
            if stage == 9:
                pe.wait_ge(x_done, stage)
            if n:
                for c in range(4):
                    if c >= 2:
                        pe.wait_ge(k_ready, 4 * n + c - 1)
                    for i in range(4):
                        b = 4 * c + i
                        last = mm(pe, bank(VBANK[c])[:, 128 * i:128 * i + 128], ctxc[:, 128 * b:128 * b + 128], w(wv))
                    last.then_inc(vproj, 1)

        def pe_project(pe, n, stage, m):
            if stage == 0:
                pe.wait_ge(ctx_loaded, 16)
                pe_keys(pe, n, stage)
                pe.wait_ge(const_loaded, 16)
            elif stage == 9:
                pe_keys(pe, n, stage)
            pe_turn(pe, m, xn)
            pe.wait_ge(k_ready, 4 * n + 4)
            for h in range(2):
                pe.wait_ge(xnt_ready, 2 * m + h + 1)
                mm(pe, bank(2 + h), w(CROSS[n][0]), xnt[:, 512 * h:512 * h + 512]).then_inc(qproj, 1)

        def act_keys(act, n):
            for c in range(4):
                act.wait_ge(kproj, 4 * n + c + 1)
                act.activation(k[:, 512 * c:512 * c + 512], bank(c), ACT.Identity,
                               bias=bias(CROSS[n][3])).then_inc(k_ready, 1)

        def act_project(act, n, m):
            if n in (0, 3):
                act_keys(act, n)
            act_turn(act, m)
            for h in range(2):
                act.wait_ge(qproj, 2 * n + h + 1)
                act.activation(q[:, 512 * h:512 * h + 512], bank(2 + h), ACT.Identity,
                               bias=bias(CROSS[n][1])).then_inc(q_ready, 1)

        def dve_values(dve, n):
            for c in range(4):
                dve.wait_ge(vproj, 4 * (n - 1) + c + 1)
                dve.tensor_tensor(v[:, 4 * c:4 * c + 4, :], banks(VBANK[c], 1, 128), rows_of(row(CROSS[n][5]), 4),
                                  ALU.add).then_inc(v_ready, 1)

        xs_score = sem("xs_score")
        xs_less = sem("xs_less")
        xs_exp = sem("xs_exp")
        xs_turn = sem("xs_turn")
        xs_et = sem("xs_et")
        xs_out = sem("xs_out")

        def pe_xs(pe, n, stage, m):
            c = 2 * n
            pe_project(pe, c, stage, m)
            if n:
                pe.wait_ge(v_ready, 4 * c)
            for h in range(2):
                pe.wait_ge(q_ready, 2 * c + h + 1)
                for i in range(8):
                    b = 8 * h + i
                    o = bank(h)[64 * (b % 2):64 * (b % 2) + 64, i // 2 * 128:i // 2 * 128 + 128]
                    last = mm(pe, o, q[:, L * b:L * b + L], k[:, S * b:S * b + S])
                last.then_inc(xs_score, 1)
            for h in range(2):
                pe.wait_ge(xs_exp, 2 * n + h + 1)
                for i in range(4):
                    t = 4 * h + i
                    last = pe.transpose(bank(2 + h)[:, 128 * i:128 * i + 128], e[:, 128 * t:128 * t + 128], cst("ident"))
                last.then_inc(xs_turn, 1)
            if not n:
                pe.wait_ge(ctxr_loaded, 16)
            for h in range(2):
                pe.wait_ge(xs_et, 2 * n + h + 1)
                for i in range(8):
                    b = 8 * h + i
                    o = bank(4 + h)[64 * (b % 2):64 * (b % 2) + 64, i // 2 * 128:i // 2 * 128 + 128]
                    last = mm(pe, o, et[:, L * b:L * b + L], v[:, b, :] if n else ctxr[:, b, :])
                last.then_inc(xs_out, 1)

        def act_xs(act, n, m):
            act_project(act, 2 * n, m)
            for h in range(2):
                act.wait_ge(xs_less, 2 * n + h + 1)
                act.activation(e[:, 512 * h:512 * h + 512], big[:, 512 * h:512 * h + 512], ACT.Exp,
                               scale=float(D) ** -0.5 if n else 1.0).then_inc(xs_exp, 1)
            for h in range(2):
                act.wait_ge(xs_turn, 2 * n + h + 1)
                act.copy(et[:, 512 * h:512 * h + 512], bank(2 + h)).then_inc(xs_et, 1)

        def dve_xs(dve, n, norm):
            dve_norm(dve, norm, x, xn, 1e-5)
            if not n:
                dve.wait_ge(other_loaded, 48)
                dve.wait_ge(const_loaded, 16)
                dve.tensor_copy(cbs[:, :], work[:, 0:B_COLUMNS])
            top, total, inverse = small[:, 0, 0:8], small[:, 1, 0:8], small[:, 2, 0:8]
            for h in range(2):
                dve.wait_ge(xs_score, 2 * n + h + 1)
                dve.tensor_reduce(top[:, 4 * h:4 * h + 4], banks(h, 1, 128), AX.X, ALU.max)
                dve.drain()
                dve.tensor_tensor(big[:, 512 * h:512 * h + 512].rearrange("p (t s) -> p t s", s=S), banks(h, 1, 128),
                                  top[:, 4 * h:4 * h + 4].unsqueeze(2).to_broadcast([128, 4, S]),
                                  ALU.subtract).then_inc(xs_less, 1)
            for h in range(2):
                dve.wait_ge(xs_exp, 2 * n + h + 1)
                dve.tensor_reduce(total[:, 4 * h:4 * h + 4], e[:, 512 * h:512 * h + 512].rearrange("p (t s) -> p t s", s=S),
                                  AX.X, ALU.add)
            dve.drain()
            dve.reciprocal(inverse, total)
            dve.drain()
            for h in range(2):
                dve.wait_ge(xs_out, 2 * n + h + 1)
                for i in range(4):
                    t = 4 * h + i
                    last = dve.scalar_tensor_tensor(x[:, t, :], bank(4 + h)[:, 128 * i:128 * i + 128],
                                                    inverse[:, t:t + 1], x[:, t, :], ALU.mult, ALU.add)
            last.then_inc(x_done, 1)
            dve.drain()

        la_q = sem("la_q")
        la_kv = sem("la_kv")
        la_neg = sem("la_neg")
        la_exp = sem("la_exp")
        la_feat = sem("la_feat")
        la_sum = sem("la_sum")
        la_kvm = sem("la_kvm")
        la_ctx = sem("la_ctx")
        la_div = sem("la_div")
        la_turn = sem("la_turn")
        la_cols = sem("la_cols")
        la_out = sem("la_out")
        KV = D + 1
        KVH = D + H
        vone = work[:, 0:T * KV].rearrange("p (t c) -> p t c", c=KV)
        kfeat = big[:, 0:N].rearrange("p (t c) -> p t c", c=D)
        kvm = slots[:, 0:2, :].rearrange("p a b -> p (a b)")[:, 0:B * KVH].rearrange("p (b c) -> p b c", c=KVH)

        def pe_la(pe, stage, m):
            pe_turn(pe, m, xn)
            pe.wait_ge(w_loaded[stage], 16)
            for h in range(2):
                pe.wait_ge(xnt_ready, 2 * m + h + 1)
                mm(pe, bank(4 + h), w("l0a_wq"), xnt[:, 512 * h:512 * h + 512]).then_inc(la_q, 1)
            for t in range(T):
                last = mm(pe, bank(t // 2)[:, 256 * (t % 2):256 * (t % 2) + 256], xnt[:, 128 * t:128 * t + 128],
                          w("l0a_wkv"))
                if t % 2:
                    last.then_inc(la_kv, 1)
            pe.wait_ge(la_feat, 3)
            for b in range(B):
                p = 64 * (b % 2)
                t = b // 2
                last = mm(pe, bank(3 * (b % 2) + t // 3)[:, KV * (t % 3):KV * (t % 3) + KV], kfeat[p:p + 64, t, :],
                          vone[p:p + 64, t, :])
            last.then_inc(la_sum, 1)
            pe.wait_ge(la_kvm, 1)
            for b in range(B):
                t, p = b // 2, 64 * (b % 2)
                last = mm(pe, bank(t // 3)[p:p + 64, KVH * (t % 3):KVH * (t % 3) + KVH], q[:, L * b:L * b + L],
                          kvm[:, T * (b % 2) + t, :])
            last.then_inc(la_ctx, 1)
            pe.wait_ge(la_div, 1)
            for t in range(T):
                last = pe.transpose(bank(6 + t // 4)[:, t % 4 * 128:t % 4 * 128 + 128], xi[:, t, :], cst("ident"))
                if t % 4 == 3:
                    last.then_inc(la_turn, 1)
            for t in range(T):
                if t % 4 == 0:
                    pe.wait_ge(la_cols, t // 4 + 1)
                last = mm(pe, bank(3 + t // 4)[:, t % 4 * 128:t % 4 * 128 + 128], at[:, 128 * t:128 * t + 128],
                          w("l0a_wd"))
            last.then_inc(la_out, 1)

        def act_la(act, m):
            act_turn(act, m)
            act.wait_ge(la_neg, 1)
            act.activation(e[:, 0:N], e[:, 0:N], ACT.Exp).then_inc(la_exp, 1)
            act.wait_ge(la_neg, 2)
            act.activation(et[:, 0:N], et[:, 0:N], ACT.Exp).then_inc(la_exp, 1)
            for h in range(2):
                act.wait_ge(la_turn, h + 1)
                act.copy(at[:, 512 * h:512 * h + 512], bank(6 + h)).then_inc(la_cols, 1)

        def dve_la(dve, norm):
            dve_norm(dve, norm, x, xn, 1e-5)
            dve.wait_ge(la_q, 2)
            dve.tensor_scalar(e[:, 0:N], ps[:, 4:6, :].rearrange("p b c -> p (b c)"), bias("l0a_bq"), 0.0,
                              ALU.add, ALU.min).then_inc(la_neg, 1)
            dve.tensor_scalar(q[:, :], ps[:, 4:6, :].rearrange("p b c -> p (b c)"), bias("l0a_bq"), 0.0,
                              ALU.add, ALU.max)
            dve.wait_ge(la_kv, 4)
            kv = banks(0, 4, 256)
            krow = rows_of(row("l0a_bkv")[:, 0:128])
            vrow = rows_of(row("l0a_bkv")[:, 128:256])
            dve.tensor_tensor(kfeat, kv[:, :, 0:128], krow, ALU.add)
            dve.memset(vone[:, :, 128:129], 1.0)
            dve.tensor_tensor(vone[:, :, 0:128], kv[:, :, 128:256], vrow, ALU.add).then_inc(la_feat, 1)
            dve.drain()
            dve.tensor_scalar(et[:, 0:N], big[:, 0:N], 0.0, None, ALU.min).then_inc(la_neg, 1)
            dve.wait_ge(la_exp, 1)
            dve.tensor_tensor(q[:, :], q[:, :], e[:, 0:N], ALU.add).then_inc(la_feat, 1)
            dve.wait_ge(la_exp, 2)
            dve.scalar_tensor_tensor(big[:, 0:N], big[:, 0:N], 0.0, et[:, 0:N], ALU.max,
                                     ALU.add).then_inc(la_feat, 1)
            dve.wait_ge(la_sum, 1)
            for g in range(6):
                nb, a = min(3, T - 3 * (g % 3)), T * (g // 3) + 3 * (g % 3)
                src = bank(g)[:, 0:nb * KV].rearrange("p (b c) -> p b c", c=KV)
                dve.tensor_tensor(kvm[:, a:a + nb, 0:128], src[:, :, 0:128], rows_of(cst("same_head"), nb), ALU.mult)
                dve.tensor_tensor(kvm[:, a:a + nb, 128:KVH], rows_of(cst("head"), nb),
                                  src[:, :, 128:129].to_broadcast([128, nb, H]), ALU.mult)
            dve.drain()
            dve.tensor_tensor(kvm[:, :, 128:KVH], kvm[:, :, 128:KVH], rows_of(cst("head_eps"), B), ALU.add)\
               .then_inc(la_kvm, 1)
            dve.wait_ge(la_ctx, 1)
            z = small[:, 0:8, :]
            for g in range(3):
                nt = min(3, T - 3 * g)
                src = bank(g)[:, 0:nt * KVH].rearrange("p (t c) -> p t c", c=KVH)
                dve.reciprocal(z[:, 3 * g:3 * g + nt, :], src[:, :, 128:KVH])
            dve.drain()
            for t in range(T):
                src = bank(t // 3)[:, KVH * (t % 3):KVH * (t % 3) + 128].rearrange("p (h d) -> p h d", d=HD)
                last = dve.tensor_tensor(xi[:, t, :].rearrange("p (h d) -> p h d", d=HD), src,
                                         z[:, t, :].unsqueeze(2).to_broadcast([128, H, HD]), ALU.mult)
            last.then_inc(la_div, 1)
            dve.tensor_tensor(xn[:, :, :], xn[:, :, :], rows_of(row("l0a_bd")), ALU.add)
            dve.tensor_tensor(x[:, :, :], x[:, :, :], rows_of(row("l0a_beta")), ALU.add)
            dve.drain()
            dve.wait_ge(la_out, 1)
            dve.tensor_tensor(xi[:, :, :], banks(3, 2, 128), xn[:, :, :], ALU.add)
            dve.drain()
            dve_norm(dve, norm + 1, xi, xi, 1e-12, publish=False)
            dve.drain()
            dve.tensor_tensor(xi[:, :, :], xi[:, :, :], rows_of(row("l0a_gamma")), ALU.mult)
            dve.drain()
            dve.tensor_tensor(x[:, :, :], x[:, :, :], xi[:, :, :], ALU.add).then_inc(x_done, 1)
            dve.drain()

        route_logit = sem("route_logit")
        route_less = sem("route_less")
        route_exp = sem("route_exp")
        choice = sem("choice")
        counted = sem("counted")
        NB = 36
        lg = sb("lg", [128, T, 32])
        probs = sb("probs", [128, T, 32])
        best = sb("best", [128, T, 8])
        best_at = sb("best_at", [128, T, 8], U32)
        best_atf = sb("best_atf", [128, T, 8])
        picks = sb("picks", [128, 4, T, 32])
        share = sb("share", [128, T, 8])
        tot = sb("tot", [128, T])
        gates = sb("gates", [128, T, NB])
        picksb = sb("picksb", [128, 2 * T, 8], BF16)
        tmp = sb("tmp", [128, T, 32])
        silus = work[:, 0:1024].rearrange("p (a c) -> p a c", a=2)
        gcol = sb("gcol", [128, 4, 2 * T])

        def pe_route(pe, m, stage, wname, E, at_bank=5):
            pe.wait_ge(w_loaded[stage], 16)
            for t in range(T):
                if t % 4 == 0:
                    pe.wait_ge(xnt_ready, 2 * m + t // 4 + 1)
                last = mm(pe, bank(at_bank)[:, E * t:E * t + E], xnt[:, 128 * t:128 * t + 128], w(wname))
            last.then_inc(route_logit, 1)

        def per_token(ap, E):
            return ap.unsqueeze(2).to_broadcast([128, T, E])

        def dve_logits(dve, n, E, brow=None, at_bank=5):
            lgE = lg[:, :, 0:E]
            dve.wait_ge(route_logit, n + 1)
            src = bank(at_bank)[:, 0:T * E].rearrange("p (t e) -> p t e", e=E)
            if brow is None:
                dve.tensor_copy(lgE, src)
            else:
                dve.tensor_tensor(lgE, src, rows_of(row(brow)), ALU.add)
            dve.drain()
            dve.tensor_reduce(tot[:, :], lgE, AX.X, ALU.max)
            dve.drain()
            dve.tensor_tensor(lgE, lgE, per_token(tot[:, :], E), ALU.subtract).then_inc(route_less, 1)

        def dve_probs(dve, n, E):
            pr = probs[:, :, 0:E]
            dve.wait_ge(route_exp, n + 1)
            dve.tensor_reduce(tot[:, :], pr, AX.X, ALU.add)
            dve.drain()
            dve.reciprocal(tot[:, :], tot[:, :])
            dve.drain()
            dve.tensor_tensor(pr, pr, per_token(tot[:, :], E), ALU.mult)
            dve.drain()

        def act_probs(act, n, E, scale=1.0):
            act.wait_ge(route_less, n + 1)
            act.activation(probs[:, :, 0:E], lg[:, :, 0:E], ACT.Exp, scale=scale).then_inc(route_exp, 1)

        def dve_best(dve, E):
            for t in range(T):
                dve.max(best[:, t, :], probs[:, t, 0:E])
            dve.drain()

        def dve_best_at(dve, E, K):
            for t in range(T):
                dve.max_index(best_at[:, t, :], best[:, t, :], probs[:, t, 0:E])
            dve.tensor_reduce(tot[:, :], best[:, :, 0:K], AX.X, ALU.add)
            dve.drain()

        def dve_picks(dve, E, K, floor):
            dve.tensor_copy(best_atf[:, :, :], best_at[:, :, :])
            if floor:
                dve.tensor_scalar(tot[:, :], tot[:, :], floor, None, ALU.max)
            dve.drain()
            for j in range(K):
                dve.tensor_tensor(picks[:, j, :, 0:E], rows_of(cst("iota")[:, 0:E]),
                                  best_atf[:, :, j:j + 1].to_broadcast([128, T, E]), ALU.is_equal)
            dve.reciprocal(tot[:, :], tot[:, :])
            dve.drain()
            dve.tensor_tensor(share[:, :, 0:K], best[:, :, 0:K], per_token(tot[:, :], K), ALU.mult)
            dve.drain()

        def dve_gates(dve, E, K, first=0):
            g = gates[:, :, first:first + E]
            dve.tensor_tensor(g, picks[:, 0, :, 0:E], share[:, :, 0:1].to_broadcast([128, T, E]), ALU.mult)
            for j in range(1, K):
                if j > 1:
                    dve.drain()
                dve.tensor_tensor(tmp[:, :, 0:E], picks[:, j, :, 0:E], share[:, :, j:j + 1].to_broadcast([128, T, E]),
                                  ALU.mult)
                dve.drain()
                dve.tensor_tensor(g, g, tmp[:, :, 0:E], ALU.add)
            dve.drain()

        def pe_prefix(pe, o, src, n):
            pe.matmul(o, cstb("earlier"), src, start=True, stop=False)
            for d in range(1, n):
                last = pe.matmul(o[:, 8 * d:8 * n], cstb("onesb"), src[:, 0:8 * (n - d)], start=False, stop=(d == n - 1))
            return last

        f0_b = sem("f0_b")

        def h_at(u, c):
            return big[:, 2048 * (u % 2) + 512 * c:2048 * (u % 2) + 512 * c + 512]

        class Routed:

            def __init__(self, n, src, capacity, slot, gated):
                self.n, self.src, self.capacity, self.slot, self.gated = n, src, capacity, slot, gated
                self.slots = 8 * capacity
                self.groups = self.slots // 512
                self.tiles = [min(128, capacity - a) for a in range(0, capacity, 128)]
                self.stores = 1 if capacity % 128 == 0 else 2
                self.sent = nc.dram_tensor(f"sent{n}", (self.slots + 2 * N, D), F32).ap()
                self.made = nc.dram_tensor(f"made{n}", (self.slots + 1, D), F32).ap()

        r0 = Routed(0, l0f, L0_CAPACITY, L0F_SLOT, False)
        r1 = Routed(1, l1f, L1_CAPACITY, L1F_SLOT, True)
        zeros_set = sem("zeros_set")
        cleared = sem("cleared")
        rt_slots = sem("rt_slots")
        rt_sent = sem("rt_sent")
        rt_back = [sem(f"rt_back{g}") for g in range(5)]
        rt_turn = sem("rt_turn")
        rt_cols = sem("rt_cols")
        rt_w = [sem(f"rt_w{i}") for i in range(4)]
        rt_up = sem("rt_up")
        rt_silu = sem("rt_silu")
        rt_h = sem("rt_h")
        rt_y = sem("rt_y")
        rt_rows = sem("rt_rows")
        rt_made = [sem(f"rt_made{i}") for i in range(4)]
        rt_got = [sem(f"rt_got{g}") for g in range(4)]
        slot_at = sb("slot_at", [128, 2 * T])
        kept = sb("kept", [128, 2 * T])
        row_to = sb("row_to", [128, 2 * T], U32)
        row_from = sb("row_from", [128, 2 * T], U32)
        slot_cols = work[:, 1024:1024 + r1.slots]

        def slot_rows(g):
            return v[:, 4 * g:4 * g + 4, :] if g < 4 else q[:, 0:512].rearrange("p (n d) -> p n d", d=D)

        def hidden(s, c, r):
            at0 = 2048 * (s % 2) + r.capacity * c
            return big[:, at0:at0 + r.capacity]

        def pool_clear(pool):
            pool.memset(slots[:, 2:4, :], 0.0).then_inc(zeros_set, 1)

        def sp_clear(sp):
            zeros = slots[:, 2:4, :].rearrange("p a b -> p (a b)")
            sp.wait_ge(zeros_set, 1)
            for r in (r0, r1):
                width = r.slots * D // 128
                sp.dma_start(r.sent[0:r.slots, :].rearrange("(p a) d -> p (a d)", p=128), zeros[:, 0:width]).then_inc(cleared, 16)
                sp.dma_start(r.made[r.slots:r.slots + 1, :], zeros[0:1, 0:D]).then_inc(cleared, 16)

        def sp_routed(sp, r):
            n = r.n

            def load(e, s):
                sp.dma_start(slots[:, s, 0:r.slot], r.src[e]).then_inc(rt_w[s], 16)

            for s in range(4):
                load(s, s)
            sp.wait_ge(rt_sent, 256 * (n + 1))
            for g in range(r.groups):
                sp.dma_start(slot_rows(g), r.sent[512 * g:512 * g + 512, :].rearrange("(n p) d -> p n d", p=128))\
                    .then_inc(rt_back[g], 16)
            for e in range(8):
                s = e % 4
                if e < 4:
                    sp.wait_ge(rt_y, 8 * r.n + e + 1)
                    load(e + 4, s)
                sp.wait_ge(rt_rows, 8 * r.n + e + 1)
                a = r.capacity * e
                full = r.capacity // 128
                sp.dma_start(r.made[a:a + 128 * full, :].rearrange("(n p) d -> p n d", p=128),
                             result(s)[:, 0:128 * full].rearrange("p (n d) -> p n d", d=D)).then_inc(rt_made[s], 16)
                if r.stores == 2:
                    m = r.tiles[-1]
                    sp.dma_start(r.made[a + 128 * full:a + r.capacity, :],
                                 result(s)[0:m, 128 * full:128 * full + 128]).then_inc(rt_made[s], 16)

        def result(s):
            return e[:, 512 * s:512 * s + 512]

        def stored(r, experts):
            return 32 * r.n + 16 * r.stores * experts

        def pool_routed(pool, r):
            if r.n == 0:
                pool.wait_ge(cleared, 64)
            pool.wait_ge(rt_slots, r.n + 1)
            for c in range(2 * T):
                pool.indirect_dma_start(r.sent, bass.IndirectOffsetOnAxis(ap=row_to[:, c:c + 1], axis=0),
                                        xn[:, c % T, :], None).then_inc(rt_sent, 16)
            for s in range(4):
                pool.wait_ge(rt_made[s], stored(r, 2))
            for g in range(4):
                for c in (2 * g, 2 * g + 1, T + 2 * g, T + 2 * g + 1):
                    pool.indirect_dma_start(et[:, 128 * c:128 * c + 128], None, r.made,
                                            bass.IndirectOffsetOnAxis(ap=row_from[:, c:c + 1], axis=0)).then_inc(rt_got[g], 16)

        def pe_routed(pe, r):
            n = r.n
            for g in range(r.groups):
                pe.wait_ge(rt_back[g], 16 * (n + 1) if g < 4 else 16)
                if g >= 2:
                    pe.wait_ge(rt_cols, 4 * n + g - 1)
                for i in range(4):
                    last = pe.transpose(bank(6 + g % 2)[:, 128 * i:128 * i + 128], slot_rows(g)[:, i, :], cst("ident"))
                last.then_inc(rt_turn, 1)
            pe.wait_ge(rt_cols, 4 * n + r.groups)

            def y(e, s):
                pe.wait_ge(rt_h, 32 * n + 4 * (e + 1))
                waitfrom(pe, rt_rows, 8 * n, e - 1)
                for i, m in enumerate(r.tiles):
                    for c in range(4):
                        a = 512 * (1 + r.gated) + 128 * c
                        last = mm(pe, bank(4 + s % 2)[0:m, 128 * i:128 * i + 128], hidden(s, c, r)[:, 128 * i:128 * i + m],
                                  slots[:, s, a:a + 128], start=(c == 0), stop=(c == 3))
                last.then_inc(rt_y, 1)

            def body(i):
                for s in range(4):
                    e = 4 * i + s
                    pe.wait_ge(rt_w[s], 32 * n + 16 * (i + 1))
                    cols = slot_cols[:, bass.ds(e * r.capacity, r.capacity)] if not isinstance(e, int) else \
                        slot_cols[:, e * r.capacity:(e + 1) * r.capacity]
                    for c in range(4):
                        if r.gated:
                            waitfrom(pe, rt_h, 32 * n, 4 * e + c - 1)
                            for part in range(2):
                                a = 512 * (1 - part) + 128 * c
                                last = mm(pe, bank(2 * (c % 2) + part)[:, 0:r.capacity], slots[:, s, a:a + 128], cols)
                        else:
                            waitfrom(pe, rt_h, 32 * n, 4 * e + c - 3)
                            last = mm(pe, bank(c)[:, 0:r.capacity], slots[:, s, 128 * c:128 * c + 128], cols)
                        last.then_inc(rt_up, 1)
                        if c == 1 and (s or not isinstance(i, int) or i > 0):
                            y(e - 1, (s - 1) % 4)
            peeled(pe, 2, body)
            y(7, 3)
            pe.wait_ge(rt_rows, 8 * (n + 1))
            pe_keys(pe, n + 1, 3 * n + 3)

        def act_routed(act, r):
            n = r.n
            for g in range(r.groups):
                act.wait_ge(rt_turn, 4 * n + g + 1)
                act.copy(slot_cols[:, 512 * g:512 * g + 512], bank(6 + g % 2)).then_inc(rt_cols, 1)

            def body(i):
                for s in range(4):
                    e = 4 * i + s
                    for c in range(4):
                        act.wait_ge(rt_up, 32 * n + 4 * e + c + 1)
                        if r.gated:
                            waitfrom(act, rt_h, 32 * n, 4 * e + c - 1)
                            act.activation(silus[:, c % 2, 0:r.capacity], bank(2 * (c % 2))[:, 0:r.capacity],
                                           ACT.Silu).then_inc(rt_silu, 1)
                        else:
                            if c == 0:
                                waitfrom(act, rt_y, 8 * n, e - 1)
                            act.activation(hidden(s, c, r), bank(c)[:, 0:r.capacity], ACT.Relu,
                                           bias=slots[:, s, 1024 + c:1025 + c]).then_inc(rt_h, 1)
            peeled(act, 2, body)
            act_keys(act, n + 1)

        def dve_slots(dve, r, pick, place):
            for j in range(2):
                dve.tensor_tensor(tmp[:, :, 8 * j:8 * j + 8], place[j], rows_of(cst(f"first_slot{r.n}")), ALU.add)
                dve.tensor_tensor(tmp[:, :, 16 + 8 * j:24 + 8 * j], pick[j], gates[:, :, 0:8], ALU.mult)
                dve.tensor_reduce(kept[:, T * j:T * j + T], pick[j], AX.X, ALU.add)
            dve.drain()
            for j in range(2):
                dve.tensor_tensor(tmp[:, :, 8 * j:8 * j + 8], tmp[:, :, 8 * j:8 * j + 8], pick[j], ALU.mult)
                dve.tensor_reduce(gcol[:, j, 0:T], tmp[:, :, 16 + 8 * j:24 + 8 * j], AX.X, ALU.add)
            dve.tensor_scalar(kept[:, :], kept[:, :], -1.0, 1.0, ALU.mult, ALU.add)
            dve.drain()
            for j in range(2):
                dve.tensor_reduce(slot_at[:, T * j:T * j + T], tmp[:, :, 8 * j:8 * j + 8], AX.X, ALU.add)
            dve.drain()
            dve.scalar_tensor_tensor(slot_at[:, :], kept[:, :], float(r.slots), slot_at[:, :], ALU.mult, ALU.add)
            dve.drain()
            dve.tensor_copy(row_from[:, :], slot_at[:, :])
            dve.tensor_tensor(kept[:, :], kept[:, :], cst("spare_row"), ALU.mult)
            dve.drain()
            dve.tensor_tensor(kept[:, :], kept[:, :], slot_at[:, :], ALU.add)
            dve.drain()
            dve.tensor_copy(row_to[:, :], kept[:, :]).then_inc(rt_slots, 1)

        def dve_routed(dve, r):
            n = r.n

            def rows_out(e, s, i):
                dve.wait_ge(rt_y, 8 * n + e + 1)
                if not isinstance(i, int) or i > 0:
                    dve.wait_ge(rt_made[s], stored(r, i))
                full = r.capacity // 128
                last = dve.tensor_copy(result(s)[:, 0:128 * full], bank(4 + s % 2)[:, 0:128 * full])
                if r.stores == 2:
                    m = r.tiles[-1]
                    last = dve.tensor_copy(result(s)[0:m, 128 * full:128 * full + 128],
                                           bank(4 + s % 2)[0:m, 128 * full:128 * full + 128])
                last.then_inc(rt_rows, 1)

            def body(i):
                for s in range(4):
                    e = 4 * i + s
                    if r.gated:
                        for c in range(4):
                            dve.wait_ge(rt_silu, 4 * e + c + 1)
                            if c == 0:
                                waitfrom(dve, rt_y, 8 * n, e - 1)
                            dve.tensor_tensor(hidden(s, c, r), silus[:, c % 2, 0:r.capacity],
                                              bank(2 * (c % 2) + 1)[:, 0:r.capacity], ALU.mult).then_inc(rt_h, 1)
                            if c == 2 and (s or not isinstance(i, int) or i > 0):
                                rows_out(e - 1, (s - 1) % 4, i if s else i - 1)
                    else:
                        rows_out(e, s, i)
            peeled(dve, 2, body)
            if r.gated:
                rows_out(7, 3, 1)
            dve_values(dve, n + 1)
            dve.drain()
            for g in range(4):
                dve.wait_ge(rt_got[g], 64 * (n + 1))
                for j in range(2):
                    for t in (2 * g, 2 * g + 1):
                        c = T * j + t
                        last = dve.scalar_tensor_tensor(x[:, t, :], et[:, 128 * c:128 * c + 128], gcol[:, j, t:t + 1],
                                                        x[:, t, :], ALU.mult, ALU.add)
                    dve.drain()
            dve.nop().then_inc(x_done, 1)

        def pe_f0(pe, stage, m):
            pe_turn(pe, m, xn)
            pe_route(pe, m, stage, "l0f_wg", 8)
            pe.wait_ge(choice, 1)
            pe_prefix(pe, bank(6)[:, 0:16 * 8], picksb[:, :, :].rearrange("p t e -> p (t e)"), 2 * T).then_inc(counted, 1)
            pe.wait_ge(f0_b, 1)
            pe.transpose(bank(7)[0:64, 0:128], xi[:, 0, 0:64], cst("ident")).then_inc(f0_b, 1)
            pe.wait_ge(f0_b, 3)
            for t in range(T):
                last = mm(pe, bank(t // 4)[:, t % 4 * 128:t % 4 * 128 + 128], et[0:64, 0:128],
                          w("l0f_b2", 128 * t, 128)[0:64, :])
            last.then_inc(f0_b, 1)
            pe.wait_ge(f0_b, 5)
            pe_routed(pe, r0)

        def act_f0(act, m):
            act_turn(act, m)
            act_probs(act, 0, 8)
            act.wait_ge(f0_b, 2)
            act.copy(et[0:64, 0:128], bank(7)[0:64, 0:128]).then_inc(f0_b, 1)
            act_routed(act, r0)

        def dve_add_gated(dve, t, src, gate):
            return dve.scalar_tensor_tensor(x[:, t, :], src, gate, x[:, t, :], ALU.mult, ALU.add)

        def dve_f0(dve, norm):
            dve_norm(dve, norm, x, xn, 1e-5)
            dve_logits(dve, 0, 8)
            dve_probs(dve, 0, 8)
            dve_best(dve, 8)
            dve_best_at(dve, 8, 2)
            dve_picks(dve, 8, 2, None)
            for j in range(2):
                last = dve.tensor_copy(picksb[:, T * j:T * j + T, :], picks[:, j, :, 0:8])
            last.then_inc(choice, 1)
            dve.wait_ge(counted, 1)
            place = bank(6)[:, 0:128].rearrange("p (t e) -> p t e", e=8)
            for j in range(2):
                dve.scalar_tensor_tensor(picks[:, j, :, 0:8], place[:, T * j:T * j + T, :], float(L0_CAPACITY),
                                         picks[:, j, :, 0:8], ALU.is_lt, ALU.mult)
            dve.drain()
            dve_gates(dve, 8, 2)
            dve_slots(dve, r0, [picks[:, j, :, 0:8] for j in range(2)], [place[:, T * j:T * j + T, :] for j in range(2)])
            dve.tensor_copy(xi[:, 0, 0:64].rearrange("p (t e) -> p t e", e=8), gates[:, :, 0:8]).then_inc(f0_b, 1)
            dve.wait_ge(f0_b, 4)
            dve.tensor_tensor(x[:, :, :], x[:, :, :], banks(0, 2, 128), ALU.add).then_inc(f0_b, 1)
            dve.drain()
            dve_routed(dve, r0)

        ha_in = sem("ha_in")
        ha_val = sem("ha_val")
        ha_score = sem("ha_score")
        ha_less = sem("ha_less")
        ha_exp = sem("ha_exp")
        ha_v = sem("ha_v")
        ha_turn = sem("ha_turn")
        ha_et = sem("ha_et")
        ha_av = sem("ha_av")
        ha_at = sem("ha_at")
        ha_out = sem("ha_out")
        USES = {3: "in score less exp v av at", 4: "in val score less av at", 7: "in val score less exp turn et av at",
                9: "in val score less exp turn et av at", 10: "in val score less exp turn et av at"}

        def base(name, stage, per=B):
            return per * sum(name in uses.split() for st, uses in USES.items() if st < stage)

        moving = big[:, 0:2048].rearrange("p (a c) -> p a c", a=2)
        less = big[:, 2048:4096].rearrange("p (a c) -> p a c", a=2)
        exps = e[:, :].rearrange("p (a c) -> p a c", a=2)
        still = work[:, 0:512].rearrange("p (a c) -> p a c", a=2)
        values = work[:, 512:1024].rearrange("p (a c) -> p a c", a=2)
        scratch = work[:, 1024:2048].rearrange("p (a c) -> p a c", a=2)
        exps_t = et[:, :].rearrange("p (a c) -> p a c", a=2)
        SCALE = float(HD) ** -0.5
        low = sb("low", [128, 2, H])

        def rounds(eng, step, lags):
            def body(i):
                for s in range(2):
                    step(2 * i + s, s)
            peeled(eng, B // 2, body, 2)
            for b in range(B, B + lags):
                step(b, b % 2)

        def has(b, lag):
            return not isinstance(b, int) or 0 <= b - lag < B

        def seq(ap, b, n):
            return ap[:, bass.ds(b * n, n)] if not isinstance(b, int) else ap[:, b * n:b * n + n]

        def pe_out_heads(pe, stage, wname, wo_banks):
            pe.wait_ge(ha_at, base("at", stage) + B - 2)
            for t in range(T):
                if t == T - 1:
                    pe.wait_ge(ha_at, base("at", stage) + B)
                last = mm(pe, bank(wo_banks + t // 4)[:, t % 4 * 128:t % 4 * 128 + 128], at[:, 128 * t:128 * t + 128],
                          w(wname))
                if t % 4 == 3:
                    last.then_inc(ha_out, 1)

        def dve_out_heads(dve, stage):
            for h in range(2):
                dve.wait_ge(ha_out, base("at", stage, 2) + h + 1)
                last = dve.tensor_tensor(x[:, 4 * h:4 * h + 4, :], x[:, 4 * h:4 * h + 4, :], banks(h, 1, 128), ALU.add)
            last.then_inc(x_done, 1)
            dve.drain()

        def dve_mask_heads(dve, src, parts):
            for n in range(parts):
                dve.tensor_tensor(scratch[:, 0, 256 * n:256 * n + 256].rearrange("p (j l) -> p j l", l=L),
                                  src[:, 256 * n:256 * n + 256].rearrange("p (j l) -> p j l", l=L),
                                  cst("head_of_four").unsqueeze(2).to_broadcast([128, 4, L]), ALU.mult)

        def dve_pick_heads(dve, dst, parts):
            for n in range(parts):
                last = dve.tensor_reduce(dst[n], scratch[:, 0, 256 * n:256 * n + 256].rearrange("p (j l) -> p l j", l=L),
                                         AX.X, ALU.add)
            return last

        OWN = 10

        def pool_l1x(pool):
            st = 3
            pool.wait_ge(q_ready, 2 * 1 + 2)
            pool.wait_ge(k_ready, 4 * 1 + 4)

            def step(b, s):
                waitfrom(pool, ha_score, base("score", st), b - 1)
                pool.tensor_tensor(moving[:, s, :].rearrange("p (h l) -> p h l", l=L),
                                   seq(q, b, L).unsqueeze(1).to_broadcast([128, H, L]),
                                   cst("head").unsqueeze(2).to_broadcast([128, H, L]), ALU.mult)
                pool.tensor_copy(still[:, s, 0:128], seq(k, b, S)).then_inc(ha_in, 1)
            rounds(pool, step, 0)

        def pe_l1x(pe, stage, m):
            st = 3
            pe_project(pe, 1, stage, m)
            pe.wait_ge(v_ready, 4)
            pe.wait_ge(q_ready, 4)

            def step(b, s):
                if has(b, 0):
                    pe.wait_ge(ha_in, base("in", st) + b + 1)
                    waitfrom(pe, ha_exp, base("exp", st), b - 1)
                    for h in range(2):
                        last = mm(pe, bank(2 * s + h), still[:, s, 0:128], moving[:, s, 512 * h:512 * h + 512])
                    last.then_inc(ha_score, 1)
                if has(b, 2):
                    pe.wait_ge(ha_v, base("v", st) + b - 1)
                    waitfrom(pe, ha_at, base("at", st), b - 3)
                    for g in range(4):
                        last = mm(pe, bank(4 + s)[32 * g:32 * g + 32, 0:256], values[:, s, 32 * g:32 * g + 32],
                                  exps[:, s, 256 * g:256 * g + 256])
                    last.then_inc(ha_av, 1)
            rounds(pe, step, 2)
            pe_out_heads(pe, stage, "l1x_wo", 0)

        def act_l1x(act, m):
            st = 3
            act_project(act, 1, m)

            def step(b, s):
                act.wait_ge(ha_less, base("less", st) + b + 1)
                waitfrom(act, ha_av, base("av", st), b - 1)
                act.activation(exps[:, s, L * OWN:], less[:, s, 0:L * (H - OWN)], ACT.Exp, scale=SCALE)
                for h in range(OWN):
                    last = act.activation(exps[:, s, L * h:L * h + L], bank(2 * s + h // 8)[:, h % 8 * L:h % 8 * L + L],
                                          ACT.Exp, bias=low[:, s, h:h + 1], scale=SCALE,
                                          accum_out=small[:, 2 + s, h:h + 1])
                last.then_inc(ha_exp, 1)
            rounds(act, step, 0)

        def dve_l1x(dve, norm):
            st = 3
            dve_norm(dve, norm, x, xn, 1e-5)
            dve.drain()
            dve.tensor_tensor(x[:, :, :], x[:, :, :], rows_of(row("l1x_bo")), ALU.add)

            def step(b, s):
                top, z = small[:, s, :], 1 - s
                if has(b, 0):
                    dve.wait_ge(ha_score, base("score", st) + b + 1)
                    dve.tensor_reduce(top, banks(2 * s, 2, L), AX.X, ALU.max)
                    dve.drain()
                    waitfrom(dve, ha_exp, base("exp", st), b - 1)
                    dve.tensor_tensor(less[:, s, 0:L * (H - OWN)].rearrange("p (h l) -> p h l", l=L),
                                      banks(2 * s, 2, L)[:, OWN:, :],
                                      top[:, OWN:].unsqueeze(2).to_broadcast([128, H - OWN, L]), ALU.subtract)
                    dve.tensor_scalar(low[:, s, :], top, -SCALE, None, ALU.mult).then_inc(ha_less, 1)
                total = small[:, 2 + z, :]
                if has(b, 1):
                    dve.wait_ge(ha_exp, base("exp", st) + b)
                    dve.tensor_reduce(total[:, OWN:], exps[:, z, L * OWN:].rearrange("p (h l) -> p h l", l=L), AX.X, ALU.add)
                if has(b, 2):
                    dve.wait_ge(ha_av, base("av", st) + b - 1)
                    dve_mask_heads(dve, bank(4 + s), 1)
                dve.drain()
                if has(b, 1):
                    dve.reciprocal(total, total)
                if has(b, 2):
                    dve_pick_heads(dve, [seq(at, b - 2, L)], 1).then_inc(ha_at, 1)
                dve.drain()
                if has(b, 1):
                    waitfrom(dve, ha_av, base("av", st), b - 2)
                    vb = seq(v[:, :, :].rearrange("p b c -> p (b c)"), b - 1, D)
                    dve.tensor_tensor(values[:, z, 0:128].rearrange("p (h d) -> p h d", d=HD),
                                      vb.rearrange("p (h d) -> p h d", d=HD),
                                      total.unsqueeze(2).to_broadcast([128, H, HD]), ALU.mult).then_inc(ha_v, 1)
            rounds(dve, step, 2)
            dve_out_heads(dve, 3)


        def pool_l3x(pool):
            st = 9
            pool.wait_ge(q_ready, 2 * 3 + 2)
            pool.wait_ge(k_ready, 4 * 3 + 4)
            pool.wait_ge(v_ready, 12)

            def step(b, s):
                if has(b, 0):
                    waitfrom(pool, ha_score, base("score", st), b - 1)
                    pool.tensor_tensor(moving[:, s, :].rearrange("p (i c) -> p i c", c=S),
                                       seq(k, b, S).unsqueeze(1).to_broadcast([128, 8, S]),
                                       cst("head_pair").unsqueeze(2).to_broadcast([128, 8, S]), ALU.mult)
                    pool.tensor_tensor(still[:, s, 0:128].rearrange("p (j l) -> p j l", l=L),
                                       seq(q, b, L).unsqueeze(1).to_broadcast([128, 2, L]),
                                       cst("head_parity").unsqueeze(2).to_broadcast([128, 2, L]), ALU.mult).then_inc(ha_in, 1)
                if has(b, 2):
                    waitfrom(pool, ha_av, base("av", st), b - 3)
                    pool.tensor_copy(values[:, s, 0:128],
                                     seq(v[:, :, :].rearrange("p b c -> p (b c)"), b - 2, D)).then_inc(ha_val, 1)
            rounds(pool, step, 2)

        def pe_l3x(pe, stage, m):
            st = 9
            pe_project(pe, 3, stage, m)
            pe.wait_ge(v_ready, 12)
            pe.wait_ge(q_ready, 8)

            def step(b, s):
                z = 1 - s
                if has(b, 0):
                    pe.wait_ge(ha_in, base("in", st) + b + 1)
                    waitfrom(pe, ha_exp, base("exp", st), b - 1)
                    for h in range(2):
                        last = mm(pe, bank(2 * s + h), still[:, s, 0:128], moving[:, s, 512 * h:512 * h + 512])
                    last.then_inc(ha_score, 1)
                if has(b, 2):
                    pe.wait_ge(ha_exp, base("exp", st) + b - 1)
                    waitfrom(pe, ha_et, base("et", st), b - 2)
                    for i in range(8):
                        last = pe.transpose(bank(4 + i // 4)[:, i % 4 * 128:i % 4 * 128 + 128],
                                            exps[:, s, 128 * i:128 * i + 128], cst("ident"))
                    last.then_inc(ha_turn, 1)
                if has(b, 3):
                    pe.wait_ge(ha_et, base("et", st) + b - 2)
                    pe.wait_ge(ha_val, base("val", st) + b - 2)
                    waitfrom(pe, ha_at, base("at", st), b - 4)
                    for g in range(4):
                        o = bank(6 + z)[32 * g:32 * g + 32, :]
                        mm(pe, o[:, 0:256], values[:, z, 32 * g:32 * g + 32], exps_t[:, z, 256 * g:256 * g + 256])
                        last = mm(pe, o[:, 256:512], cst("ones")[:, 0:32], exps_t[:, z, 256 * g:256 * g + 256])
                    last.then_inc(ha_av, 1)
            rounds(pe, step, 3)
            pe_out_heads(pe, stage, "l3x_wo", 0)

        def act_l3x(act, m):
            st = 9
            act_project(act, 3, m)

            def step(b, s):
                if has(b, 2):
                    act.wait_ge(ha_turn, base("turn", st) + b - 1)
                    waitfrom(act, ha_av, base("av", st), b - 3)
                    act.copy(exps_t[:, s, :], ps[:, 4:6, :].rearrange("p b c -> p (b c)")).then_inc(ha_et, 1)
                if has(b, 0):
                    act.wait_ge(ha_less, base("less", st) + b + 1)
                    waitfrom(act, ha_turn, base("turn", st), b - 1)
                    for i in range(8):
                        last = act.activation(exps[:, s, S * i:S * i + S], bank(2 * s + i // 4)[:, i % 4 * S:i % 4 * S + S],
                                              ACT.Exp, bias=low[:, s, i:i + 1], scale=SCALE)
                    last.then_inc(ha_exp, 1)
            rounds(act, step, 2)

        def dve_l3x(dve, norm):
            st = 9
            dve_norm(dve, norm, x, xn, 1e-5)
            dve_values(dve, 3)
            dve.drain()
            dve.tensor_tensor(x[:, :, :], x[:, :, :], rows_of(row("l3x_bo")), ALU.add)

            def step(b, s):
                top = small[:, s, 0:8]
                if has(b, 0):
                    dve.wait_ge(ha_score, base("score", st) + b + 1)
                    dve.tensor_reduce(top, banks(2 * s, 2, S), AX.X, ALU.max)
                    dve.drain()
                    waitfrom(dve, ha_exp, base("exp", st), b - 1)
                    dve.tensor_scalar(low[:, s, 0:8], top, -SCALE, None, ALU.mult).then_inc(ha_less, 1)
                if has(b, 3):
                    dve.drain()
                    dve.wait_ge(ha_av, base("av", st) + b - 2)
                    dve_mask_heads(dve, bank(7 - s), 2)
                    dve.drain()
                    dve_pick_heads(dve, [scratch[:, 1, 0:64], scratch[:, 1, 64:128]], 2)
                    dve.drain()
                    dve.reciprocal(scratch[:, 1, 128:192], scratch[:, 1, 64:128])
                    dve.drain()
                    dve.tensor_tensor(seq(at, b - 3, L), scratch[:, 1, 0:64], scratch[:, 1, 128:192],
                                      ALU.mult).then_inc(ha_at, 1)
            rounds(dve, step, 3)
            dve_out_heads(dve, 9)

        sa_dup = sem("sa_dup")
        sa_v = sem("sa_v")
        sa_vb = sem("sa_vb")
        sa_proj = sem("sa_proj")
        sa_rot = sem("sa_rot")
        SELF = {7: ("l2a", "rope2", True), 10: ("l3a", "rope3", False)}

        def act_duplicate(act, m, dst, gain=None, shift=None):
            act_turn(act, m, gain, shift)
            for h in range(2):
                twice = dst[:, 1024 * h:1024 * h + 1024].rearrange("p (b r l) -> p b r l", r=2, l=L)
                src = bank(6 + h).rearrange("p (b l) -> p b l", l=L).unsqueeze(2).to_broadcast([128, 8, 2, L])
                if gain is None:
                    act.activation(twice, src, ACT.Copy).then_inc(sa_dup, 1)
                else:
                    act.activation(twice, src, ACT.Identity, scale=gain, bias=shift).then_inc(sa_dup, 1)

        def pe_self_values(pe, n, src, wname):
            for b in range(B):
                if b % 8 == 0:
                    pe.wait_ge(sa_dup, 2 * n + b // 8 + 1)
                last = mm(pe, bank(b // 4)[:, b % 4 * 128:b % 4 * 128 + 128], src[:, 128 * b:128 * b + 128], w(wname))
            last.then_inc(sa_v, 1)

        def make_values(eng, b, s, mask):
            eng.tensor_tensor(values[:, s, :].rearrange("p (c g d) -> p c g d", c=2, g=4),
                               seq(v[:, :, :].rearrange("p b c -> p (b c)"), b, D)
                               .rearrange("p (g d) -> p g d", g=4).unsqueeze(1).to_broadcast([128, 2, 4, 32]),
                               cst(mask).rearrange("p (c d) -> p c d", c=2).unsqueeze(2).to_broadcast([128, 2, 4, 32]),
                               ALU.mult).then_inc(ha_val, 1)

        def pool_self(pool, st):
            n = {7: 1, 10: 2}[st]
            pool.wait_ge(sa_rot, 4 * n - 2)

            def step(b, s):
                if isinstance(b, int) and b == 2:
                    pool.wait_ge(sa_vb, n + 1)
                if has(b, 0):
                    waitfrom(pool, ha_score, base("score", st), b - 1)
                    pool.tensor_tensor(moving[:, s, 0:512].rearrange("p (i c) -> p i c", c=L),
                                       seq(k, b, L).unsqueeze(1).to_broadcast([128, 8, L]),
                                       cst("head_pair").unsqueeze(2).to_broadcast([128, 8, L]), ALU.mult)
                    pool.tensor_tensor(still[:, s, 0:128].rearrange("p (j l) -> p j l", l=L),
                                       seq(q, b, L).unsqueeze(1).to_broadcast([128, 2, L]),
                                       cst("head_parity").unsqueeze(2).to_broadcast([128, 2, L]), ALU.mult).then_inc(ha_in, 1)
                if has(b, 2):
                    waitfrom(pool, ha_av, base("av", st), b - 3)
                    make_values(pool, b - 2, s, "value_soft")
            rounds(pool, step, 2)

        def pe_self(pe, st, m):
            name, _, _ = SELF[st]
            n = {7: 1, 10: 2}[st]
            pe_turn(pe, m, xn)
            pe.wait_ge(w_loaded[st], 16)
            for h in range(2):
                pe.wait_ge(xnt_ready, 2 * m + h + 1)
                if h:
                    pe.wait_ge(sa_dup, 2 * n + 2)
                for j, part in enumerate(("_wq", "_wqr", "_wk", "_wkr")):
                    last = mm(pe, bank(4 * h + j), w(name + part), xnt[:, 512 * h:512 * h + 512])
                    if j % 2:
                        last.then_inc(sa_proj, 1)
            pe.wait_ge(sa_rot, 4 * n - 2)
            pe_self_values(pe, n, e, name + "_wv")
            pe.wait_ge(sa_rot, 4 * n)

            def step(b, s):
                z = 1 - s
                if has(b, 0):
                    pe.wait_ge(ha_in, base("in", st) + b + 1)
                    waitfrom(pe, ha_less, base("less", st), b - 1)
                    mm(pe, bank(6 + s), still[:, s, 0:128], moving[:, s, 0:512], start=True, stop=False)
                    mm(pe, bank(6 + s), cstb("identb"), cstb("causal"), start=False, stop=True).then_inc(ha_score, 1)
                if has(b, 2):
                    pe.wait_ge(ha_exp, base("exp", st) + b - 1)
                    waitfrom(pe, ha_et, base("et", st), b - 3)
                    for g in range(4):
                        last = pe.transpose(bank(4 + s)[:, 128 * g:128 * g + 128], exps[:, s, 128 * g:128 * g + 128],
                                            cst("ident"))
                    last.then_inc(ha_turn, 1)
                if has(b, 3):
                    pe.wait_ge(ha_et, base("et", st) + b - 2)
                    pe.wait_ge(ha_val, base("val", st) + b - 2)
                    waitfrom(pe, ha_at, base("at", st), b - 4)
                    if isinstance(b, int) and b == 3:
                        pe.wait_ge(sa_vb, n + 1)
                    for g in range(4):
                        for j in range(2):
                            mm(pe, bank(2 + z)[32 * g:32 * g + 32, 0:64], values[:, z, 128 * j + 32 * g:128 * j + 32 * g + 32],
                               exps_t[:, z, 128 * g + 64 * j:128 * g + 64 * j + 64], start=(j == 0), stop=(j == 1))
                        for j in range(2):
                            last = mm(pe, bank(2 + z)[32 * g:32 * g + 32, 64:128], cst("value_soft")[:, 32 * j:32 * j + 32],
                                      exps_t[:, z, 128 * g + 64 * j:128 * g + 64 * j + 64], start=(j == 0), stop=(j == 1))
                    last.then_inc(ha_av, 1)
            rounds(pe, step, 3)
            pe_out_heads(pe, st, name + "_wo", 0)

        def act_self(act, st, m):
            act_duplicate(act, m, e)

            def step(b, s):
                if has(b, 2):
                    act.wait_ge(ha_turn, base("turn", st) + b - 1)
                    waitfrom(act, ha_av, base("av", st), b - 3)
                    act.copy(exps_t[:, s, 0:512], bank(4 + s)).then_inc(ha_et, 1)
                if has(b, 0):
                    act.wait_ge(ha_less, base("less", st) + b + 1)
                    waitfrom(act, ha_turn, base("turn", st), b - 1)
                    act.activation(exps[:, s, 0:512], less[:, s, 0:512], ACT.Exp, scale=SCALE).then_inc(ha_exp, 1)
            rounds(act, step, 2)

        def dve_self(dve, st, norm):
            name, rope, biased = SELF[st]
            n = {7: 1, 10: 2}[st]
            dve_norm(dve, norm, x, xn, 1e-5)
            for h in range(2):
                for j, (dst, bq) in enumerate(((q, "_bq"), (k, "_bk"))):
                    dve.wait_ge(sa_proj, 4 * (n - 1) + 2 * h + j + 1)
                    turn = scratch[:, j, :].rearrange("p (b l) -> p b l", l=L)
                    out = dst[:, 512 * h:512 * h + 512].rearrange("p (b l) -> p b l", l=L)
                    for o, bk, tab, sfx in ((out, 4 * h + 2 * j, "_cos", ""), (turn, 4 * h + 2 * j + 1, "_sin", "r")):
                        table = cst(rope + tab).unsqueeze(1).to_broadcast([128, 8, L])
                        src = bank(bk).rearrange("p (b l) -> p b l", l=L)
                        if biased:
                            dve.scalar_tensor_tensor(o, src, bias(name + bq + sfx), table, ALU.add, ALU.mult)
                        else:
                            dve.tensor_tensor(o, src, table, ALU.mult)
                dve.drain()
                for j, dst in enumerate((q, k)):
                    dve.tensor_tensor(dst[:, 512 * h:512 * h + 512], dst[:, 512 * h:512 * h + 512], scratch[:, j, :],
                                      ALU.add).then_inc(sa_rot, 1)
                dve.drain()
            dve.wait_ge(sa_v, n + 1)
            if biased:
                dve.tensor_tensor(v[:, :, :], banks(0, 4, 128), rows_of(row(name + "_bv"), B), ALU.add).then_inc(sa_vb, 1)
                dve.tensor_tensor(x[:, :, :], x[:, :, :], rows_of(row(name + "_bo")), ALU.add)
            else:
                dve.tensor_copy(v[:, :, :], banks(0, 4, 128)).then_inc(sa_vb, 1)

            def step(b, s):
                top = small[:, s, 0:8]
                if has(b, 0):
                    dve.wait_ge(ha_score, base("score", st) + b + 1)
                    sc = banks(6 + s, 1, L)
                    dve.tensor_reduce(top, sc, AX.X, ALU.max)
                    dve.drain()
                    waitfrom(dve, ha_exp, base("exp", st), b - 1)
                    dve.tensor_tensor(less[:, s, 0:512].rearrange("p (i c) -> p i c", c=L), sc,
                                      top.unsqueeze(2).to_broadcast([128, 8, L]), ALU.subtract).then_inc(ha_less, 1)
                if has(b, 3):
                    dve.wait_ge(ha_av, base("av", st) + b - 2)
                    dve.reciprocal(scratch[:, s, 0:64], bank(3 - s)[:, 64:128])
                    dve.drain()
                    dve.tensor_tensor(seq(at, b - 3, L), bank(3 - s)[:, 0:64], scratch[:, s, 0:64],
                                      ALU.mult).then_inc(ha_at, 1)
            rounds(dve, step, 3)
            dve_out_heads(dve, st)

        wv_proj = sem("wv_proj")
        wv_arg = sem("wv_arg")
        wv_near = sem("wv_near")
        wv_frac = sem("wv_frac")
        wv_sin = sem("wv_sin")
        wv_sum = sem("wv_sum")
        wv_norm = sem("wv_norm")
        wv_inverse = sem("wv_inverse")
        wv_spread = sem("wv_spread")
        wv_unit = sem("wv_unit")
        wf_up = sem("wf_up")
        wf_bias = sem("wf_bias")
        wf_turns = sem("wf_turns")
        wf_frac = sem("wf_frac")
        wf_sin = sem("wf_sin")
        wf_h = sem("wf_h")
        wf_gelu = sem("wf_gelu")
        wf_out = sem("wf_out")
        b1_turns = sb("b1_turns", [128, 4])
        MAGIC = 1.5 * 2.0 ** 23
        TURNS = float(np.float32(1.0 / (2.0 * np.pi)))
        ANGLE = float(np.float32(6.283185))
        waves = slots[:, :, :].rearrange("p a b -> p (a b)")[:, 0:4096].rearrange("p (c n) -> p c n", c=4)
        bigc = big[:, :].rearrange("p (c n) -> p c n", c=4)
        workc = work[:, :].rearrange("p (c n) -> p c n", c=4)

        def wholes(c):
            return (e if c < 2 else et)[:, 1024 * (c % 2):1024 * (c % 2) + 1024]

        def two(i):
            return ps[:, i:i + 2, :].rearrange("p b c -> p (b c)")

        def pool_wave(pool):
            st = 4
            pool.wait_ge(wv_unit, 8)

            def step(b, s):
                waitfrom(pool, ha_score, base("score", st), b - 1)
                for hf in range(2):
                    pool.tensor_tensor(moving[:, s, 256 * hf:256 * hf + 256].rearrange("p (i t) -> p i t", t=L),
                                       seq(waves[:, hf, :], b, L).unsqueeze(1).to_broadcast([128, 4, L]),
                                       cst("wave_pair").unsqueeze(2).to_broadcast([128, 4, L]), ALU.mult)
                    last = pool.tensor_tensor(still[:, s, 128 * hf:128 * hf + 128].rearrange("p (j t) -> p j t", t=L),
                                       seq(waves[:, 2 + hf, :], b, L).unsqueeze(1).to_broadcast([128, 2, L]),
                                       cst("wave_parity").unsqueeze(2).to_broadcast([128, 2, L]),
                                       ALU.mult)
                last.then_inc(ha_in, 1)
            rounds(pool, step, 0)

        def pe_wave(pe, stage, m):
            st = 4
            pe_turn(pe, m, xn)
            pe.wait_ge(w_loaded[stage], 16)
            for c in range(4):
                a = 4 if c % 2 else 0
                if c == 0:
                    pe.wait_ge(xnt_ready, 2 * m + 2)
                if c == 1:
                    pe.wait_ge(sa_dup, 2)
                if c >= 2:
                    pe.wait_ge(wv_arg, c - 1)
                for j, part in enumerate(("f", "p")):
                    name = "l1a_w" + "qk"[c // 2] + part
                    for h in range(2):
                        last = mm(pe, bank(a + 2 * j + h), w(name, 128 * (c % 2), 128), xnt[:, 512 * h:512 * h + 512])
                last.then_inc(wv_proj, 1)
            pe.wait_ge(wv_arg, 3)
            pe_self_values(pe, 0, k, "l1a_wv")
            pe.wait_ge(wv_arg, 4)
            for c in range(4):
                pe.wait_ge(wv_sin, c + 1)
                for h in range(2):
                    last = mm(pe, bank(4)[32 * c:32 * c + 32, :], cst("wave_sum")[:, 32 * h:32 * h + 32],
                              bigc[:, c, 512 * h:512 * h + 512], start=(h == 0), stop=(h == 1))
            last.then_inc(wv_sum, 1)
            pe.wait_ge(sa_vb, 1)
            pe.wait_ge(wv_inverse, 1)
            for h in range(2):
                for c in range(4):
                    a = 128 * (2 * c + h)
                    mm(pe, bank((4 * h + c + 1) % 8), cst("wave_spread")[:, a:a + 128],
                       workc[:, 0, 0:512]).then_inc(wv_spread, 1)
            pe.wait_ge(wv_unit, 8)

            def step(b, s):
                if has(b, 0):
                    pe.wait_ge(ha_in, base("in", st) + b + 1)
                    waitfrom(pe, ha_less, base("less", st), b - 1)
                    for hf in range(2):
                        last = mm(pe, bank(s)[:, 256 * hf:256 * hf + 256], still[:, s, 128 * hf:128 * hf + 128],
                                  moving[:, s, 256 * hf:256 * hf + 256])
                    last.then_inc(ha_score, 1)
                if has(b, 2):
                    pe.wait_ge(ha_less, base("less", st) + b - 1)
                    pe.wait_ge(ha_val, base("val", st) + b - 1)
                    waitfrom(pe, ha_at, base("at", st), b - 3)
                    for g in range(4):
                        for c in range(2):
                            i = 2 * g + c
                            last = mm(pe, bank(4 + s)[32 * g:32 * g + 32, 0:64],
                                      values[:, s, 128 * c + 32 * g:128 * c + 32 * g + 32],
                                      exps_t[:, s, 64 * i:64 * i + 64], start=(c == 0), stop=(c == 1))
                    last.then_inc(ha_av, 1)
            rounds(pe, step, 2)
            pe_out_heads(pe, st, "l1a_wo", 2)
            pe_turn(pe, m + 1, xn)
            for c in range(4):
                for h in range(2):
                    if c == 0:
                        pe.wait_ge(xnt_ready, 2 * m + 2 + h + 1)
                    last = mm(pe, bank(2 * c + h), w("l1a_w1", 128 * c, 128), xnt[:, 512 * h:512 * h + 512])
                last.then_inc(wf_up, 1)
            pe.wait_ge(wf_gelu, 4)
            for c in range(4):
                pe.wait_ge(wf_h, c + 1)
                for t in range(T):
                    last = mm(pe, bank(t // 4)[:, t % 4 * 128:t % 4 * 128 + 128], bigc[:, c, 128 * t:128 * t + 128],
                              w("l1a_w2", 128 * c, 128), start=(c == 0 and t % 4 == 0), stop=(c == 3 and t % 4 == 3))
            last.then_inc(wf_out, 1)

        def act_wave(act, m):
            st = 4
            act_duplicate(act, m, k, bias("l1a_g1"), bias("l1a_be1"))
            def near(c):
                act.wait_ge(wv_arg, c + 1)
                act.activation(workc[:, c, :], bigc[:, c, :], ACT.Identity, scale=TURNS)
                act.activation(wholes(c), bigc[:, c, :], ACT.Copy, scale=TURNS, bias=MAGIC).then_inc(wv_near, 1)

            def sine(c):
                act.wait_ge(wv_frac, c + 1)
                act.activation(waves[:, c, :], waves[:, c, :], ACT.Sin, scale=-ANGLE)
                act.drain()
                act.square(bigc[:, c, :], waves[:, c, :]).then_inc(wv_sin, 1)

            near(0)
            near(1)
            sine(0)
            near(2)
            sine(1)
            near(3)
            sine(2)
            sine(3)
            act.wait_ge(wv_sum, 1)
            act.sqrt(workc[:, 0, 0:512], bank(4)).then_inc(wv_norm, 1)

            def step(b, s):
                act.wait_ge(ha_av, base("av", st) + b + 1)
                act.copy(seq(at, b, L), bank(4 + s)[:, 0:64]).then_inc(ha_at, 1)
            rounds(act, step, 0)
            act_turn(act, m + 1, bias("l1a_g2"), bias("l1a_be2"))
            act.wait_ge(wf_bias, 1)
            for c in range(4):
                act.wait_ge(wf_up, c + 1)
                act.activation(workc[:, c, :], two(2 * c), ACT.Identity, scale=TURNS,
                               bias=b1_turns[:, c:c + 1]).then_inc(wf_turns, 1)
                act.activation(bigc[:, c, :], two(2 * c), ACT.Gelu, bias=bias("l1a_b1", c)).then_inc(wf_gelu, 1)
            for c in range(4):
                act.wait_ge(wf_frac, c + 1)
                act.activation(waves[:, c, :], waves[:, c, :], ACT.Sin, scale=-ANGLE).then_inc(wf_sin, 1)

        def dve_fraction(dve, near, turns, c, out_sem):
            dve.scalar_tensor_tensor(waves[:, c, :], near, MAGIC, turns, ALU.subtract, ALU.subtract)
            dve.drain()
            dve.tensor_scalar(waves[:, c, :], waves[:, c, :], -0.5, 0.5, ALU.max, ALU.min).then_inc(out_sem, 1)

        def dve_wave(dve, norm):
            st = 4
            dve_norm(dve, norm, x, xi, 1e-5, publish=False)
            dve.drain()
            dve_norm(dve, norm + 1, xi, xn, 1e-5)
            dve.tensor_scalar(b1_turns[:, :], bsb[:, BIAS_AT["l1a_b1"][0]:BIAS_AT["l1a_b1"][0] + 4], TURNS, None,
                              ALU.mult).then_inc(wf_bias, 1)
            dve.drain()
            dve.tensor_tensor(xi[:, :, :], xi[:, :, :], rows_of(row("l1a_bo")), ALU.add)
            def argument(c):
                a = 4 if c % 2 else 0
                dve.wait_ge(wv_proj, c + 1)
                name = "l1a_b" + "qk"[c // 2]
                dve.scalar_tensor_tensor(bigc[:, c, :].rearrange("p (b l) -> p b l", l=L),
                                         two(a).rearrange("p (b l) -> p b l", l=L), bias(name + "f", c % 2),
                                         cst("position").unsqueeze(1).to_broadcast([128, B, L]), ALU.add, ALU.mult)
                dve.drain()
                dve.scalar_tensor_tensor(bigc[:, c, :], two(a + 2), bias(name + "p", c % 2), bigc[:, c, :],
                                         ALU.add, ALU.add).then_inc(wv_arg, 1)

            def fraction(c):
                dve.wait_ge(wv_near, c + 1)
                dve_fraction(dve, wholes(c), workc[:, c, :], c, wv_frac)

            argument(0)
            argument(1)
            fraction(0)
            argument(2)
            fraction(1)
            argument(3)
            fraction(2)
            fraction(3)
            dve.wait_ge(sa_v, 1)
            dve.tensor_tensor(v[:, :, :], banks(0, 4, 128), rows_of(row("l1a_bv"), B), ALU.add).then_inc(sa_vb, 1)
            norms = workc[:, 0, 0:512]
            dve.wait_ge(wv_norm, 1)
            dve.tensor_scalar(norms, norms, 1e-12, None, ALU.max)
            dve.drain()
            dve.reciprocal(norms, norms).then_inc(wv_inverse, 1)
            for h in range(2):
                for c in range(4):
                    dve.wait_ge(wv_spread, 4 * h + c + 1)
                    dve.tensor_tensor(waves[:, c, 512 * h:512 * h + 512], waves[:, c, 512 * h:512 * h + 512],
                                      bank((4 * h + c + 1) % 8), ALU.mult).then_inc(wv_unit, 1)
            dve.tensor_tensor(v[:, :, :].rearrange("p b (h d) -> p b h d", d=HD),
                              v[:, :, :].rearrange("p b (h d) -> p b h d", d=HD),
                              row("l1a_iscale").unsqueeze(2).unsqueeze(1).to_broadcast([128, B, H, HD]), ALU.mult)
            dve.drain()

            def step(b, s):
                waitfrom(dve, ha_av, base("av", st), b - 1)
                make_values(dve, b, s, "value_wave")
                dve.wait_ge(ha_score, base("score", st) + b + 1)
                dve.tensor_tensor(exps_t[:, s, 0:512].rearrange("p (i t) -> p i t", t=L), banks(s, 1, L),
                                  cst("wave_causal").unsqueeze(1).to_broadcast([128, 8, L]), ALU.mult).then_inc(ha_less, 1)
            rounds(dve, step, 0)
            for h in range(2):
                dve.wait_ge(ha_out, base("at", st, 2) + h + 1)
                dve.tensor_tensor(xi[:, 4 * h:4 * h + 4, :], xi[:, 4 * h:4 * h + 4, :], banks(2 + h, 1, 128), ALU.add)
            dve.drain()
            dve_norm(dve, norm + 2, xi, xn, 1e-5)
            dve.drain()
            dve.tensor_tensor(x[:, :, :], x[:, :, :], xi[:, :, :], ALU.add)
            dve.drain()
            dve.tensor_tensor(x[:, :, :], x[:, :, :], rows_of(row("l1a_b2")), ALU.add)
            for c in range(4):
                dve.wait_ge(wf_turns, c + 1)
                dve.tensor_scalar(wholes(c), workc[:, c, :], MAGIC, None, ALU.add)
                dve.drain()
                dve_fraction(dve, wholes(c), workc[:, c, :], c, wf_frac)
            dve.wait_ge(wf_gelu, 4)
            for c in range(4):
                dve.wait_ge(wf_sin, c + 1)
                dve.scalar_tensor_tensor(bigc[:, c, :], waves[:, c, :], 0.1, bigc[:, c, :], ALU.mult, ALU.add)\
                   .then_inc(wf_h, 1)
            dve.wait_ge(wf_out, 1)
            dve.tensor_tensor(x[:, :, :], x[:, :, :], banks(0, 2, 128), ALU.add).then_inc(x_done, 1)
            dve.drain()

        class Gated:

            def __init__(self, name, src, experts, slot):
                self.src, self.experts, self.slot = src, experts, slot
                self.per = 4
                self.w = [sem(f"{name}_w{i}") for i in range(self.per)]
                self.up = sem(name + "_up")
                self.silu = sem(name + "_silu")
                self.h = sem(name + "_h")
                self.y = sem(name + "_y")

        f2 = Gated("f2", l2f, L2F_EXPERTS, L2F_SLOT)
        f3 = Gated("f3", l3f, L3F_PAIRS, L3F_SLOT)
        f2_acc = sem("f2_acc")
        f3_gate = sem("f3_gate")
        f3_product = sem("f3_product")
        f3_pick = sem("f3_pick")

        def units(eng, f, step, first=1):
            n = 2 * f.per

            def body(i):
                for s in range(n):
                    step(n * i + s, s, i)
            rounds_n = f.experts // f.per
            peeled(eng, rounds_n, body, first)
            for u in range(rounds_n * n, 2 * f.experts + 1):
                step(u, u % n, rounds_n)

        def exists(f, u):
            return not isinstance(u, int) or 0 <= u < 2 * f.experts

        def pe_gate_up(pe, f, used, u, s, i):
            if s % 2 == 0:
                pe.wait_ge(f.w[s // 2], 16 * (i + 1))
            waitfrom(pe, used, 0, u - 1)
            for part in range(2):
                a = 128 * (1 - part)
                last = mm(pe, bank(2 * (s % 2) + part), slots[:, s // 2, a:a + 128],
                          xnt[:, 512 * (s % 2):512 * (s % 2) + 512])
            last.then_inc(f.up, 1)

        def act_gated(act, f, used):
            def step(u, s, i):
                if exists(f, u):
                    act.wait_ge(f.up, u + 1)
                    waitfrom(act, used, 0, u - 1)
                    act.activation(silus[:, s % 2, :], bank(2 * (s % 2)), ACT.Silu).then_inc(f.silu, 1)
            units(act, f, step)

        def sp_gated(sp, f):
            def load(i, s):
                wait(sp, f.y, 2 * (f.per * (i - 1) + s) + 2)
                sp.dma_start(slots[:, s, 0:f.slot], f.src[f.per * i + s]).then_inc(f.w[s], 16)

            def body(i):
                for s in range(f.per):
                    load(i, s)
            peeled(sp, f.experts // f.per, body)
            for s in range(f.experts % f.per):
                load(f.experts // f.per, s)

        weigh_turn = sem("weigh_turn")
        met = sem("met")
        met_sum = sem("met_sum")
        edge = sem("edge")
        edge_row = sem("edge_row")

        def pe_capacity(pe):
            pe.wait_ge(choice, 2)
            for t in range(T):
                last = pe.transpose(bank(t // 4)[:, t % 4 * 128:t % 4 * 128 + 128], xi[:, t, :], cst("ident"))
            last.then_inc(weigh_turn, 1)
            for i in range(len(SHIFTS)):
                pe.wait_ge(met, i + 1)
                mm(pe, bank(4)[:, 128:129], cstb("same_expert"), metb[:, 0:1]).then_inc(met_sum, 1)
            pe.wait_ge(edge, 1)
            mm(pe, bank(4)[:, 256:272], cst("ones"), edges[:, :]).then_inc(edge_row, 1)
            pe.wait_ge(choice, 3)
            pe_prefix(pe, bank(6)[:, 0:64], picksb[:, 0:T, :].rearrange("p t e -> p (t e)"), T).then_inc(counted, 1)
            pe.wait_ge(choice, 4)
            pe_prefix(pe, bank(6)[:, 64:128], picksb[:, T:2 * T, :].rearrange("p t e -> p (t e)"), T).then_inc(counted, 1)

        metb = sb("metb", [128, 1], BF16)
        edges = sb("edges", [128, 16])
        edger = sb("edger", [128, 16])
        found = sb("found", [128, 1], I32)
        trial = sb("trial", [128, 1], I32)
        step_i = sb("step_i", [128, 1], I32)
        count = sb("count", [128, 1])

        def dve_capacity(dve):
            sel, wt = picks[:, 2, :, 0:8], picks[:, 3, :, 0:8]
            mine = [picks[:, j, :, 8:16] for j in range(2)]
            for j in range(2):
                dve.tensor_copy(mine[j], picks[:, j, :, 0:8])
            dve.tensor_tensor(sel, picks[:, 0, :, 0:8], picks[:, 1, :, 0:8], ALU.add)
            dve.drain()
            dve.scalar_tensor_tensor(wt, sel, 1.0, gates[:, :, 0:8], ALU.subtract, ALU.add)
            dve.drain()
            dve.tensor_copy(xi[:, :, :].rearrange("p t (k e) -> p t k e", e=8),
                            wt.unsqueeze(2).to_broadcast([128, T, 16, 8])).then_inc(choice, 1)
            dve.memset(found[:, :], 0)
            dve.tensor_copy(trial[:, :], cis[:, 0:1])
            dve.wait_ge(weigh_turn, 1)
            row_w, hit = ps[:, 0:2, :].rearrange("p b c -> p (b c)"), e[:, N:2 * N]
            for i, shift in enumerate(SHIFTS):
                dve.drain()
                dve.tensor_scalar(hit, row_w, trial[:, :].bitcast(F32), 0.0, ALU.is_ge, ALU.add, accum_out=count[:, :])
                dve.drain()
                dve.tensor_scalar(metb[:, :], count[:, :], cst("needed"), None, ALU.is_ge).then_inc(met, 1)
                if i + 1 < len(SHIFTS):
                    dve.tensor_tensor(trial[:, :], found[:, :], cis[:, i + 1:i + 2], ALU.add)
                dve.wait_ge(met_sum, i + 1)
                dve.tensor_scalar(step_i[:, :], bank(4)[:, 128:129], 1.0, float(1 << shift), ALU.subtract, ALU.mult)
                dve.drain()
                dve.tensor_tensor(found[:, :], found[:, :], step_i[:, :], ALU.add)
                if i + 1 < len(SHIFTS):
                    dve.tensor_tensor(trial[:, :], trial[:, :], step_i[:, :], ALU.add)
            dve.drain()
            dve.tensor_scalar(hit, row_w, found[:, :].bitcast(F32), 0.0, ALU.is_gt, ALU.add, accum_out=count[:, :])
            dve.tensor_scalar(edges[:, 0:8], cst("expert_row"), found[:, :].bitcast(F32), None, ALU.mult)
            dve.drain()
            dve.tensor_scalar(edges[:, 8:16], cst("expert_row"), count[:, :], None, ALU.mult).then_inc(edge, 1)
            dve.wait_ge(edge_row, 1)
            dve.tensor_copy(edger[:, :], bank(4)[:, 256:272])
            dve.drain()
            dve.tensor_scalar(edger[:, 8:16], edger[:, 8:16], -1.0, float(L1_CAPACITY), ALU.mult, ALU.add)
            over, same = picks[:, 0, :, 0:8], picks[:, 1, :, 0:8]
            dve.tensor_tensor(over, wt, rows_of(edger[:, 0:8]), ALU.is_gt)
            dve.tensor_tensor(same, wt, rows_of(edger[:, 0:8]), ALU.is_equal)
            dve.drain()
            dve.tensor_copy(picksb[:, 0:T, :], same).then_inc(choice, 1)
            dve.wait_ge(counted, 2)
            dve.tensor_tensor(sel, bank(6)[:, 0:64].rearrange("p (t e) -> p t e", e=8), rows_of(edger[:, 8:16]), ALU.is_lt)
            dve.drain()
            dve.tensor_tensor(same, same, sel, ALU.mult)
            dve.drain()
            dve.tensor_tensor(same, same, over, ALU.add)
            dve.drain()
            g8 = gates[:, :, 0:8]
            dve.tensor_copy(picksb[:, T:2 * T, :], same).then_inc(choice, 1)
            for j in range(2):
                dve.tensor_tensor(mine[j], mine[j], same, ALU.mult)
            dve.tensor_tensor(g8, g8, same, ALU.mult)
            dve.drain()
            dve.tensor_reduce(tot[:, :], g8, AX.X, ALU.add)
            dve.drain()
            dve.tensor_scalar(tot[:, :], tot[:, :], 1.1920929e-07, None, ALU.max)
            dve.drain()
            dve.reciprocal(tot[:, :], tot[:, :])
            dve.drain()
            dve.tensor_tensor(g8, g8, per_token(tot[:, :], 8), ALU.mult)
            dve.drain()
            dve.wait_ge(counted, 3)
            dve_slots(dve, r1, mine, [bank(6)[:, 64:128].rearrange("p (t e) -> p t e", e=8)] * 2)

        def pe_f1(pe, m):
            pe_turn(pe, m, xn)
            pe_route(pe, m, 5, "l1f_wr", 8)
            pe_capacity(pe)
            pe_routed(pe, r1)

        def act_f1(act, m):
            act_turn(act, m)
            act_probs(act, 1, 8)
            act_routed(act, r1)

        def dve_f1(dve, norm):
            dve_norm(dve, norm, x, xn, 1e-5)
            dve_logits(dve, 1, 8)
            dve_probs(dve, 1, 8)
            dve_best(dve, 8)
            dve_best_at(dve, 8, 2)
            dve_picks(dve, 8, 2, 1.1920929e-07)
            dve_gates(dve, 8, 2)
            dve_capacity(dve)
            dve_routed(dve, r1)

        def pe_f2(pe, m):
            pe_turn(pe, m, xn)
            pe_route(pe, m, 8, "l2f_wr", 32, 6)

            def y(u, s):
                pe.wait_ge(f2.h, u + 1)
                waitfrom(pe, f2_acc, 0, u - 1)
                for t in range(4):
                    last = mm(pe, bank(4 + s % 2)[:, 128 * t:128 * t + 128], h_at(s % 2, 0)[:, 128 * t:128 * t + 128],
                              slots[:, s // 2, 256:384])
                last.then_inc(f2.y, 1)

            def step(u, s, i):
                if exists(f2, u):
                    pe_gate_up(pe, f2, f2.h, u, s, i)
                if exists(f2, u - 1):
                    y(u - 1, (s - 1) % 8)
            units(pe, f2, step)

        def act_f2(act, m):
            act_turn(act, m)
            act_probs(act, 2, 32)
            act_gated(act, f2, f2.h)

        def dve_f2(dve, norm):
            dve_norm(dve, norm, x, xn, 1e-5)
            dve_logits(dve, 2, 32, "l2f_br", 6)
            dve.memset(gates[:, :, 0:4], 1.0)
            dve.drain()
            routing = {0: lambda: dve_probs(dve, 2, 32), 1: lambda: dve_best(dve, 32), 2: lambda: dve_best_at(dve, 32, 4),
                       3: lambda: dve_picks(dve, 32, 4, 1e-12), 4: lambda: dve_gates(dve, 32, 4, 4)}

            def add(u, s):
                dve.drain()
                dve.wait_ge(f2.y, u + 1)
                for t in range(4):
                    tt = 4 * (s % 2) + t
                    last = dve_add_gated(dve, tt, bank(4 + s % 2)[:, 128 * t:128 * t + 128], gcol[:, s // 2, tt:tt + 1])
                last.then_inc(f2_acc, 1)

            def step(u, s, i):
                if exists(f2, u):
                    if s % 2 == 0:
                        col = 4 * i + s // 2
                        src = gates[:, :, col] if isinstance(col, int) else gates[:, :, bass.ds(col, 1)].rearrange("p t o -> p (t o)")
                        dve.tensor_copy(gcol[:, s // 2, 0:T], src)
                    dve.wait_ge(f2.silu, u + 1)
                    waitfrom(dve, f2.y, 0, u - 1)
                    dve.tensor_tensor(h_at(s % 2, 0), silus[:, s % 2, :], bank(2 * (s % 2) + 1), ALU.mult).then_inc(f2.h, 1)
                if exists(f2, u - 1):
                    add(u - 1, (s - 1) % 8)
                if isinstance(u, int) and u in routing:
                    routing[u]()
            units(dve, f2, step)
            dve.drain()
            dve.nop().then_inc(x_done, 1)

        f3_parts = sem("f3_parts")
        gate_parts = sb("gate_parts", [128, T, 3 * L3F_GATES], BF16)
        products = work[:, 1024:2048].rearrange("p (a c) -> p a c", a=2)
        def early_product(u):
            return (k[:, :] if u < 4 else v[:, :, :].rearrange("p b c -> p (b c)"))[:, u % 4 * 512:u % 4 * 512 + 512]

        gate_cols = sb("gate_cols", [128, N], BF16)
        pair_pick = sb("pair_pick", [128, 4, 128], BF16)

        def pool_f3(pool):
            def pick(i, s):
                wait(pool, f3_gate, 2 * (4 * (i - 1) + s) + 2)
                col = 2 * (4 * i + s)
                src = cst("gate_row")[:, col:col + 2] if isinstance(col, int) else cst("gate_row")[:, bass.ds(col, 2)]
                pool.tensor_copy(pair_pick[:, s, :].rearrange("p (j c) -> p j c", j=2),
                                 src.unsqueeze(2).to_broadcast([128, 2, 64])).then_inc(f3_pick, 1)

            def body(i):
                for s in range(4):
                    pick(i, s)
            peeled(pool, L3F_PAIRS // 4, body)
            for s in range(L3F_PAIRS % 4):
                pick(L3F_PAIRS // 4, s)

        def pe_f3(pe, m):
            pe_turn(pe, m, xn)
            pe_route(pe, m, 11, "l3f_wg", 32)

            def gate(u, s, i):
                pe.wait_ge(f3_pick, 4 * i + s // 2 + 1)
                waitfrom(pe, f3.h, 0, u - 1)
                mm(pe, bank(4 + s % 2), pair_pick[0:3 * L3F_GATES, s // 2, :],
                   gate_cols[0:3 * L3F_GATES, 512 * (s % 2):512 * (s % 2) + 512]).then_inc(f3_gate, 1)

            def y(u, s):
                pe.wait_ge(f3.h, u + 1)
                first = isinstance(u, int) and u < 2
                final = isinstance(u, int) and u >= 2 * f3.experts - 2
                for t in range(4):
                    last = mm(pe, bank(6 + s % 2)[:, 128 * t:128 * t + 128], h_at(s % 2, 0)[:, 128 * t:128 * t + 128],
                              slots[:, s // 2, 256:384], start=first and t == 0, stop=final and t == 3)
                last.then_inc(f3.y, 1)

            def step(u, s, i):
                if isinstance(u, int) and u == 8:
                    pe.wait_ge(f3_parts, 1)
                    for t in range(T):
                        o = bank(4 + t // 4)[0:3 * L3F_GATES, t % 4 * 128:t % 4 * 128 + 128]
                        last = mm(pe, o, gate_parts[:, t, :], cstb("identb"))
                    last.then_inc(f3_parts, 1)
                    pe.wait_ge(f3_parts, 3)
                    for early in range(8):
                        gate(early, early, 0)
                        if early:
                            y(early - 1, early - 1)
                if exists(f3, u):
                    pe_gate_up(pe, f3, f3_product, u, s, i)
                    if not isinstance(u, int) or u >= 8:
                        gate(u, s, i)
                if exists(f3, u - 1) and (not isinstance(u, int) or u >= 8):
                    y(u - 1, (s - 1) % 8)
            units(pe, f3, step, 2)

        def act_f3(act, m):
            act_turn(act, m)
            act.wait_ge(route_less, 4)
            act.activation(probs[:, :, :], lg[:, :, :], ACT.Exp, scale=-1.0).then_inc(route_exp, 1)
            def step(u, s, i):
                if isinstance(u, int) and u == 8:
                    act.wait_ge(f3_parts, 2)
                    act.copy(gate_cols[0:3 * L3F_GATES, :], ps[0:3 * L3F_GATES, 4:6, :].rearrange("p b c -> p (b c)"))\
                        .then_inc(f3_parts, 1)
                if exists(f3, u):
                    act.wait_ge(f3.up, u + 1)
                    waitfrom(act, f3_product, 0, u - 1)
                    act.activation(silus[:, s % 2, :], bank(2 * (s % 2)), ACT.Silu).then_inc(f3.silu, 1)
            units(act, f3, step, 2)

        def dve_f3(dve, norm):
            LOW = -3.0e38
            dve_norm(dve, norm, x, xn, 1e-5)
            dve.wait_ge(route_logit, 4)
            dve.tensor_copy(lg[:, :, :], bank(5)[:, 0:256].rearrange("p (t e) -> p t e", e=32)).then_inc(route_less, 1)
            group = small[:, 0:8, 0:8]
            gmask = small[:, 8:16, 0:8]
            gbest = xi[:, 1, :].rearrange("p (t c) -> p t c", c=16)[:, :, 0:8]
            tops = xi[:, 2:4, :].rearrange("p a (n c) -> p (a n) c", c=8)
            dve.memset(group, LOW)

            def early(u):
                dve.wait_ge(f3.silu, u + 1)
                dve.tensor_tensor(early_product(u), silus[:, u % 2, :], bank(2 * (u % 2) + 1), ALU.mult).then_inc(f3_product, 1)

            dve.wait_ge(route_exp, 4)
            dve.tensor_scalar(probs[:, :, :], probs[:, :, :], 1.0, None, ALU.add)
            dve.drain()
            dve.reciprocal(probs[:, :, :], probs[:, :, :])
            dve.drain()
            dve.tensor_tensor(lg[:, :, :], probs[:, :, :], rows_of(row("l3f_bg")), ALU.add)
            dve.drain()
            early(0)
            for t in range(T):
                for g in range(4):
                    dve.max(tops[:, 4 * t + g, :], lg[:, t, 8 * g:8 * g + 8])
            dve.drain()
            early(1)
            dve.tensor_tensor(group[:, :, 0:4], tops[:, :, 0].rearrange("p (t g) -> p t g", g=4),
                              tops[:, :, 1].rearrange("p (t g) -> p t g", g=4), ALU.add)
            dve.drain()
            for t in range(T):
                dve.max(gbest[:, t, :], group[:, t, :])
            dve.drain()
            early(2)
            for t in range(T):
                dve.max_index(best_at[:, t, :], gbest[:, t, :], group[:, t, :])
            dve.drain()
            early(3)
            dve.tensor_copy(best_atf[:, :, :], best_at[:, :, :])
            dve.drain()
            dve.tensor_tensor(gmask[:, :, 0:4], rows_of(cst("iota")[:, 0:4]),
                              best_atf[:, :, 0:1].to_broadcast([128, T, 4]), ALU.is_equal)
            dve.tensor_tensor(gmask[:, :, 4:8], rows_of(cst("iota")[:, 0:4]),
                              best_atf[:, :, 1:2].to_broadcast([128, T, 4]), ALU.is_equal)
            dve.drain()
            dve.tensor_tensor(gmask[:, :, 0:4], gmask[:, :, 0:4], gmask[:, :, 4:8], ALU.add)
            dve.drain()
            dve.tensor_tensor(lg[:, :, :].rearrange("p t (g c) -> p t g c", c=8),
                              lg[:, :, :].rearrange("p t (g c) -> p t g c", c=8),
                              gmask[:, :, 0:4].unsqueeze(3).to_broadcast([128, T, 4, 8]), ALU.mult)
            dve.drain()
            early(4)
            for t in range(T):
                dve.max(best[:, t, :], lg[:, t, :])
            dve.drain()
            early(5)
            for t in range(T):
                dve.match_replace(tmp[:, t, :], best[:, t, :], lg[:, t, :], LOW)
            dve.drain()
            early(6)
            dve.tensor_scalar(tmp[:, :, :], tmp[:, :, :], LOW * 0.99, None, ALU.is_le)
            dve.drain()
            dve.tensor_tensor(gates[:, :, 0:32], tmp[:, :, :], probs[:, :, :], ALU.mult)
            dve.drain()
            early(7)
            dve.tensor_reduce(tot[:, :], gates[:, :, 0:32], AX.X, ALU.add)
            dve.drain()
            dve.tensor_scalar(tot[:, :], tot[:, :], 1e-20, None, ALU.add)
            dve.drain()
            dve.reciprocal(tot[:, :], tot[:, :])
            dve.drain()
            dve.tensor_tensor(gates[:, :, 0:32], gates[:, :, 0:32], per_token(tot[:, :], 32), ALU.mult)
            dve.drain()
            dve.tensor_scalar(gates[:, :, 0:32], gates[:, :, 0:32], 2.5, None, ALU.mult)
            dve.memset(gates[:, :, 32:34], 1.0)
            dve.drain()
            g, n = gates[:, :, 0:L3F_GATES], L3F_GATES
            for part in range(3):
                dve.tensor_copy(gate_parts[:, :, n * part:n * part + n], g)
                dve.drain()
                if part < 2:
                    dve.tensor_tensor(g, g, gate_parts[:, :, n * part:n * part + n], ALU.subtract)
                    dve.drain()
            dve.nop().then_inc(f3_parts, 1)

            def gated(u, s, product):
                waitfrom(dve, f3.y, 0, u - 1)
                dve.wait_ge(f3_gate, u + 1)
                dve.tensor_tensor(h_at(s % 2, 0), product, bank(4 + s % 2), ALU.mult).then_inc(f3.h, 1)

            def step(u, s, i):
                if isinstance(u, int) and u < 8:
                    gated(u, s, early_product(u))
                elif exists(f3, u):
                    dve.wait_ge(f3.silu, u + 1)
                    dve.tensor_tensor(products[:, s % 2, :], silus[:, s % 2, :], bank(2 * (s % 2) + 1), ALU.mult)\
                        .then_inc(f3_product, 1)
                    dve.drain()
                    gated(u, s, products[:, s % 2, :])
            units(dve, f3, step, 2)
            dve.wait_ge(f3.y, 2 * L3F_PAIRS)
            dve.tensor_tensor(x[:, :, :], x[:, :, :], banks(6, 2, 128), ALU.add).then_inc(x_done, 1)

        block = ctx.enter_context(nc.Block())

        @block.sync
        def _(sp):
            sp.dma_start(x[:, :, :], xin.rearrange("(t p) d -> p t d", p=128)).then_inc(x_loaded, 16)
            sp.dma_start(wsb[:, 0:128], weights[:, 0:128]).then_inc(w_loaded[0], 16)
            sp.dma_start(ctxc[:, :], ctx_cols).then_inc(ctx_loaded, 16)
            sp.dma_start(bsb[:, :], biases).then_inc(bias_loaded, 16)
            sp.dma_start(cfs[:, :], cf).then_inc(const_loaded, 16)
            sp.dma_start(ctxr[:, :, :], ctx_rows).then_inc(ctxr_loaded, 16)
            sp.dma_start(work[:, 0:B_COLUMNS], cb).then_inc(other_loaded, 16)
            sp.dma_start(cis[:, :], ci).then_inc(other_loaded, 16)
            sp.dma_start(rsb[:, :], rows.to_broadcast([128, ROW_COLUMNS])).then_inc(other_loaded, 16)
            for i in range(1, STAGES):
                a = WEIGHT_AT[WEIGHTS[i][0][0]][0]
                n = sum(width for _, width in WEIGHTS[i])
                sp.dma_start(wsb[:, a:a + n], weights[:, a:a + n]).then_inc(w_loaded[i], 16)
            sp_clear(sp)
            sp.wait_ge(cleared, 64)
            sp.wait_ge(x_done, 2)
            sp_routed(sp, r0)
            sp.wait_ge(x_done, 5)
            sp_routed(sp, r1)
            sp.wait_ge(x_done, 8)
            sp_gated(sp, f2)
            sp.wait_ge(x_done, 9)
            sp_gated(sp, f3)
            sp.wait_ge(x_done, STAGES)
            sp.dma_start(out.rearrange("(t p) d -> p t d", p=128), x[:, :, :]).then_inc(x_loaded, 16)
            sp.wait_ge(x_loaded, 32)

        @block.gpsimd
        def _(pool):
            pool.memset(minus_half[:, :], -0.5).then_inc(half_set, 1)
            pool.wait_ge(half_set, 1)
            pool_clear(pool)
            pool_rstd(pool, 0)
            pool_rstd(pool, 1)
            pool_rstd(pool, 2)
            pool_rstd(pool, 3)
            pool_routed(pool, r0)
            for st in range(3, STAGES):
                if st == 4:
                    for n in range(5, 8):
                        if n == 7:
                            pool_wave(pool)
                        pool_rstd(pool, n)
                    continue
                pool_rstd(pool, 4 if st == 3 else st + 3)
                if st == 3:
                    pool_l1x(pool)
                if st == 5:
                    pool_routed(pool, r1)
                if st in (7, 10):
                    pool_self(pool, st)
                if st == 9:
                    pool_l3x(pool)
                if st == 11:
                    pool_f3(pool)

        @block.scalar
        def _(act):
            act.wait_ge(bias_loaded, 16)
            act_xs(act, 0, 0)
            act_la(act, 1)
            act_f0(act, 2)
            act_l1x(act, 3)
            act_wave(act, 4)
            act_f1(act, 6)
            act_xs(act, 1, 7)
            act_self(act, 7, 8)
            act_f2(act, 9)
            act_l3x(act, 10)
            act_self(act, 10, 11)
            act_f3(act, 12)

        @block.vector
        def _(dve):
            dve.wait_ge(x_loaded, 16)
            dve_xs(dve, 0, 0)
            dve_la(dve, 1)
            dve_f0(dve, 3)
            dve_l1x(dve, 4)
            dve_wave(dve, 5)
            dve_f1(dve, 8)
            dve_xs(dve, 1, 9)
            dve_self(dve, 7, 10)
            dve_f2(dve, 11)
            dve_l3x(dve, 12)
            dve_self(dve, 10, 13)
            dve_f3(dve, 14)

        @block.tensor
        def _(pe):
            pe_xs(pe, 0, 0, 0)
            pe_la(pe, 1, 1)
            pe_f0(pe, 2, 2)
            pe_l1x(pe, 3, 3)
            pe_wave(pe, 4, 4)
            pe_f1(pe, 6)
            pe_xs(pe, 1, 6, 7)
            pe_self(pe, 7, 8)
            pe_f2(pe, 9)
            pe_l3x(pe, 9, 10)
            pe_self(pe, 10, 11)
            pe_f3(pe, 12)



def laid_out(i):
    f = lambda a: np.asarray(a)
    t = lambda a: np.swapaxes(np.asarray(a), -1, -2)
    half = np.concatenate([np.arange(HD // 2, HD), np.arange(HD // 2)])
    swap = np.arange(HD) ^ 1
    by_half = (np.arange(H)[:, None] * HD + half[None, :]).ravel()
    by_two = (np.arange(H)[:, None] * HD + swap[None, :]).ravel()
    b2 = np.zeros((128, T, D), np.float32)
    for tt in range(T):
        b2[8 * tt:8 * tt + 8, tt] = f(i["L0_ffn_b2"])
    wt = {
        "l0x_w": t(i["L0_xattn_W"]),
        "l0a_wq": t(i["L0_attn_Wq"]), "l0a_wkv": np.concatenate([t(i["L0_attn_Wk"]), t(i["L0_attn_Wv"])], 1),
        "l0a_wd": t(i["L0_attn_Wd"]),
        "l0f_wg": f(i["L0_ffn_wg"]), "l0f_b2": b2.reshape(128, T * D),
        "l1x_wq": f(i["L1_xattn_Wq"]), "l1x_wk": f(i["L1_xattn_Wk"]), "l1x_wv": f(i["L1_xattn_Wv"]),
        "l1x_wo": f(i["L1_xattn_Wo"]),
        "l1a_wqf": f(i["L1_attn_Wqf"]), "l1a_wqp": f(i["L1_attn_Wqp"]), "l1a_wkf": f(i["L1_attn_Wkf"]),
        "l1a_wkp": f(i["L1_attn_Wkp"]), "l1a_wv": f(i["L1_attn_Wv"]), "l1a_wo": f(i["L1_attn_Wo"]),
        "l1a_w1": f(i["L1_attn_W1"]),
        "l1a_w2": f(i["L1_attn_W2"]).reshape(4, 128, 128).transpose(1, 0, 2).reshape(128, 512),
        "l1f_wr": t(i["L1_ffn_router_weight"]),
        "l2x_wq": f(i["L2_xattn_W_q"]), "l2x_wk": f(i["L2_xattn_W_k"]), "l2x_wv": f(i["L2_xattn_W_v"]),
        "l2a_wq": t(i["L2_attn_Wq"]), "l2a_wqr": t(i["L2_attn_Wq"])[:, by_half],
        "l2a_wk": t(i["L2_attn_Wk"]), "l2a_wkr": t(i["L2_attn_Wk"])[:, by_half],
        "l2a_wv": t(i["L2_attn_Wv"]), "l2a_wo": t(i["L2_attn_Wo"]),
        "l2f_wr": t(i["L2_ffn_router_w"]),
        "l3x_wq": f(i["L3_xattn_W_Q"]), "l3x_wk": f(i["L3_xattn_W_K"]), "l3x_wv": f(i["L3_xattn_W_V"]),
        "l3x_wo": f(i["L3_xattn_W_O"]),
        "l3a_wq": t(i["L3_attn_Wq"]), "l3a_wqr": t(i["L3_attn_Wq"])[:, by_two],
        "l3a_wk": t(i["L3_attn_Wk"]), "l3a_wkr": t(i["L3_attn_Wk"])[:, by_two],
        "l3a_wv": t(i["L3_attn_Wv"]), "l3a_wo": t(i["L3_attn_Wo"]),
        "l3f_wg": t(i["L3_ffn_gate_w"]),
    }
    rw = {
        "l0a_bkv": np.concatenate([f(i["L0_attn_bk"]), f(i["L0_attn_bv"])]), "l0a_bd": i["L0_attn_bd"],
        "l0a_gamma": i["L0_attn_gamma"], "l0a_beta": i["L0_attn_beta"], "l1x_bv": i["L1_xattn_bv"],
        "l1x_bo": i["L1_xattn_bo"],
        "l1a_bv": i["L1_attn_bv"], "l1a_bo": i["L1_attn_bo"], "l1a_iscale": f(i["L1_attn_iscale"]).reshape(-1),
        "l1a_b2": i["L1_attn_b2"],
        "l2x_bv": i["L2_xattn_b_v"], "l2a_bv": i["L2_attn_bv"], "l2a_bo": i["L2_attn_bo"],
        "l2f_br": i["L2_ffn_router_bias"], "l3x_bv": i["L3_xattn_b_V"], "l3x_bo": i["L3_xattn_b_O"],
        "l3f_bg": i["L3_ffn_gate_bias"],
    }
    two = lambda a: f(a).reshape(-1, 128).T
    bs = {
        "l0x_b": two(i["L0_xattn_b"]), "l0a_bq": two(i["L0_attn_bq"]), "l1x_bq": two(i["L1_xattn_bq"]),
        "l1x_bk": two(i["L1_xattn_bk"]), "l1a_bqf": two(i["L1_attn_bqf"]), "l1a_bqp": two(i["L1_attn_bqp"]),
        "l1a_bkf": two(i["L1_attn_bkf"]), "l1a_bkp": two(i["L1_attn_bkp"]), "l1a_b1": two(i["L1_attn_b1"]), "l1a_g1": two(i["L1_attn_ln1_g"]),
        "l1a_be1": two(i["L1_attn_ln1_b"]), "l1a_g2": two(i["L1_attn_ln2_g"]), "l1a_be2": two(i["L1_attn_ln2_b"]),
        "l2x_bq": two(i["L2_xattn_b_q"]), "l2x_bk": two(i["L2_xattn_b_k"]), "l2a_bq": two(i["L2_attn_bq"]),
        "l2a_bqr": two(f(i["L2_attn_bq"])[by_half]), "l2a_bk": two(i["L2_attn_bk"]),
        "l2a_bkr": two(f(i["L2_attn_bk"])[by_half]), "l3x_bq": two(i["L3_xattn_b_Q"]), "l3x_bk": two(i["L3_xattn_b_K"]),
    }
    chunks = lambda a: a.reshape(a.shape[0], -1, 128, 128).transpose(0, 2, 1, 3).reshape(a.shape[0], 128, -1)
    l0f = np.concatenate([f(i["L0_ffn_w1"]), chunks(f(i["L0_ffn_w2"])),
                          f(i["L0_ffn_b1"]).reshape(8, 4, 128).transpose(0, 2, 1)], 2)
    l1f = np.concatenate([t(i["L1_ffn_ff_pre_act_weight"]), t(i["L1_ffn_gate_weight"]),
                          chunks(t(i["L1_ffn_ff_post_act_weight"]))], 2)
    shared = lambda a: t(a).reshape(128, 4, 128).transpose(1, 0, 2)
    l2f = np.concatenate([
        np.concatenate([shared(i["L2_ffn_sup_w"]), t(i["L2_ffn_up_w"])], 0),
        np.concatenate([shared(i["L2_ffn_sgate_w"]), t(i["L2_ffn_gate_w"])], 0),
        np.concatenate([t(i["L2_ffn_sdown_w"]).reshape(4, 128, 128), t(i["L2_ffn_down_w"])], 0)], 2)
    pair = lambda a, s: np.concatenate([t(a).reshape(16, 2, 128, 64).transpose(0, 2, 1, 3).reshape(16, 128, 128),
                                        t(s)[None]], 0)
    down = np.concatenate([t(i["L3_ffn_expert_down"]).reshape(16, 128, 128), t(i["L3_ffn_shared_down"])[None]], 0)
    l3f = np.concatenate([pair(i["L3_ffn_expert_up"], i["L3_ffn_shared_up"]),
                          pair(i["L3_ffn_expert_gate"], i["L3_ffn_shared_gate"]), down], 2)
    ctxs = f(i["ctx_1024"])
    return {
        "xin": f(i["x"]).reshape(N, D),
        "ctx_cols": ctxs.reshape(B * S, D).T,
        "ctx_rows": ctxs.transpose(1, 0, 2),
        "weights": np.concatenate([wt[n] for n, _ in [w for g in WEIGHTS for w in g]], 1),
        "rows": np.concatenate([f(rw[n]) for n, _ in ROWS])[None, :],
        "biases": np.concatenate([bs[n] for n, _ in BIASES], 1),
        "l0f": l0f, "l1f": l1f, "l2f": l2f, "l3f": l3f,
        "cf": np.concatenate(list(const_columns().values()), 1),
        "cb": np.concatenate(list(const_bf_columns().values()), 1),
        "ci": const_int_columns(),
    }


def kernel(**inputs):
    import concourse.bacc as bacc
    from concourse.bass_utils import run_bass_kernel_spmd as run

    nc = bacc.Bacc("TRN2", target_bir_lowering=False, num_devices=1)
    arrays = {f"in_{k}": np.ascontiguousarray(v) for k, v in laid_out(inputs).items()}
    args = {k[3:]: nc.dram_tensor(k, a.shape, mybir.dt.from_np(a.dtype), kind="ExternalInput").ap()
            for k, a in arrays.items()}
    out = nc.dram_tensor("out_0", (N, D), F32, kind="ExternalOutput").ap()
    perceiver(nc, out=out, **args)
    r = run(nc, [arrays], core_ids=[0])
    return r.results[0]["out_0"].reshape(B, L, D)
```
